# Optimizing a Trainium2 kernel written in Bass

```python
import numpy as np
import jax
import jax.numpy as jnp

def _softmax(x, axis=-1):
    return jax.nn.softmax(x, axis=axis)

def _gelu(x):
    return jax.nn.gelu(x, approximate=True)

def _silu(x):
    return jax.nn.silu(x)

def _sigmoid(x):
    return jax.nn.sigmoid(x)

def _layernorm(x, axis=-1, eps=1e-05):
    m = jnp.mean(x, axis=axis, keepdims=True)
    v = jnp.var(x, axis=axis, keepdims=True)
    return (x - m) / jnp.sqrt(v + eps)

def _scatter_add(tgt, idx, src, axis=0):
    return tgt.at[idx].add(src)

def _segment_sum(src, seg, n):
    return jax.ops.segment_sum(src, seg, n)
kernel_name = 'mk_early_fusion_embed_d2_tok_img1024_r4_21337b'

def setup_inputs(seed: int=0):
    np.random.seed(seed)
    _w = jnp.asarray

    def _rec_inputs():
        import jax
        import jax.numpy as jnp
        _rk = jax.random.key(seed)
        x = jax.random.uniform(jax.random.fold_in(_rk, 1), (16, 3, 256, 256), jnp.float32, 0.0, 1)
        x_txt = jax.random.randint(jax.random.fold_in(_rk, 51), (16, 128), 0, 24991, jnp.int32)
        return (x, x_txt)
    x, x_txt = _rec_inputs()

    def _L0_tok_setup():
        import jax, jax.numpy as jnp
        import numpy as np
        _GRAY_W = (0.2989, 0.587, 0.114)
        key = jax.random.key(seed)
        x = jax.random.uniform(key, (32, 3, 256, 256), dtype=jnp.float32)
        sx = jnp.array([[-3.0, 0.0, 3.0], [-10.0, 0.0, 10.0], [-3.0, 0.0, 3.0]], dtype=jnp.float32)
        scharr = jnp.stack([sx, sx.T])[:, None, :, :]
        return {'x': x, 'scharr': scharr}
    _L0_tok_all = _L0_tok_setup()
    _L0_tok_in = {k: v for k, v in _L0_tok_all.items() if k in ('scharr',)}
    del _L0_tok_all

    def _L0_txt_setup():
        import jax, jax.numpy as jnp
        import numpy as np
        V, R, D = (25000, 64, 256)
        B, S = (8, 512)
        key = jax.random.key(seed)
        k1, k2, k3, k4 = jax.random.split(key, 4)
        input_ids = jax.random.randint(k1, (B, S), 0, V, dtype=jnp.int64 if jax.config.jax_enable_x64 else jnp.int32)
        U = jax.random.normal(k2, (V, R), dtype=jnp.float32)
        s = jax.random.uniform(k3, (R,), dtype=jnp.float32)
        Vt = jax.random.normal(k4, (R, D), dtype=jnp.float32)
        return {'input': input_ids, 'U': U, 's': s, 'Vt': Vt}
    _L0_txt_all = _L0_txt_setup()
    _L0_txt_in = {k: v for k, v in _L0_txt_all.items() if k in ('U', 's', 'Vt')}
    del _L0_txt_all

    def _L0_attn_setup():
        import jax, jax.numpy as jnp
        import numpy as np
        D_MODEL = 256
        N_HEADS = 16
        D_K = D_MODEL // N_HEADS
        SEQ = 1024
        BATCH = 2
        LOCAL_WINDOW = 128
        SCALE = 1.0 / float(np.sqrt(D_K))
        INIT = 1.0 / float(np.sqrt(D_MODEL))

        def _local_mask(seq_len: int) -> jnp.ndarray:
            i = jnp.arange(seq_len)[:, None]
            j = jnp.arange(seq_len)[None, :]
            return (j <= i) & (j >= i - LOCAL_WINDOW)
        key = jax.random.key(seed)
        ks = jax.random.split(key, 9)
        mk = lambda k: jax.random.normal(k, (D_MODEL, D_MODEL), dtype=jnp.float32) * INIT
        return {'x': jax.random.normal(ks[0], (BATCH, SEQ, D_MODEL), dtype=jnp.float32), 'Wq': mk(ks[1]), 'bq': jnp.zeros((D_MODEL,), jnp.float32), 'Wk': mk(ks[2]), 'bk': jnp.zeros((D_MODEL,), jnp.float32), 'Wv': mk(ks[3]), 'bv': jnp.zeros((D_MODEL,), jnp.float32), 'Wo': mk(ks[4]), 'bo': jnp.zeros((D_MODEL,), jnp.float32)}
    _L0_attn_all = _L0_attn_setup()
    _L0_attn_in = {k: v for k, v in _L0_attn_all.items() if k in ('Wq', 'bq', 'Wk', 'bk', 'Wv', 'bv', 'Wo', 'bo')}
    del _L0_attn_all

    def _L0_ffn_setup():
        import jax, jax.numpy as jnp
        import numpy as np
        CAPACITY_RATIO = 0.75
        key = jax.random.key(seed)
        k1, k2, k3 = jax.random.split(key, 3)
        B, L, D = (4, 2048, 256)
        x = jax.random.normal(k1, (B, L, D), dtype=jnp.float32)
        w_router = jax.random.normal(k2, (D,), dtype=jnp.float32) * 0.02
        w_block = jax.random.normal(k3, (D, D), dtype=jnp.float32) * 0.02
        return {'x': x, 'w_router': w_router, 'w_block': w_block}
    _L0_ffn_all = _L0_ffn_setup()
    _L0_ffn_in = {k: v for k, v in _L0_ffn_all.items() if k in ('w_router', 'w_block')}
    del _L0_ffn_all

    def _L1_attn_setup():
        import jax, jax.numpy as jnp
        import numpy as np
        BATCH, SEQ, D_MODEL, STATE_DIM = (8, 512, 256, 256)

        def _cayley_circulant_eigenvalues(a_params, n):
            half_n = n // 2
            a_full = jnp.zeros((n,), dtype=a_params.dtype)
            a_full = a_full.at[1:half_n].set(a_params[:half_n - 1])
            a_full = a_full.at[half_n + 1:].set(-a_params[:half_n - 1][::-1])
            omega = jnp.fft.fft(a_full).imag
            w2 = omega * omega
            denom = 1.0 + w2
            return ((1.0 - w2) / denom + 1j * (-2.0 * omega / denom)).astype(jnp.complex64)
        key = jax.random.key(seed)
        k1, k2, k3, k4 = jax.random.split(key, 4)
        u = jax.random.normal(k1, (BATCH, SEQ, D_MODEL), dtype=jnp.float32)
        a_params = jax.random.normal(k2, (STATE_DIM // 2,), dtype=jnp.float32) * 0.1
        B_w = jax.random.normal(k3, (STATE_DIM, D_MODEL), dtype=jnp.float32) / np.sqrt(D_MODEL).astype(np.float32)
        C_w = jax.random.normal(k4, (D_MODEL, STATE_DIM), dtype=jnp.float32) / np.sqrt(STATE_DIM).astype(np.float32)
        D = jnp.zeros((D_MODEL,), dtype=jnp.float32)
        return {'u': u, 'a_params': a_params, 'B_w': B_w, 'C_w': C_w, 'D': D}
    _L1_attn_all = _L1_attn_setup()
    _L1_attn_in = {k: v for k, v in _L1_attn_all.items() if k in ('a_params', 'B_w', 'C_w', 'D')}
    del _L1_attn_all

    def _L1_ffn_setup():
        import jax, jax.numpy as jnp
        import numpy as np
        D_MODEL = 256
        D_FF = 1024
        N_EXPERTS = 8
        TOP_K = 2

        def _ffn(x, w1, b1, w2, b2):
            h = jax.nn.gelu(x @ w1.T + b1)
            return h @ w2.T + b2
        key = jax.random.key(seed)
        ks = jax.random.split(key, 12)
        s = 0.02
        x = jax.random.normal(ks[0], (4, 512, D_MODEL), dtype=jnp.float32)
        shared_w1 = jax.random.normal(ks[1], (D_FF, D_MODEL), dtype=jnp.float32) * s
        shared_b1 = jnp.zeros((D_FF,), dtype=jnp.float32)
        shared_w2 = jax.random.normal(ks[2], (D_MODEL, D_FF), dtype=jnp.float32) * s
        shared_b2 = jnp.zeros((D_MODEL,), dtype=jnp.float32)
        router_w = jax.random.normal(ks[3], (N_EXPERTS, D_MODEL), dtype=jnp.float32) * s
        router_b = jnp.zeros((N_EXPERTS,), dtype=jnp.float32)
        spec_w1 = jax.random.normal(ks[4], (N_EXPERTS, D_FF, D_MODEL), dtype=jnp.float32) * s
        spec_b1 = jnp.zeros((N_EXPERTS, D_FF), dtype=jnp.float32)
        spec_w2 = jax.random.normal(ks[5], (N_EXPERTS, D_MODEL, D_FF), dtype=jnp.float32) * s
        spec_b2 = jnp.zeros((N_EXPERTS, D_MODEL), dtype=jnp.float32)
        return dict(x=x, shared_w1=shared_w1, shared_b1=shared_b1, shared_w2=shared_w2, shared_b2=shared_b2, router_w=router_w, router_b=router_b, spec_w1=spec_w1, spec_b1=spec_b1, spec_w2=spec_w2, spec_b2=spec_b2)
    _L1_ffn_all = _L1_ffn_setup()
    _L1_ffn_in = {k: v for k, v in _L1_ffn_all.items() if k in ('shared_w1', 'shared_b1', 'shared_w2', 'shared_b2', 'router_w', 'router_b', 'spec_w1', 'spec_b1', 'spec_w2', 'spec_b2')}
    del _L1_ffn_all
    return {'x': x, 'x_txt': x_txt, 'L0_tok_scharr': _L0_tok_in['scharr'], 'L0_txt_U': _L0_txt_in['U'], 'L0_txt_s': _L0_txt_in['s'], 'L0_txt_Vt': _L0_txt_in['Vt'], 'L0_attn_Wq': _L0_attn_in['Wq'], 'L0_attn_bq': _L0_attn_in['bq'], 'L0_attn_Wk': _L0_attn_in['Wk'], 'L0_attn_bk': _L0_attn_in['bk'], 'L0_attn_Wv': _L0_attn_in['Wv'], 'L0_attn_bv': _L0_attn_in['bv'], 'L0_attn_Wo': _L0_attn_in['Wo'], 'L0_attn_bo': _L0_attn_in['bo'], 'L0_ffn_w_router': _L0_ffn_in['w_router'], 'L0_ffn_w_block': _L0_ffn_in['w_block'], 'L1_attn_a_params': _L1_attn_in['a_params'], 'L1_attn_B_w': _L1_attn_in['B_w'], 'L1_attn_C_w': _L1_attn_in['C_w'], 'L1_attn_D': _L1_attn_in['D'], 'L1_ffn_shared_w1': _L1_ffn_in['shared_w1'], 'L1_ffn_shared_b1': _L1_ffn_in['shared_b1'], 'L1_ffn_shared_w2': _L1_ffn_in['shared_w2'], 'L1_ffn_shared_b2': _L1_ffn_in['shared_b2'], 'L1_ffn_router_w': _L1_ffn_in['router_w'], 'L1_ffn_router_b': _L1_ffn_in['router_b'], 'L1_ffn_spec_w1': _L1_ffn_in['spec_w1'], 'L1_ffn_spec_b1': _L1_ffn_in['spec_b1'], 'L1_ffn_spec_w2': _L1_ffn_in['spec_w2'], 'L1_ffn_spec_b2': _L1_ffn_in['spec_b2']}

def reference(x, x_txt, L0_tok_scharr, L0_txt_U, L0_txt_s, L0_txt_Vt, L0_attn_Wq, L0_attn_bq, L0_attn_Wk, L0_attn_bk, L0_attn_Wv, L0_attn_bv, L0_attn_Wo, L0_attn_bo, L0_ffn_w_router, L0_ffn_w_block, L1_attn_a_params, L1_attn_B_w, L1_attn_C_w, L1_attn_D, L1_ffn_shared_w1, L1_ffn_shared_b1, L1_ffn_shared_w2, L1_ffn_shared_b2, L1_ffn_router_w, L1_ffn_router_b, L1_ffn_spec_w1, L1_ffn_spec_b1, L1_ffn_spec_w2, L1_ffn_spec_b2):
    import jax
    import jax.numpy as jnp

    def _L0_tok_ref(x, scharr):
        import jax, jax.numpy as jnp
        import numpy as np
        _GRAY_W = (0.2989, 0.587, 0.114)
        w = jnp.asarray(_GRAY_W, dtype=x.dtype)
        gray = jnp.einsum('bchw,c->bhw', x, w)[:, None]
        edges = jax.lax.conv_general_dilated(gray, scharr, window_strides=(1, 1), padding='SAME', dimension_numbers=('NCHW', 'OIHW', 'NCHW'))
        abs_edges = jnp.sqrt(jnp.square(edges))
        edge = abs_edges.sum(axis=1) / 2
        return edge

    def _L0_txt_ref(input, U, s, Vt):
        import jax, jax.numpy as jnp
        import numpy as np
        V, R, D = (25000, 64, 256)
        B, S = (8, 512)
        weight = U * s @ Vt
        return weight[input]

    def _L0_attn_ref(x, Wq, bq, Wk, bk, Wv, bv, Wo, bo):
        import jax, jax.numpy as jnp
        import numpy as np
        D_MODEL = 256
        N_HEADS = 16
        D_K = D_MODEL // N_HEADS
        SEQ = 1024
        BATCH = 2
        LOCAL_WINDOW = 128
        SCALE = 1.0 / float(np.sqrt(D_K))
        INIT = 1.0 / float(np.sqrt(D_MODEL))

        def _local_mask(seq_len: int) -> jnp.ndarray:
            i = jnp.arange(seq_len)[:, None]
            j = jnp.arange(seq_len)[None, :]
            return (j <= i) & (j >= i - LOCAL_WINDOW)
        B, S, _ = x.shape
        q = (x @ Wq.T + bq).reshape(B, S, N_HEADS, D_K)
        k = (x @ Wk.T + bk).reshape(B, S, N_HEADS, D_K)
        v = (x @ Wv.T + bv).reshape(B, S, N_HEADS, D_K)
        scores = jnp.einsum('bqhd,bkhd->bhqk', q, k) * SCALE
        mask = _local_mask(S)[None, None]
        scores = jnp.where(mask, scores, jnp.float32(-10000.0))
        attn = jax.nn.softmax(scores, axis=-1) + jnp.float32(1e-09)
        ctx = jnp.einsum('bhqk,bkhd->bqhd', attn, v).reshape(B, S, D_MODEL)
        return ctx @ Wo.T + bo

    def _L0_ffn_ref(x, w_router, w_block):
        import jax, jax.numpy as jnp
        import numpy as np
        CAPACITY_RATIO = 0.75
        B, L, D = x.shape
        k = max(1, int(L * CAPACITY_RATIO))
        scores = jnp.einsum('bld,d->bl', x, w_router)
        _, top_idx = jax.lax.top_k(scores, k)
        selected = jnp.take_along_axis(x, top_idx[:, :, None], axis=1)
        processed = jax.nn.gelu(jnp.einsum('bkd,de->bke', selected, w_block))
        batch_idx = jnp.arange(B)[:, None]
        out = x.at[batch_idx, top_idx].set(processed)
        return out

    def _L1_attn_ref(u, a_params, B_w, C_w, D):
        import jax, jax.numpy as jnp
        import numpy as np
        BATCH, SEQ, D_MODEL, STATE_DIM = (8, 512, 256, 256)

        def _cayley_circulant_eigenvalues(a_params, n):
            half_n = n // 2
            a_full = jnp.zeros((n,), dtype=a_params.dtype)
            a_full = a_full.at[1:half_n].set(a_params[:half_n - 1])
            a_full = a_full.at[half_n + 1:].set(-a_params[:half_n - 1][::-1])
            omega = jnp.fft.fft(a_full).imag
            w2 = omega * omega
            denom = 1.0 + w2
            return ((1.0 - w2) / denom + 1j * (-2.0 * omega / denom)).astype(jnp.complex64)
        n = B_w.shape[0]
        lambdas = _cayley_circulant_eigenvalues(a_params, n)
        Bu = jnp.einsum('bsd,nd->bsn', u, B_w)

        def step(h, bu_t):
            Wh = jnp.fft.ifft(lambdas * jnp.fft.fft(h.astype(jnp.float32))).real.astype(h.dtype)
            h_new = Wh + bu_t
            return (h_new, h_new)
        h0 = jnp.zeros((u.shape[0], n), dtype=u.dtype)
        _, hs = jax.lax.scan(step, h0, jnp.swapaxes(Bu, 0, 1))
        y = jnp.einsum('sbn,dn->bsd', hs, C_w) + D * u
        return y

    def _L1_ffn_ref(x, shared_w1, shared_b1, shared_w2, shared_b2, router_w, router_b, spec_w1, spec_b1, spec_w2, spec_b2):
        import jax, jax.numpy as jnp
        import numpy as np
        D_MODEL = 256
        D_FF = 1024
        N_EXPERTS = 8
        TOP_K = 2

        def _ffn(x, w1, b1, w2, b2):
            h = jax.nn.gelu(x @ w1.T + b1)
            return h @ w2.T + b2
        B, T, D = x.shape
        xf = x.reshape(-1, D)
        U = xf.shape[0]
        logits = xf @ router_w.T + router_b
        routing = jax.nn.softmax(logits, axis=-1)
        sel_w, sel_idx = jax.lax.top_k(routing, TOP_K)
        sel_w = sel_w / sel_w.sum(axis=-1, keepdims=True)
        comb = jnp.zeros_like(routing).at[jnp.arange(U)[:, None], sel_idx].set(sel_w)
        shared_out = _ffn(xf, shared_w1, shared_b1, shared_w2, shared_b2)

        def body(acc, params):
            w1, b1, w2, b2, we = params
            return (acc + we[:, None] * _ffn(xf, w1, b1, w2, b2), None)
        acc0 = jnp.zeros_like(shared_out)
        acc, _ = jax.lax.scan(body, acc0, (spec_w1, spec_b1, spec_w2, spec_b2, comb.T))
        return (shared_out + acc).reshape(B, T, D)
    h = _L0_tok_ref(x, L0_tok_scharr)
    h = jnp.concatenate([h, _L0_txt_ref(x_txt, L0_txt_U, L0_txt_s, L0_txt_Vt)], axis=1)
    h = h + _L0_attn_ref(_layernorm(h, axis=-1), L0_attn_Wq, L0_attn_bq, L0_attn_Wk, L0_attn_bk, L0_attn_Wv, L0_attn_bv, L0_attn_Wo, L0_attn_bo)
    h = h + _L0_ffn_ref(_layernorm(h, axis=-1), L0_ffn_w_router, L0_ffn_w_block)
    h = h + _L1_attn_ref(_layernorm(h, axis=-1), L1_attn_a_params, L1_attn_B_w, L1_attn_C_w, L1_attn_D)
    h = h + _L1_ffn_ref(_layernorm(h, axis=-1), L1_ffn_shared_w1, L1_ffn_shared_b1, L1_ffn_shared_w2, L1_ffn_shared_b2, L1_ffn_router_w, L1_ffn_router_b, L1_ffn_spec_w1, L1_ffn_spec_b1, L1_ffn_spec_w2, L1_ffn_spec_b2)
    return h

_drawn_inputs = setup_inputs


def setup_inputs(seed=0):
    import zlib

    import numpy as np

    out = dict(_drawn_inputs(seed))
    spreads = {'L0_attn_bq': (0.0, 0.405),
     'L0_attn_bk': (0.0, 0.8),
     'L0_attn_bv': (0.0, 0.1),
     'L0_attn_bo': (0.0, 0.1),
     'L1_attn_D': (0.0, 0.8),
     'L1_ffn_shared_b1': (0.0, 0.8),
     'L1_ffn_shared_b2': (0.0, 0.8),
     'L1_ffn_router_b': (0.0, 0.8),
     'L1_ffn_spec_b1': (0.0, 0.8),
     'L1_ffn_spec_b2': (0.0, 0.8)}
    factors = {'L1_ffn_shared_w1': 8.0,
     'L1_ffn_shared_w2': 8.0,
     'L1_ffn_router_w': 8.0,
     'L1_ffn_spec_w1': 8.0,
     'L1_ffn_spec_w2': 8.0}
    for name, (base, spread) in spreads.items():
        noise = np.random.default_rng([zlib.crc32(name.encode()), seed]).standard_normal(out[name].shape)
        drawn = base * np.exp(spread * noise) if base else spread * noise
        out[name] = jnp.asarray(drawn.astype(out[name].dtype))
    for name, factor in factors.items():
        out[name] = (out[name] * factor).astype(out[name].dtype)
    return out
```

```python
from contextlib import ExitStack

import numpy as np
import concourse.bass as bass
from concourse import mybir

F32 = mybir.dt.float32
BF16 = mybir.dt.bfloat16
I32 = mybir.dt.int32
U32 = mybir.dt.uint32
ALU = mybir.AluOpType
ACT = mybir.ActivationFunctionType
AX_X = mybir.AxisListType.X

P = 128
NB = 16
IMG = 256
D = 256
KB = D // P
NT = 3
T = NT * P
R = 64
NH, DK = 16, 16
SCALE = 0.25
MASKED = -30000.0
GRAY = (0.2989, 0.587, 0.114)
KEEP = 288
F = 1024
FB = F // P
NE = 8
EPS = 1e-5
TILES = NB * NT
CHUNK = 2 * P
CHUNKS = NB * T * 2 // CHUNK + NE
SLOT_TILES = 2 * (CHUNKS + 1)
RAMP = NB * T // CHUNK
SCAT = 12
COMB = 4
HG = 4
NU = NT * NH // HG


class Signal:

    def __init__(self, sem, per, start):
        self.sem, self.per, self.start = sem, per, start

    def at(self, b, n):
        return b * self.per + (n + self.start)


def build(nc, t):
    with ExitStack() as ctx:
        def sb(name, shape, dt=F32):
            return ctx.enter_context(nc.sbuf_tensor(name, shape, dt))

        signals = []

        def signal(name, per):
            signals.append(Signal(ctx.enter_context(nc.semaphore(name)), per, 1))
            return signals[-1]

        def dma_signal(name, per):
            return Signal(ctx.enter_context(nc.semaphore(name)), per, 0)

        ps = ctx.enter_context(nc.psum_tensor("ps", [P, 8, 512], F32))

        ident = sb("ident", [P, P])
        ident_bf = sb("ident_bf", [P, P], BF16)
        mask_f = sb("mask_f", [P, 2 * P])
        mask_bf = sb("mask_bf", [P, 2, 2 * P], BF16)
        ones9 = sb("ones9", [P, P])
        shift = sb("shift", [P, 3, P])
        tap = sb("tap", [P, 18])
        tap_edge = sb("tap_edge", [3, 2, 3])
        band = sb("band", [P, 2, 3, P])
        band_edge = sb("band_edge", [3, 2, 2, P])
        parity = sb("parity", [P, 2])
        wq = sb("wq", [P, KB, D])
        wk = sb("wk", [P, KB, D])
        wv = sb("wv", [P, KB, D])
        wo = sb("wo", [P, KB, D])
        bq = sb("bq", [P, KB])
        bk = sb("bk", [P, KB])
        bv_row = sb("bv_row", [P, D])
        bo_row = sb("bo_row", [P, D])
        vt = sb("vt", [R, D])
        s_col = sb("s_col", [R, 1])
        ids = sb("ids", [P, NB], I32)
        u_all = sb("u_all", [P, NB, R])
        h_all = sb("h_all", [P, NB, NT, D])

        zeros = sb("zeros", [SLOT_TILES, P])
        wr_col = sb("wr_col", [P, KB])
        wr_bc = sb("wr_bc", [P, KB, P])
        wb = sb("wb", [P, KB, D])
        before = sb("before", [P, NT, T])
        after = sb("after", [P, NT, T])
        dft = sb("dft", [P, KB, D])
        idft = sb("idft", [P, KB, D])
        sines = sb("sines", [P, P])
        a_col = sb("a_col", [P, 1])
        b_w = sb("b_w", [P, KB, D])
        c_wT = sb("c_wT", [P, KB, D])
        d_row = sb("d_row", [P, D])
        d_diag = sb("d_diag", [P, KB, P])
        fb = sb("fb", [P, KB, D])
        ce = sb("ce", [P, 2, D])
        turn = sb("turn", [P, 2, T])
        om = sb("om", [P, 8])
        ones_t = sb("ones_t", [P, T])
        rw = sb("rw", [P, KB, NE])
        rb_row = sb("rb_row", [P, NE])
        sw1 = sb("sw1", [P, KB, F])
        sw2 = sb("sw2", [P, FB, D])
        sb1 = sb("sb1", [P, FB])
        sb2_row = sb("sb2_row", [P, D])
        top_v = sb("top_v", [P, NB, NT, 2])
        top_i = sb("top_i", [P, NB, NT, 2])

        spare = sb("spare", [P, 1])
        h = sb("h", [P, NT, D])
        hbo = sb("hbo", [P, NT, D])
        stats = sb("stats", [P, NT, 6])
        mv = sb("mv", [P, NT, 2])
        std = sb("std", [P, NT])
        rstd = sb("rstd", [P, NT])
        xn = sb("xn", [P, NT, D])
        xT = sb("xT", [P, KB, T])
        eps = sb("eps", [P, 1])

        with ExitStack() as space:
            def room(name, shape, dt=F32):
                return space.enter_context(nc.sbuf_tensor(name, shape, dt))

            xin = room("xin", [P, 2, 3, IMG])
            gsum = room("gsum", [P, 2, IMG])
            gray = room("gray", [P, 2, IMG + 2])
            halo = room("halo", [3, 2, IMG])
            edges = room("edges", [P, 2, 2 * IMG])
            ub = room("ub", [P, P])
            usT = room("usT", [R, P])
            qT = room("qT", [P, KB, T])
            km = room("km", [P, KB, 2, T])
            vaug = room("vaug", [P, NT, NH, DK + 1])
            sumv = room("sumv", [P, D])
            mx = room("mx", [P, 2, HG])
            prob = room("prob", [P, 2, HG, 2 * P])
            pT = room("pT", [P, 2, HG, 2, P])
            rden = room("rden", [P, NH])
            cx = room("cx", [P, D])
            cxT = room("cxT", [P, KB, P])

        with ExitStack() as space:
            def room(name, shape, dt=F32):
                return space.enter_context(nc.sbuf_tensor(name, shape, dt))

            srow = room("srow", [P, T])
            junk = room("junk", [P, 2 * NT, T])
            own = room("own", [P, NT])
            count = room("count", [P, 2, NT])
            sel = room("sel", [P, NT])
            g = room("g", [P, NT, D])
            rot = room("rot", [P, 4, T])
            pre = room("pre", [P, 2, T])
            cum = room("cum", [P, 2, T])
            rot2 = room("rot2", [P, 4, T])
            st = room("st", [P, 2, T])
            logit = room("logit", [P, NT, NE])
            v8 = room("v8", [P, NT, NE])
            i8 = room("i8", [P, NT, NE], U32)
            hid = room("hid", [P, FB, T])

        with ExitStack() as space:
            def room(name, shape, dt=F32):
                return space.enter_context(nc.sbuf_tensor(name, shape, dt))

            ltri = room("ltri", [P, P])
            ones1 = room("ones1", [P, P])
            seg = room("seg", [P, NE, TILES])
            ramp = room("ramp", [P, RAMP])
            tok = room("tok", [P, TILES])
            gates = room("gates", [P, 4, TILES])
            hot = room("hot", [P, 2, NE, TILES])
            hot2 = room("hot2", [P, NE, TILES])
            tot = room("tot", [P, NE, TILES])
            incl = room("incl", [P, NE, TILES])
            pos = room("pos", [P, NE, TILES])
            picked = room("picked", [P, 2, NE, TILES])
            pos_f = room("pos_f", [P, 2, TILES])
            pos_i = room("pos_i", [P, 2, TILES], I32)
            over = room("over", [P, NE, RAMP])
            chunks = room("chunks", [P, 3, NE])
            bounds = room("bounds", [P, NE + 1], I32)
            pos_s = room("pos_s", [P, 2, SCAT], I32)
            tok_s = room("tok_s", [P, SCAT])
            slots_r = room("slots_r", [SLOT_TILES, P])
            slots_i = room("slots_i", [P, SLOT_TILES], I32)
            idx_s = room("idx_s", [P, 2], I32)
            xg = room("xg", [P, 2, D])
            xgT = room("xgT", [P, KB, 2 * P])
            w1 = [room(f"w1_{j}", [P, KB, F]) for j in range(2)]
            w2 = [room(f"w2_{j}", [P, FB, D]) for j in range(2)]
            b1 = [room(f"b1_{j}", [P, FB]) for j in range(2)]
            b2_row = [room(f"b2_row{j}", [P, D]) for j in range(2)]
            hidg = room("hidg", [P, FB, 2 * P])
            yb = room("yb", [P, 2, D])
            pos_g = room("pos_g", [P, 2, COMB], I32)
            yg = hidg[:].rearrange("p (k c) d -> p k c d", k=2)
            part = w2[0][:, 0:COMB]
            res = w2[0][:, COMB:2 * COMB]

        slot_dram = nc.dram_tensor("slot_token", (SLOT_TILES * P, 1), F32, kind="Internal").ap()
        y_dram = nc.dram_tensor("y_rows", (SLOT_TILES * P, D), F32, kind="Internal").ap()
        xn_dram = nc.dram_tensor("xn_rows", (NB * T, D), F32, kind="Internal").ap()

        zeros_ready = signal("zeros_ready", 0)
        mats_done = signal("mats_done", 0)
        mats_read = signal("mats_read", 0)
        loaded = dma_signal("weights_loaded", 0)
        set_up = signal("constants_ready", 0)
        setup_step = signal("setup_step", 0)
        ids_loaded = dma_signal("ids_loaded", 0)
        u_gathered = dma_signal("u_gathered", 0)
        x_loaded = dma_signal("x_loaded", 32)
        gray_ready = signal("gray_ready", 1)
        halo_loaded = dma_signal("halo_loaded", 96)
        conv_done = signal("conv_done", 2)
        abs_done = signal("abs_done", 2)
        h_ready = signal("h_ready", 1)
        ub_ready = signal("ub_ready", 1)
        uT_ready = signal("uT_ready", 1)
        usT_ready = signal("usT_ready", 1)
        text_done = signal("text_done", 1)
        var_ready = signal("var_ready", 1)
        std_ready = signal("std_ready", 1)
        xn_ready = signal("xn_ready", 1)
        xT_turned = signal("xT_turned", 1)
        xT_ready = signal("xT_ready", 1)
        proj_done = signal("proj_done", 3)
        q_ready = signal("q_ready", 1)
        k_ready = signal("k_ready", 1)
        v_ready = signal("v_ready", 1)
        sumv_done = signal("sumv_done", 1)
        scores_done = signal("scores_done", NU)
        sub_done = signal("sub_done", NU)
        exp_done = signal("exp_done", NU)
        turned = signal("probs_turned", NU)
        pT_ready = signal("pT_ready", NU)
        pv_done = signal("pv_done", NU)
        pv_read = signal("pv_read", NT)
        cx_ready = signal("cx_ready", NT)
        cx_turned = signal("cx_turned", NT)
        cxT_ready = signal("cxT_ready", NT)
        wo_done = signal("wo_done", NT)
        h1_ready = signal("h1_ready", NT)
        hbo_ready = signal("hbo_ready", 1)
        dve1 = signal("dve1_step", 5 + NU + NT)
        h1_at_rest = signal("h1_at_rest", 0)
        var2_ready = signal("var2_ready", 3)
        std2_ready = signal("std2_ready", 3)
        xn2_ready = signal("xn2_ready", 3)
        x2_turned = signal("x2_turned", 3)
        x2_ready = signal("x2_ready", 3)
        block_done = signal("block_done", 1)
        block_ready = signal("block_ready", 1)
        u_done = signal("u_done", 1)
        u_read = signal("u_read", 1)
        cum_ready = signal("cum_ready", 1)
        state_re = signal("state_re_ready", 1)
        state_im = signal("state_im_ready", 1)
        rot2_step = signal("rot2_step", 1)
        ssm_done = signal("ssm_done", 1)
        h3_ready = signal("h3_ready", 1)
        hb2_ready = signal("hb2_ready", 1)
        logit_done = signal("logit_done", 1)
        logit_read = signal("logit_read", 1)
        up_done = signal("up_done", FB)
        hid_ready = signal("hid_ready", FB)
        down_done = signal("down_done", 1)
        h4_ready = signal("h4_ready", 1)
        xn_stored = dma_signal("xn_stored", 16)
        dve2 = signal("dve2_step", 17)
        zeroed = dma_signal("slots_zeroed", 0)
        route_loaded = dma_signal("route_loaded", 0)
        diff_ready = signal("diff_ready", 0)
        ratio_ready = signal("ratio_ready", 0)
        hot_ready = signal("hot_ready", 0)
        rank_done = signal("rank_done", 0)
        route_step = signal("route_step", 0)
        bounds_ready = signal("bounds_ready", 0)
        pos_ready = signal("pos_ready", 0)
        staged = signal("scatter_staged", 1)
        scattered = dma_signal("scattered", 16 * 2 * SCAT)
        slots_loaded = dma_signal("slots_loaded", 0)
        slots_turned = signal("slots_turned", 0)
        slots_ready = signal("slots_ready", 0)
        w_loaded = [dma_signal(f"w_loaded{j}", 64) for j in range(2)]
        gather_go = signal("gather_go", 1)
        idx_ready = signal("idx_ready", 1)
        xg_loaded = dma_signal("xg_loaded", 32)
        xg_turned = signal("xg_turned", 1)
        xgT_ready = signal("xgT_ready", 1)
        eup_done = signal("expert_up_done", FB)
        ehid_ready = signal("expert_hid_ready", FB)
        edown_done = signal("expert_down_done", 2)
        y_ready = signal("y_ready", 2)
        y_stored = dma_signal("y_stored", 16)
        y_sent = signal("y_sent", 1)
        pos_g_ready = signal("pos_g_ready", 1)
        yg_loaded = dma_signal("yg_loaded", 32 * COMB)
        yg_read = signal("yg_read", 1)
        part_ready = signal("part_ready", 1)
        res_ready = signal("res_ready", 1)
        res_sent = signal("res_sent", 1)
        stored = dma_signal("stored", 16)

        block = ctx.enter_context(nc.Block())

        weight_loads = [
            (ident, t["ident"]), (mask_f, t["mask"]), (shift, t["shift"]), (parity, t["parity"]),
            (wq, t["wqT"]), (wk, t["wkT"]), (wv, t["wvT"]), (wo, t["woT"]), (bq, t["bq"]), (bk, t["bk"]),
            (bv_row, t["bv"].partition_broadcast(P)), (bo_row, t["bo"].partition_broadcast(P)),
            (tap, t["scharr"].partition_broadcast(P)), (tap_edge, t["scharr_dx"]),
            (vt, t["vt"]), (s_col, t["s"]), (wr_col, t["wr"]), (wb, t["wb"]), (before, t["before"]),
            (dft, t["dft"]), (idft, t["idft"]), (sines, t["sines"]), (a_col, t["a"]), (b_w, t["b_w"]),
            (c_wT, t["c_wT"]), (d_row, t["d"].partition_broadcast(P)), (rw, t["rwT"]),
            (rb_row, t["rb"].partition_broadcast(P)), (sw1, t["sw1"]), (sw2, t["sw2"]), (sb1, t["sb1"]),
            (sb2_row, t["sb2"].partition_broadcast(P)),
        ]
        NLOAD = 16 * len(weight_loads)
        NSET = 6

        def expert_bounds(eng, e):
            lo = eng.value_load(bounds[0:1, bass.ds(e, 1)], min_val=0, max_val=CHUNKS - 1)
            hi = eng.value_load(bounds[0:1, bass.ds(e + 1, 1)], min_val=1, max_val=CHUNKS)
            return lo, hi

        @block.sync
        def _(sp):
            sp.dma_start(ids[:], t["ids"]).then_inc(ids_loaded.sem, 16)
            for dst, src in weight_loads:
                sp.dma_start(dst[:], src).then_inc(loaded.sem, 16)
            sp.wait_ge(zeros_ready.sem, zeros_ready.at(0, 1))
            sp.dma_start(slot_dram.rearrange("(c p) o -> c (p o)", p=P), zeros[:]).then_inc(zeroed.sem, 16)
            with sp.Fori(0, NB) as b:
                sp.wait_ge(gray_ready.sem, gray_ready.at(b, 0))
                for rt in range(2):
                    src = t["x"][bass.ds(b, 1), :, rt * P:(rt + 1) * P, :].rearrange("o c p w -> p (o c) w")
                    sp.dma_start(xin[:, rt], src).then_inc(x_loaded.sem, 16)
                sp.wait_ge(gray_ready.sem, gray_ready.at(b, 1))
                sp.wait_ge(conv_done.sem, conv_done.at(b, 0))
                for dx in range(3):
                    sp.dma_start(halo[dx:dx + 1, 0, :], gray[0:1, 1, dx:dx + IMG]).then_inc(halo_loaded.sem, 16)
                    sp.dma_start(halo[dx:dx + 1, 1, :], gray[P - 1:P, 0, dx:dx + IMG]).then_inc(halo_loaded.sem, 16)
            sp.wait_ge(h1_ready.sem, h1_ready.at(NB - 1, NT))
            with sp.Fori(0, NB) as b:
                sp.wait_ge(xn2_ready.sem, xn2_ready.at(b, 3))
                rows = xn_dram.rearrange("(b i p) d -> b p i d", b=NB, i=NT)
                sp.dma_start(rows[bass.ds(b, 1)].rearrange("o p i d -> p (o i) d"), xn[:]).then_inc(xn_stored.sem, 16)
            sp.wait_ge(h4_ready.sem, h4_ready.at(NB - 1, 1))
            for dst, src in ((ltri, t["ltri"]), (ramp, t["ramp"].partition_broadcast(P)), (tok, t["tok"])):
                sp.dma_start(dst[:], src).then_inc(route_loaded.sem, 16)

            def load_weights(half, e):
                for dst, src in ((w1, t["w1"][e]), (w2, t["w2"][e]), (b1, t["b1"][e])):
                    sp.dma_start(dst[half][:], src).then_inc(w_loaded[half].sem, 16)
                sp.dma_start(b2_row[half][:], t["b2"][e].partition_broadcast(P)).then_inc(w_loaded[half].sem, 16)

            def load_weights_at(half, e):
                for dst, src in ((w1, t["w1"]), (w2, t["w2"])):
                    sp.dma_start(dst[half][:], src[bass.ds(e, 1)].rearrange("o p k n -> (o p) k n")
                                 ).then_inc(w_loaded[half].sem, 16)
                sp.dma_start(b1[half][:], t["b1"][bass.ds(e, 1)].rearrange("o p n -> (o p) n")
                             ).then_inc(w_loaded[half].sem, 16)
                sp.dma_start(b2_row[half][:], t["b2"][bass.ds(e, 1)].to_broadcast([P, D])
                             ).then_inc(w_loaded[half].sem, 16)

            load_weights(0, 0)
            load_weights(1, 1)
            sp.wait_ge(scattered.sem, scattered.at(TILES // SCAT - 1, scattered.per))
            sp.dma_start(slots_r[:], slot_dram.rearrange("(c p) o -> c (p o)", p=P)).then_inc(slots_loaded.sem, 16)
            sp.wait_ge(bounds_ready.sem, bounds_ready.at(0, 1))

            def store_chunk(j):
                sp.dma_start(y_dram.rearrange("(j c p) d -> j p c d", c=2, p=P)[bass.ds(j, 1)]
                             .rearrange("o p c d -> p (o c) d"), yb[:]).then_inc(y_stored.sem, 16)
                sp.wait_ge(y_stored.sem, y_stored.at(j, 16))
                sp.sem_inc(y_sent.sem, 1)

            def store_chunks(e):
                lo, hi = expert_bounds(sp, e)
                with sp.Fori(lo, hi) as j:
                    sp.wait_ge(y_ready.sem, y_ready.at(j, 2))
                    store_chunk(j)

            with sp.Fori(0, NE // 2 - 1) as q:
                for half in range(2):
                    store_chunks(2 * q + half)
                    load_weights_at(half, 2 * q + (2 + half))
            for half in range(2):
                store_chunks(NE - 2 + half)
            total = sp.value_load(bounds[0:1, NE:NE + 1], min_val=NE, max_val=CHUNKS)
            with sp.Fori(total, CHUNKS + 1) as j:
                store_chunk(j)
            with sp.Fori(0, TILES // COMB) as c:
                sp.wait_ge(res_ready.sem, res_ready.at(c, 1))
                sp.dma_start(t["out"].rearrange("(c i p) d -> c p i d", i=COMB, p=P)[bass.ds(c, 1)]
                             .rearrange("o p i d -> p (o i) d"), res).then_inc(stored.sem, 16)
                sp.wait_ge(stored.sem, stored.at(c, 16))
                sp.sem_inc(res_sent.sem, 1)

        @block.gpsimd
        def _(pool):
            for sig in signals:
                pool.sem_inc(sig.sem, 1)
            pool.memset(zeros[:], 0.0).then_inc(zeros_ready.sem, 1)
            pool.wait_ge(ids_loaded.sem, ids_loaded.at(0, 16))
            for b in range(NB):
                pool.indirect_dma_start(u_all[:, b, :], None, t["U"],
                                        bass.IndirectOffsetOnAxis(ids[:, b:b + 1], axis=0)
                                        ).then_inc(u_gathered.sem, 16)
            pool.wait_ge(loaded.sem, loaded.at(0, NLOAD))
            with pool.Fori(0, NB) as b:
                pool.wait_ge(h_ready.sem, h_ready.at(b, 1))
                pool.wait_ge(h1_ready.sem, h1_ready.at(b, 0))
                for i in range(NT):
                    ins = pool.tensor_tensor(hbo[:, i], h[:, i], bo_row[:], ALU.add)
                ins.then_inc(hbo_ready.sem, 1)

            pool.wait_ge(h1_ready.sem, h1_ready.at(NB - 1, NT))
            with pool.Fori(0, NB) as b:
                pool.wait_ge(cum_ready.sem, cum_ready.at(b, 1))
                pool.tensor_tensor(rot2[:, 2], cum[:, 0], turn[:, 1], ALU.mult)
                pool.tensor_tensor(rot2[:, 3], cum[:, 1], turn[:, 0], ALU.mult).then_inc(rot2_step.sem, 1)
                pool.wait_ge(rot2_step.sem, rot2_step.at(b, 1))
                pool.wait_ge(ssm_done.sem, ssm_done.at(b, 0))
                pool.tensor_tensor(st[:, 1], rot2[:, 2], rot2[:, 3], ALU.add).then_inc(state_im.sem, 1)
                pool.wait_ge(h3_ready.sem, h3_ready.at(b, 1))
                pool.wait_ge(h4_ready.sem, h4_ready.at(b, 0))
                for i in range(NT):
                    ins = pool.tensor_tensor(hbo[:, i], h[:, i], sb2_row[:], ALU.add)
                ins.then_inc(hb2_ready.sem, 1)

            pool.wait_ge(pos_ready.sem, pos_ready.at(0, 1))
            pool.wait_ge(zeroed.sem, zeroed.at(0, 16))
            with pool.Fori(0, TILES // SCAT) as c:
                pool.tensor_copy(pos_s[:], pos_i[:, :, bass.ds(c * SCAT, SCAT)])
                pool.tensor_copy(tok_s[:], tok[:, bass.ds(c * SCAT, SCAT)]).then_inc(staged.sem, 1)
                pool.wait_ge(staged.sem, staged.at(c, 1))
                pool.sem_inc(gather_go.sem, 1)
                for k in range(2):
                    for i in range(SCAT):
                        pool.indirect_dma_start(slot_dram, bass.IndirectOffsetOnAxis(pos_s[:, k, i:i + 1], axis=0),
                                                tok_s[:, i:i + 1], None).then_inc(scattered.sem, 16)
                pool.wait_ge(scattered.sem, scattered.at(c, scattered.per))
            pool.wait_ge(slots_ready.sem, slots_ready.at(0, 1))
            pool.wait_ge(xn_stored.sem, xn_stored.at(NB - 1, 16))
            total = pool.value_load(bounds[0:1, NE:NE + 1], min_val=NE, max_val=CHUNKS)
            with pool.Fori(0, total + 1) as j:
                pool.wait_ge(xg_turned.sem, xg_turned.at(j, 0))
                pool.tensor_copy(idx_s[:], slots_i[:, bass.ds(2 * j, 2)]).then_inc(idx_ready.sem, 1)
                pool.wait_ge(idx_ready.sem, idx_ready.at(j, 1))
                pool.sem_inc(gather_go.sem, 1)
                for k in range(2):
                    pool.indirect_dma_start(xg[:, k], None, xn_dram,
                                            bass.IndirectOffsetOnAxis(idx_s[:, k:k + 1], axis=0)
                                            ).then_inc(xg_loaded.sem, 16)
            pool.wait_ge(y_sent.sem, y_sent.at(CHUNKS + 1, 0))
            with pool.Fori(0, TILES // COMB) as c:
                pool.wait_ge(yg_read.sem, yg_read.at(c, 0))
                pool.tensor_copy(pos_g[:], pos_i[:, :, bass.ds(c * COMB, COMB)]).then_inc(pos_g_ready.sem, 1)
                pool.wait_ge(pos_g_ready.sem, pos_g_ready.at(c, 1))
                pool.sem_inc(gather_go.sem, 1)
                for i in range(COMB):
                    for k in range(2):
                        pool.indirect_dma_start(yg[:, k, i], None, y_dram,
                                                bass.IndirectOffsetOnAxis(pos_g[:, k, i:i + 1], axis=0)
                                                ).then_inc(yg_loaded.sem, 16)

        @block.scalar
        def _(act):
            act.wait_ge(loaded.sem, loaded.at(0, NLOAD))
            act.wait_ge(u_gathered.sem, u_gathered.at(0, 16 * NB))
            act.wait_ge(set_up.sem, set_up.at(0, NSET))
            with act.Fori(0, NB) as b:
                act.wait_ge(uT_ready.sem, uT_ready.at(b, 0))
                act.activation(ub[:, 0:R], u_all[:, bass.ds(b, 1), :], ACT.Copy).then_inc(ub_ready.sem, 1)
                act.wait_ge(h_ready.sem, h_ready.at(b, 0))
                for i in range(2):
                    act.wait_ge(conv_done.sem, conv_done.at(b, i + 1))
                    act.activation(edges[:, i], ps[:, i], ACT.Abs, scale=0.5).then_inc(abs_done.sem, 1)
                act.wait_ge(var_ready.sem, var_ready.at(b, 1))
                act.activation(std[:], mv[:, :, 1], ACT.Sqrt, bias=eps[:]).then_inc(std_ready.sem, 1)
                act.wait_ge(xT_turned.sem, xT_turned.at(b, 1))
                act.wait_ge(proj_done.sem, proj_done.at(b, 0))
                act.activation(xT[:], ps[:, 4:6, 0:T], ACT.Copy).then_inc(xT_ready.sem, 1)
                act.wait_ge(proj_done.sem, proj_done.at(b, 1))
                act.wait_ge(scores_done.sem, scores_done.at(b, 0))
                for m in range(KB):
                    ins = act.activation(qT[:, m], ps[:, m, 0:T], ACT.Identity, bias=bq[:, m:m + 1], scale=SCALE)
                ins.then_inc(q_ready.sem, 1)
                for s in range(NU + 3):
                    if s < NU:
                        w = slice(0 if s >= HG else P, 2 * P)
                        act.wait_ge(sub_done.sem, sub_done.at(b, s + 1))
                        act.activation(prob[:, s % 2, :, w], prob[:, s % 2, :, w], ACT.Exp
                                       ).then_inc(exp_done.sem, 1)
                    if 1 <= s <= NU:
                        u = s - 1
                        k0 = 0 if u >= HG else 1
                        act.wait_ge(turned.sem, turned.at(b, u + 1))
                        act.wait_ge(pv_done.sem, pv_done.at(b, max(u - 1, 0)))
                        act.activation(pT[:, u % 2, :, k0:2, :],
                                       ps[:, 4:6, :].rearrange("p a (h k q) -> p (a h) k q", h=2, k=2)[:, :, k0:2, :],
                                       ACT.Copy).then_inc(pT_ready.sem, 1)
                    if s >= 6 and (s - 6) % 4 == 0:
                        i = (s - 6) // 4
                        act.wait_ge(cx_turned.sem, cx_turned.at(b, i + 1))
                        act.wait_ge(wo_done.sem, wo_done.at(b, i))
                        act.activation(cxT[:], ps[:, 7, 0:D].rearrange("p (k q) -> p k q", k=KB), ACT.Copy
                                       ).then_inc(cxT_ready.sem, 1)

            act.wait_ge(h1_ready.sem, h1_ready.at(NB - 1, NT))
            with act.Fori(0, NB) as b:
                for n in range(3):
                    act.wait_ge(var2_ready.sem, var2_ready.at(b, n + 1))
                    act.activation(std[:], mv[:, :, 1], ACT.Sqrt, bias=eps[:]).then_inc(std2_ready.sem, 1)
                    act.wait_ge(x2_turned.sem, x2_turned.at(b, n + 1))
                    if n == 0:
                        act.wait_ge(up_done.sem, up_done.at(b, 0))
                    elif n == 1:
                        act.wait_ge(block_done.sem, block_done.at(b, 1))
                    else:
                        act.wait_ge(ssm_done.sem, ssm_done.at(b, 1))
                    act.activation(xT[:], ps[:, 6:8, 0:T], ACT.Copy).then_inc(x2_ready.sem, 1)
                    if n == 0:
                        act.wait_ge(block_done.sem, block_done.at(b, 1))
                        act.activation(srow[:], ps[:, 0, 0:T], ACT.Copy)
                        act.activation(g[:].rearrange("p i d -> p (i d)"),
                                       ps[:, 1:3, :].rearrange("p a c -> p (a c)")[:, 0:NT * D],
                                       ACT.Gelu_apprx_tanh).then_inc(block_ready.sem, 1)
                act.wait_ge(down_done.sem, down_done.at(b, 0))
                for f in range(FB):
                    act.wait_ge(up_done.sem, up_done.at(b, f + 1))
                    act.activation(hid[:, f], ps[:, 3 + f % 2, 0:T], ACT.Gelu_apprx_tanh, bias=sb1[:, f:f + 1]
                                   ).then_inc(hid_ready.sem, 1)

            act.wait_ge(diff_ready.sem, diff_ready.at(0, 1))
            act.activation(gates[:, 1], gates[:, 0], ACT.Exp).then_inc(ratio_ready.sem, 1)
            act.wait_ge(bounds_ready.sem, bounds_ready.at(0, 1))

            def hidden(q, half, e):
                lo, hi = expert_bounds(act, e)
                with act.Fori(lo, hi) as j:
                    act.wait_ge(w_loaded[half].sem, w_loaded[half].at(q, 64))
                    act.wait_ge(edown_done.sem, edown_done.at(j, 0))
                    for f in range(FB):
                        act.wait_ge(eup_done.sem, eup_done.at(j, f + 1))
                        act.activation(hidg[:, f], ps[:, f % 4, 0:CHUNK], ACT.Gelu_apprx_tanh, bias=b1[half][:, f:f + 1]
                                       ).then_inc(ehid_ready.sem, 1)

            with act.Fori(0, NE // 2) as q:
                for half in range(2):
                    hidden(q, half, 2 * q + half)

        @block.vector
        def _(dve):
            dve.wait_ge(loaded.sem, loaded.at(0, NLOAD))
            steps = [0]

            def link(ins):
                steps[0] += 1
                ins.then_inc(setup_step.sem, 1)
                dve.wait_ge(setup_step.sem, setup_step.at(0, steps[0]))

            dve.memset(ones9[:], 1e-9).then_inc(set_up.sem, 1)
            dve.memset(eps[:], EPS).then_inc(set_up.sem, 1)
            dve.memset(vaug[:], 1.0).then_inc(set_up.sem, 1)
            dve.memset(ub[:], 0.0)
            link(dve.memset(gray[:], 0.0))
            dve.tensor_copy(ident_bf[:], ident[:])
            for j in range(2):
                ins = dve.tensor_copy(mask_bf[:, j], mask_f[:])
            ins.then_inc(set_up.sem, 1)
            link(dve.memset(band_edge[:], 0.0))
            for dy in range(3):
                for o in range(2):
                    for dx in range(3):
                        k = (o * 3 + dy) * 3 + dx
                        if dy == 0:
                            ins = dve.tensor_scalar(band[:, o, dx], shift[:, dy], tap[:, k:k + 1], None, ALU.mult)
                        else:
                            ins = dve.scalar_tensor_tensor(out=band[:, o, dx], in0=shift[:, dy], scalar=tap[:, k:k + 1],
                                                           in1=band[:, o, dx], op0=ALU.mult, op1=ALU.add)
                link(ins)
            for o in range(2):
                dve.tensor_copy(band_edge[:, o, 0, P - 1:P], tap_edge[:, o, 2:3])
                ins = dve.tensor_copy(band_edge[:, o, 1, 0:1], tap_edge[:, o, 0:1])
            ins.then_inc(set_up.sem, 1)
            link(dve.tensor_scalar(bq[:], bq[:], SCALE, None, ALU.mult))
            dve.memset(sumv[:], 0.0).then_inc(set_up.sem, 1)

            dve.memset(ones_t[:], 1.0)
            dve.tensor_scalar(after[:], before[:], -1.0, 1.0, ALU.mult, ALU.add)
            for k in range(KB):
                dve.tensor_tensor(d_diag[:, k], ident[:], d_row[:, k * P:(k + 1) * P], ALU.mult)
                ins = dve.tensor_copy(wr_bc[:, k], wr_col[:, k:k + 1].to_broadcast([P, P]))
            link(ins)
            dve.wait_ge(mats_done.sem, mats_done.at(0, 1))
            for k in range(KB):
                dve.tensor_copy(fb[:, k], ps[:, k, 0:D])
                dve.tensor_copy(ce[:, k], ps[:, 2 + k, 0:D])
            w, w2, den, re, im, nim = (om[:, j:j + 1] for j in range(6))
            dve.tensor_copy(w, ps[:, 4, 0:1]).then_inc(mats_read.sem, 1)
            dve.wait_ge(mats_read.sem, mats_read.at(0, 1))
            link(dve.tensor_tensor(w2, w, w, ALU.mult))
            link(dve.tensor_scalar(den, w2, 1.0, None, ALU.add))
            link(dve.reciprocal(nim, den))
            link(dve.tensor_scalar(den, w2, -1.0, 1.0, ALU.mult, ALU.add))
            dve.tensor_tensor(re, den, nim, ALU.mult)
            link(dve.scalar_tensor_tensor(out=im, in0=w, scalar=-2.0, in1=nim, op0=ALU.mult, op1=ALU.mult))
            dve.memset(turn[:, 0, 0:1], 1.0)
            dve.memset(turn[:, 1, 0:1], 0.0)
            n = 1
            while n < T:
                m = min(n, T - n)
                link(dve.tensor_scalar(nim, im, -1.0, None, ALU.mult))
                dve.tensor_scalar(h[:, 0, 0:m], turn[:, 0, 0:m], re, None, ALU.mult)
                dve.tensor_scalar(h[:, 1, 0:m], turn[:, 0, 0:m], im, None, ALU.mult)
                dve.tensor_tensor(w2, im, im, ALU.mult)
                link(dve.tensor_tensor(den, re, im, ALU.mult))
                dve.scalar_tensor_tensor(out=turn[:, 0, n:n + m], in0=turn[:, 1, 0:m], scalar=nim,
                                         in1=h[:, 0, 0:m], op0=ALU.mult, op1=ALU.add)
                link(dve.scalar_tensor_tensor(out=turn[:, 1, n:n + m], in0=turn[:, 1, 0:m], scalar=re,
                                                   in1=h[:, 1, 0:m], op0=ALU.mult, op1=ALU.add))
                dve.tensor_scalar(im, den, 2.0, None, ALU.mult)
                link(dve.tensor_tensor(re, re, re, ALU.mult))
                link(dve.tensor_tensor(re, re, w2, ALU.subtract))
                n *= 2

            with dve.Fori(0, NB) as b:
                steps = [0]

                def link(ins):
                    steps[0] += 1
                    ins.then_inc(dve1.sem, 1)
                    dve.wait_ge(dve1.sem, dve1.at(b, steps[0]))

                dve.wait_ge(x_loaded.sem, x_loaded.at(b, 32))
                dve.wait_ge(conv_done.sem, conv_done.at(b, 0))
                link(dve.tensor_scalar(gsum[:], xin[:, :, 0], GRAY[0], None, ALU.mult))
                link(dve.scalar_tensor_tensor(out=gsum[:], in0=xin[:, :, 1], scalar=GRAY[1], in1=gsum[:],
                                                   op0=ALU.mult, op1=ALU.add))
                dve.scalar_tensor_tensor(out=gray[:, :, 1:IMG + 1], in0=xin[:, :, 2], scalar=GRAY[2], in1=gsum[:],
                                         op0=ALU.mult, op1=ALU.add).then_inc(gray_ready.sem, 1)
                dve.wait_ge(uT_ready.sem, uT_ready.at(b, 1))
                dve.wait_ge(text_done.sem, text_done.at(b, 0))
                dve.tensor_scalar(usT[:], ps[0:R, 7, 0:P], s_col[:], None, ALU.mult).then_inc(usT_ready.sem, 1)
                dve.wait_ge(abs_done.sem, abs_done.at(b, 2))
                dve.wait_ge(hbo_ready.sem, hbo_ready.at(b, 0))
                dve.tensor_tensor(h[:, 0:2], edges[:, :, 0:IMG], edges[:, :, IMG:2 * IMG], ALU.add)
                dve.wait_ge(text_done.sem, text_done.at(b, 1))
                dve.tensor_copy(h[:, 2], ps[:, 7, D:2 * D]).then_inc(h_ready.sem, 1)
                dve.wait_ge(h_ready.sem, h_ready.at(b, 1))
                for i in range(NT):
                    ins = dve.bn_stats(stats[:, i], h[:, i])
                link(ins)
                dve.memset(spare[:], 0.0)
                for i in range(NT):
                    ins = dve.bn_aggr(mv[:, i], stats[:, i])
                ins.then_inc(var_ready.sem, 1)
                dve.wait_ge(std_ready.sem, std_ready.at(b, 1))
                link(dve.reciprocal(rstd[:], std[:]))
                dve.wait_ge(xT_turned.sem, xT_turned.at(b, 0))
                for i in range(NT):
                    ins = dve.tensor_scalar(xn[:, i], h[:, i], mv[:, i, 0:1], rstd[:, i:i + 1],
                                            ALU.subtract, ALU.mult)
                ins.then_inc(xn_ready.sem, 1)
                dve.wait_ge(proj_done.sem, proj_done.at(b, 2))
                dve.wait_ge(scores_done.sem, scores_done.at(b, 0))
                for m in range(KB):
                    for j in range(2):
                        ins = dve.tensor_scalar(km[:, m, j], ps[:, 2 + m, 0:T], bk[:, m:m + 1], parity[:, j:j + 1],
                                                ALU.add, ALU.mult)
                ins.then_inc(k_ready.sem, 1)
                dve.wait_ge(proj_done.sem, proj_done.at(b, 3))
                dve.wait_ge(pv_done.sem, pv_done.at(b, 0))
                for i in range(NT):
                    src = ps[:, 6, i * D:(i + 1) * D] if i < 2 else ps[:, 7, 0:D]
                    ins = dve.tensor_tensor(vaug[:, i, :, 0:DK], src.rearrange("p (h d) -> p h d", h=NH),
                                            bv_row[:].rearrange("p (h d) -> p h d", h=NH), ALU.add)
                ins.then_inc(v_ready.sem, 1)
                dve.wait_ge(sumv_done.sem, sumv_done.at(b, 1))
                link(dve.tensor_copy(sumv[:], ps[:, 7, D:2 * D]))
                for s in range(NU + 5):
                    if s < NU:
                        w = slice(0 if s >= HG else P, 2 * P)
                        bank = 2 * (s % 2)
                        sc = ps[:, bank:bank + 2, :].rearrange("p a (h k) -> p (a h) k", h=2)[:, :, w]
                        n = 2 * P - w.start
                        dve.wait_ge(scores_done.sem, scores_done.at(b, s + 1))
                        link(dve.tensor_reduce(mx[:, s % 2], sc, AX_X, ALU.max))
                        dve.wait_ge(turned.sem, turned.at(b, max(s - 1, 0)))
                        dve.tensor_tensor(prob[:, s % 2, :, w], sc, mx[:, s % 2].unsqueeze(2).to_broadcast([P, HG, n]),
                                          ALU.subtract).then_inc(sub_done.sem, 1)
                    if s >= 5 and (s - 5) % 4 == 0 and (s - 5) // 4 < NT:
                        i = (s - 5) // 4
                        pv = ps[:, 6, 0:NH * (DK + 1)].rearrange("p (h d) -> p h d", h=NH)
                        dve.wait_ge(pv_done.sem, pv_done.at(b, HG * (i + 1)))
                        link(dve.reciprocal(rden[:], pv[:, :, DK]))
                        dve.wait_ge(cx_turned.sem, cx_turned.at(b, i))
                        dve.tensor_tensor(cx[:].rearrange("p (h d) -> p h d", h=NH), pv[:, :, 0:DK],
                                          rden[:].unsqueeze(2).to_broadcast([P, NH, DK]),
                                          ALU.mult).then_inc(pv_read.sem, 1)
                        dve.wait_ge(pv_read.sem, pv_read.at(b, i + 1))
                        dve.tensor_tensor(cx[:], cx[:], sumv[:], ALU.add).then_inc(cx_ready.sem, 1)
                    if s >= 8 and (s - 8) % 4 == 0:
                        i = (s - 8) // 4
                        dve.wait_ge(wo_done.sem, wo_done.at(b, i + 1))
                        dve.wait_ge(hbo_ready.sem, hbo_ready.at(b, 1))
                        dve.tensor_tensor(h_all[:, bass.ds(b, 1), i, :].rearrange("p o d -> p (o d)"),
                                          hbo[:, i], ps[:, 7, D:2 * D],
                                          ALU.add).then_inc(h1_ready.sem, 1)
                assert steps[0] == dve1.per, steps

            dve.wait_ge(h1_ready.sem, h1_ready.at(NB - 1, NT))
            with dve.Fori(0, NB) as b:
                steps = [0]

                def link(ins):
                    steps[0] += 1
                    ins.then_inc(dve2.sem, 1)
                    dve.wait_ge(dve2.sem, dve2.at(b, steps[0]))


                def norm(n):
                    for i in range(NT):
                        ins = dve.bn_stats(stats[:, i], h[:, i])
                    link(ins)
                    dve.memset(spare[:], 0.0)
                    for i in range(NT):
                        ins = dve.bn_aggr(mv[:, i], stats[:, i])
                    ins.then_inc(var2_ready.sem, 1)
                    dve.wait_ge(std2_ready.sem, std2_ready.at(b, n + 1))
                    link(dve.reciprocal(rstd[:], std[:]))
                    dve.wait_ge(x2_turned.sem, x2_turned.at(b, n))
                    for i in range(NT):
                        ins = dve.tensor_scalar(xn[:, i], h[:, i], mv[:, i, 0:1], rstd[:, i:i + 1],
                                                ALU.subtract, ALU.mult)
                    ins.then_inc(xn2_ready.sem, 1)

                link(dve.tensor_copy(h[:], h_all[:, bass.ds(b, 1)].rearrange("p o i d -> p (o i) d")))
                norm(0)
                dve.wait_ge(block_ready.sem, block_ready.at(b, 1))
                for i in range(NT):
                    ins = dve.scalar_tensor_tensor(out=junk[:, i, 0:P], in0=srow[:, i * P:(i + 1) * P], scalar=1.0,
                                                   in1=ident[:], op0=ALU.mult, op1=ALU.mult, accum_out=own[:, i:i + 1])
                link(ins)
                for i in range(NT):
                    dve.scalar_tensor_tensor(out=junk[:, i], in0=srow[:], scalar=own[:, i:i + 1], in1=before[:, i],
                                             op0=ALU.is_ge, op1=ALU.mult, accum_out=count[:, 0, i:i + 1])
                    ins = dve.scalar_tensor_tensor(out=junk[:, NT + i], in0=srow[:], scalar=own[:, i:i + 1], in1=after[:, i],
                                                   op0=ALU.is_gt, op1=ALU.mult, accum_out=count[:, 1, i:i + 1])
                link(ins)
                link(dve.tensor_tensor(sel[:], count[:, 0], count[:, 1], ALU.add))
                dve.tensor_scalar(sel[:], sel[:], KEEP - 0.5, None, ALU.is_lt)
                link(dve.tensor_tensor(g[:], g[:], xn[:], ALU.subtract))
                for i in range(NT):
                    ins = dve.scalar_tensor_tensor(out=g[:, i], in0=g[:, i], scalar=sel[:, i:i + 1], in1=xn[:, i],
                                                   op0=ALU.mult, op1=ALU.add)
                link(ins)
                link(dve.tensor_tensor(h[:], h[:], g[:], ALU.add))
                norm(1)
                dve.wait_ge(u_done.sem, u_done.at(b, 1))
                dve.tensor_tensor(rot[:, 0], ps[:, 3, 0:T], turn[:, 0], ALU.mult)
                dve.tensor_tensor(rot[:, 1], ps[:, 4, 0:T], turn[:, 1], ALU.mult)
                dve.tensor_tensor(rot[:, 2], ps[:, 4, 0:T], turn[:, 0], ALU.mult)
                dve.tensor_tensor(rot[:, 3], ps[:, 3, 0:T], turn[:, 1], ALU.mult).then_inc(u_read.sem, 1)
                dve.wait_ge(u_read.sem, u_read.at(b, 1))
                dve.tensor_tensor(pre[:, 0], rot[:, 0], rot[:, 1], ALU.add)
                link(dve.tensor_tensor(pre[:, 1], rot[:, 2], rot[:, 3], ALU.subtract))
                dve.wait_ge(state_im.sem, state_im.at(b, 0))
                dve.tensor_tensor_scan(cum[:, 0], ones_t[:], pre[:, 0], 0.0, ALU.mult, ALU.add)
                dve.tensor_tensor_scan(cum[:, 1], ones_t[:], pre[:, 1], 0.0, ALU.mult, ALU.add).then_inc(cum_ready.sem, 1)
                dve.wait_ge(cum_ready.sem, cum_ready.at(b, 1))
                dve.tensor_tensor(rot2[:, 0], cum[:, 0], turn[:, 0], ALU.mult)
                link(dve.tensor_tensor(rot2[:, 1], cum[:, 1], turn[:, 1], ALU.mult))
                dve.wait_ge(ssm_done.sem, ssm_done.at(b, 0))
                dve.tensor_tensor(st[:, 0], rot2[:, 0], rot2[:, 1], ALU.subtract).then_inc(state_re.sem, 1)
                dve.wait_ge(ssm_done.sem, ssm_done.at(b, 1))
                dve.tensor_tensor(h[:].rearrange("p i d -> p (i d)"), h[:].rearrange("p i d -> p (i d)"),
                                  ps[:, 1:3, :].rearrange("p a c -> p (a c)")[:, 0:NT * D], ALU.add
                                  ).then_inc(h3_ready.sem, 1)
                dve.wait_ge(h3_ready.sem, h3_ready.at(b, 1))
                norm(2)
                dve.wait_ge(logit_done.sem, logit_done.at(b, 1))
                for i in range(NT):
                    ins = dve.tensor_tensor(logit[:, i], ps[:, 5, i * NE:(i + 1) * NE], rb_row[:], ALU.add)
                ins.then_inc(logit_read.sem, 1)
                dve.wait_ge(logit_read.sem, logit_read.at(b, 1))
                dve.memset(spare[:], 0.0)
                for i in range(NT):
                    ins = dve.max(v8[:, i], logit[:, i])
                link(ins)
                dve.memset(spare[:], 0.0)
                for i in range(NT):
                    ins = dve.max_index(i8[:, i], v8[:, i], logit[:, i])
                link(ins)
                dve.tensor_copy(top_v[:, bass.ds(b, 1)].rearrange("p o i k -> p (o i) k"), v8[:, :, 0:2])
                dve.tensor_copy(top_i[:, bass.ds(b, 1)].rearrange("p o i k -> p (o i) k"), i8[:, :, 0:2])
                dve.wait_ge(xn_stored.sem, xn_stored.at(b, 16))
                dve.wait_ge(hb2_ready.sem, hb2_ready.at(b, 1))
                dve.wait_ge(down_done.sem, down_done.at(b, 1))
                dve.tensor_tensor(h_all[:, bass.ds(b, 1)].rearrange("p o i d -> p (o i d)"),
                                  hbo[:].rearrange("p i d -> p (i d)"),
                                  ps[:, 1:3, :].rearrange("p a c -> p (a c)")[:, 0:NT * D], ALU.add
                                  ).then_inc(h4_ready.sem, 1)
                assert steps[0] == dve2.per, steps

            dve.wait_ge(route_loaded.sem, route_loaded.at(0, 48))
            steps = [0]

            def link(ins):
                steps[0] += 1
                ins.then_inc(route_step.sem, 1)
                dve.wait_ge(route_step.sem, route_step.at(0, steps[0]))

            v = top_v[:].rearrange("p b i k -> p (b i) k")
            ix = top_i[:].rearrange("p b i k -> p (b i) k")
            dve.tensor_tensor(gates[:, 0], v[:, :, 1], v[:, :, 0], ALU.subtract).then_inc(diff_ready.sem, 1)
            for k in range(2):
                for e in range(NE):
                    ins = dve.tensor_scalar(hot[:, k, e], ix[:, :, k], float(e), None, ALU.is_equal)
            dve.memset(ones1[:], 1.0)
            link(dve.memset(seg[:], 1.0))
            dve.memset(seg[:, :, 0:1], 0.0)
            dve.tensor_tensor(hot2[:], hot[:, 0], hot[:, 1], ALU.add).then_inc(hot_ready.sem, 1)
            dve.wait_ge(ratio_ready.sem, ratio_ready.at(0, 1))
            link(dve.tensor_scalar(gates[:, 0], gates[:, 1], 1.0, None, ALU.add))
            link(dve.reciprocal(gates[:, 2], gates[:, 0]))
            dve.tensor_tensor(gates[:, 3], gates[:, 1], gates[:, 2], ALU.mult)
            dve.wait_ge(rank_done.sem, rank_done.at(0, 1))
            link(dve.tensor_copy(tot[:], ps[:, 1, 0:NE * TILES].rearrange("p (e t) -> p e t", e=NE)))
            flat = "p e t -> p (e t)"
            link(dve.tensor_tensor_scan(incl[:].rearrange(flat), seg[:].rearrange(flat), tot[:].rearrange(flat),
                                             0.0, ALU.mult, ALU.add))
            link(dve.tensor_tensor(over[:], incl[:, :, TILES - 1:TILES].to_broadcast([P, NE, RAMP]),
                                        ramp[:].unsqueeze(1).to_broadcast([P, NE, RAMP]), ALU.is_gt))
            link(dve.tensor_reduce(chunks[:, 0], over[:], AX_X, ALU.add))
            link(dve.tensor_scalar(chunks[:, 0], chunks[:, 0], 1.0, None, ALU.max))
            link(dve.tensor_tensor_scan(chunks[:, 1], ones1[:, 0:NE], chunks[:, 0], 0.0, ALU.mult, ALU.add))
            link(dve.tensor_tensor(chunks[:, 2], chunks[:, 1], chunks[:, 0], ALU.subtract))
            dve.memset(bounds[:, 0:1], 0)
            dve.tensor_copy(bounds[:, 1:NE + 1], chunks[:, 1]).then_inc(bounds_ready.sem, 1)
            link(dve.tensor_tensor(incl[:], incl[:], tot[:], ALU.subtract))
            link(dve.tensor_tensor(pos[:], incl[:], ps[:, 0, 0:NE * TILES].rearrange("p (e t) -> p e t", e=NE),
                                        ALU.add))
            for e in range(NE):
                ins = dve.scalar_tensor_tensor(out=tot[:, e], in0=chunks[:, 2, e:e + 1].to_broadcast([P, TILES]),
                                             scalar=float(CHUNK), in1=pos[:, e], op0=ALU.mult, op1=ALU.add)
            link(ins)
            for k in range(2):
                ins = dve.tensor_tensor(picked[:, k], hot[:, k], tot[:], ALU.mult)
            link(ins)
            for k in range(2):
                ins = dve.tensor_reduce(pos_f[:, k], picked[:, k].rearrange("p e t -> p t e"), AX_X, ALU.add)
            link(ins)
            dve.tensor_copy(pos_i[:], pos_f[:]).then_inc(pos_ready.sem, 1)
            dve.wait_ge(slots_turned.sem, slots_turned.at(0, 1))
            dve.tensor_copy(slots_i[:], ps[:, 7, 0:SLOT_TILES]).then_inc(slots_ready.sem, 1)
            dve.wait_ge(bounds_ready.sem, bounds_ready.at(0, 1))

            def turn_chunk(j):
                dve.wait_ge(xg_turned.sem, xg_turned.at(j, 1))
                dve.tensor_copy(xgT[:], ps[:, 6, :].rearrange("p (k n) -> p k n", k=KB)).then_inc(xgT_ready.sem, 1)

            def outputs(q, half, e):
                lo, hi = expert_bounds(dve, e)
                with dve.Fori(lo, hi) as j:
                    dve.wait_ge(w_loaded[half].sem, w_loaded[half].at(q, 64))
                    dve.wait_ge(eup_done.sem, eup_done.at(j, FB))
                    turn_chunk(j + 1)
                    dve.wait_ge(y_sent.sem, y_sent.at(j, 0))
                    for k in range(2):
                        dve.wait_ge(edown_done.sem, edown_done.at(j, k + 1))
                        dve.tensor_tensor(yb[:, k], ps[:, 4 + k, 0:D], b2_row[half][:], ALU.add
                                          ).then_inc(y_ready.sem, 1)

            turn_chunk(0)
            with dve.Fori(0, NE // 2) as q:
                for half in range(2):
                    outputs(q, half, 2 * q + half)
            flat_h = h_all[:].rearrange("p b i d -> p (b i) d")
            with dve.Fori(0, TILES // COMB) as c:
                dve.wait_ge(yg_loaded.sem, yg_loaded.at(c, yg_loaded.per))
                for i in range(COMB):
                    ins = dve.scalar_tensor_tensor(out=part[:, i], in0=yg[:, 0, i],
                                                   scalar=gates[:, 2, bass.ds(c * COMB + i, 1)],
                                                   in1=flat_h[:, bass.ds(c * COMB + i, 1)].rearrange("p o d -> p (o d)"),
                                                   op0=ALU.mult, op1=ALU.add)
                ins.then_inc(part_ready.sem, 1)
                dve.wait_ge(part_ready.sem, part_ready.at(c, 1))
                dve.wait_ge(res_sent.sem, res_sent.at(c, 0))
                for i in range(COMB):
                    ins = dve.scalar_tensor_tensor(out=res[:, i], in0=yg[:, 1, i],
                                                   scalar=gates[:, 3, bass.ds(c * COMB + i, 1)], in1=part[:, i],
                                                   op0=ALU.mult, op1=ALU.add)
                ins.then_inc(res_ready.sem, 1)
                dve.wait_ge(res_ready.sem, res_ready.at(c, 1))
                dve.memset(spare[:], 0.0).then_inc(yg_read.sem, 1)

        @block.tensor
        def _(pe):
            pe.wait_ge(loaded.sem, loaded.at(0, NLOAD))
            pe.wait_ge(set_up.sem, set_up.at(0, NSET))
            for k in range(KB):
                for j in range(KB):
                    pe.matmul(ps[:, k, 0:D], b_w[:, j, k * P:(k + 1) * P], dft[:, j], start=(j == 0), stop=(j == KB - 1))
                for j in range(KB):
                    pe.matmul(ps[:, 2 + k, 0:D], idft[:, j, k * P:(k + 1) * P], c_wT[:, j],
                              start=(j == 0), stop=(j == KB - 1))
            pe.matmul(ps[:, 4, 0:1], sines[:], a_col[:], start=True, stop=True).then_inc(mats_done.sem, 1)
            pe.wait_ge(mats_read.sem, mats_read.at(0, 1))
            with pe.Fori(0, NB) as b:
                pe.wait_ge(ub_ready.sem, ub_ready.at(b, 1))
                pe.wait_ge(h1_ready.sem, h1_ready.at(b, 0))
                pe.transpose(ps[:, 7, 0:P], ub[:], ident[:]).then_inc(uT_ready.sem, 1)
                pe.wait_ge(gray_ready.sem, gray_ready.at(b, 1))
                pe.wait_ge(halo_loaded.sem, halo_loaded.at(b, 96))
                pe.wait_ge(sub_done.sem, sub_done.at(b, 0))
                for i in range(2):
                    for o in range(2):
                        dst = ps[:, i, o * IMG:(o + 1) * IMG]
                        for dx in range(3):
                            pe.matmul(dst, band[:, o, dx], gray[:, i, dx:dx + IMG], start=(dx == 0), stop=False)
                        ins = pe.matmul(dst, band_edge[:, o, i], halo[:, i], start=False, stop=True)
                    ins.then_inc(conv_done.sem, 1)
                pe.wait_ge(usT_ready.sem, usT_ready.at(b, 1))
                pe.matmul(ps[:, 7, D:2 * D], usT[:], vt[:], start=True, stop=True).then_inc(text_done.sem, 1)
                pe.wait_ge(xn_ready.sem, xn_ready.at(b, 1))
                pe.wait_ge(pT_ready.sem, pT_ready.at(b, 0))
                for k in range(KB):
                    for i in range(NT):
                        ins = pe.transpose(ps[:, 4 + k, i * P:(i + 1) * P], xn[:, i, k * P:(k + 1) * P], ident[:])
                ins.then_inc(xT_turned.sem, 1)
                pe.wait_ge(xT_ready.sem, xT_ready.at(b, 1))
                pe.wait_ge(abs_done.sem, abs_done.at(b, 2))
                for w, first in ((wq, 0), (wk, 2)):
                    for m in range(KB):
                        for k in range(KB):
                            ins = pe.matmul(ps[:, first + m, 0:T], w[:, k, m * P:(m + 1) * P], xT[:, k],
                                            start=(k == 0), stop=(k == KB - 1))
                    ins.then_inc(proj_done.sem, 1)
                pe.wait_ge(pv_read.sem, pv_read.at(b, 0))
                for i in range(NT):
                    dst = ps[:, 6, i * D:(i + 1) * D] if i < 2 else ps[:, 7, 0:D]
                    for k in range(KB):
                        ins = pe.matmul(dst, xT[:, k, i * P:(i + 1) * P], wv[:, k], start=(k == 0), stop=(k == KB - 1))
                ins.then_inc(proj_done.sem, 1)
                pe.wait_ge(v_ready.sem, v_ready.at(b, 1))
                for i in range(NT):
                    ins = pe.matmul(ps[:, 7, D:2 * D].rearrange("p (h d) -> p h d", h=NH), ones9[:], vaug[:, i, :, 0:DK],
                                    start=(i == 0), stop=(i == NT - 1))
                ins.then_inc(sumv_done.sem, 1)
                for s in range(NU + 4):
                    if s < NU:
                        i, g = s // HG, s % HG
                        c0 = 0 if i else P
                        n = 2 * P - c0
                        keys = slice((i - 1) * P + c0, (i + 1) * P)
                        if s == 0:
                            pe.wait_ge(q_ready.sem, q_ready.at(b, 1))
                            pe.wait_ge(k_ready.sem, k_ready.at(b, 1))
                        pe.wait_ge(sub_done.sem, sub_done.at(b, max(s - 1, 0)))
                        m = g // 2
                        for j in range(2):
                            r = 32 * (2 * (g % 2) + j)
                            dst = ps[:, 2 * (s % 2) + j, :].rearrange("p (h k) -> p h k", h=2)[:, :, c0:2 * P]
                            pe.matmul(dst, qT[r:r + 32, m, i * P:(i + 1) * P], km[r:r + 32, m, :, keys],
                                      start=True, stop=False)
                        for j in range(2):
                            dst = ps[:, 2 * (s % 2) + j, :].rearrange("p (h k) -> p h k", h=2)[:, :, c0:2 * P]
                            ins = pe.matmul(dst, ident_bf[:], mask_bf[:, :, c0:2 * P], start=False, stop=True)
                        ins.then_inc(scores_done.sem, 1)
                    if 1 <= s <= NU:
                        u = s - 1
                        pe.wait_ge(exp_done.sem, exp_done.at(b, u + 1))
                        pe.wait_ge(pT_ready.sem, pT_ready.at(b, u))
                        for hh in range(HG):
                            for k in range(0 if u >= HG else 1, 2):
                                ins = pe.transpose(ps[:, 4 + hh // 2, ((hh % 2) * 2 + k) * P:((hh % 2) * 2 + k + 1) * P],
                                                   prob[:, u % 2, hh, k * P:(k + 1) * P], ident[:])
                        ins.then_inc(turned.sem, 1)
                    if 2 <= s <= NU + 1:
                        u = s - 2
                        i, g = u // HG, u % HG
                        if g == 0:
                            pe.wait_ge(pv_read.sem, pv_read.at(b, i))
                        pe.wait_ge(pT_ready.sem, pT_ready.at(b, u + 1))
                        for hh in range(HG):
                            hd = g * HG + hh
                            for k in range(0 if i else 1, 2):
                                ins = pe.matmul(ps[:, 6, hd * (DK + 1):(hd + 1) * (DK + 1)], pT[:, u % 2, hh, k],
                                                vaug[:, i - 1 + k, hd, :], start=(k == (0 if i else 1)), stop=(k == 1))
                        ins.then_inc(pv_done.sem, 1)
                    if s >= 6 and (s - 6) % 4 == 0 and (s - 6) // 4 < NT:
                        i = (s - 6) // 4
                        pe.wait_ge(cx_ready.sem, cx_ready.at(b, i + 1))
                        pe.wait_ge(h1_ready.sem, h1_ready.at(b, i))
                        for k in range(KB):
                            ins = pe.transpose(ps[:, 7, k * P:(k + 1) * P], cx[:, k * P:(k + 1) * P], ident[:])
                        ins.then_inc(cx_turned.sem, 1)
                    if s >= 7 and (s - 7) % 4 == 0 and (s - 7) // 4 < NT:
                        i = (s - 7) // 4
                        pe.wait_ge(cxT_ready.sem, cxT_ready.at(b, i + 1))
                        for k in range(KB):
                            ins = pe.matmul(ps[:, 7, D:2 * D], cxT[:, k], wo[:, k], start=(k == 0), stop=(k == KB - 1))
                        ins.then_inc(wo_done.sem, 1)
            pe.wait_ge(h1_ready.sem, h1_ready.at(NB - 1, NT))
            with pe.Fori(0, NB) as b:
                def turn_rows(n):
                    pe.wait_ge(xn2_ready.sem, xn2_ready.at(b, n + 1))
                    pe.wait_ge(x2_ready.sem, x2_ready.at(b, n))
                    for k in range(KB):
                        for i in range(NT):
                            ins = pe.transpose(ps[:, 6 + k, i * P:(i + 1) * P], xn[:, i, k * P:(k + 1) * P], ident[:])
                    ins.then_inc(x2_turned.sem, 1)
                    pe.wait_ge(x2_ready.sem, x2_ready.at(b, n + 1))

                def tile_out(i):
                    return ps[:, 1, i * D:(i + 1) * D] if i < 2 else ps[:, 2, 0:D]

                turn_rows(0)
                pe.wait_ge(block_ready.sem, block_ready.at(b, 0))
                pe.wait_ge(h4_ready.sem, h4_ready.at(b, 0))
                for k in range(KB):
                    pe.matmul(ps[:, 0, 0:T], wr_bc[:, k], xT[:, k], start=(k == 0), stop=(k == KB - 1))
                for i in range(NT):
                    for k in range(KB):
                        ins = pe.matmul(tile_out(i), xT[:, k, i * P:(i + 1) * P], wb[:, k],
                                        start=(k == 0), stop=(k == KB - 1))
                ins.then_inc(block_done.sem, 1)
                turn_rows(1)
                pe.wait_ge(hid_ready.sem, hid_ready.at(b, 0))
                for m in range(2):
                    for k in range(KB):
                        ins = pe.matmul(ps[:, 3 + m, 0:T], fb[:, k, m * P:(m + 1) * P], xT[:, k],
                                        start=(k == 0), stop=(k == KB - 1))
                ins.then_inc(u_done.sem, 1)
                pe.wait_ge(state_re.sem, state_re.at(b, 1))
                pe.wait_ge(state_im.sem, state_im.at(b, 1))
                pe.wait_ge(block_ready.sem, block_ready.at(b, 1))
                for i in range(NT):
                    pe.matmul(tile_out(i), st[:, 0, i * P:(i + 1) * P], ce[:, 0], start=True, stop=False)
                    for k in range(KB):
                        pe.matmul(tile_out(i)[:, k * P:(k + 1) * P], xT[:, k, i * P:(i + 1) * P], d_diag[:, k],
                                  start=False, stop=False)
                    ins = pe.matmul(tile_out(i), st[:, 1, i * P:(i + 1) * P], ce[:, 1], start=False, stop=True)
                ins.then_inc(ssm_done.sem, 1)
                turn_rows(2)
                pe.wait_ge(logit_read.sem, logit_read.at(b, 0))
                for i in range(NT):
                    for k in range(KB):
                        ins = pe.matmul(ps[:, 5, i * NE:(i + 1) * NE], xT[:, k, i * P:(i + 1) * P], rw[:, k],
                                        start=(k == 0), stop=(k == KB - 1))
                ins.then_inc(logit_done.sem, 1)
                pe.wait_ge(u_read.sem, u_read.at(b, 1))
                for f in range(FB):
                    pe.wait_ge(hid_ready.sem, hid_ready.at(b, max(f - 1, 0)))
                    for k in range(KB):
                        ins = pe.matmul(ps[:, 3 + f % 2, 0:T], sw1[:, k, f * P:(f + 1) * P], xT[:, k],
                                        start=(k == 0), stop=(k == KB - 1))
                    ins.then_inc(up_done.sem, 1)
                pe.wait_ge(hid_ready.sem, hid_ready.at(b, FB))
                pe.wait_ge(h3_ready.sem, h3_ready.at(b, 1))
                for i in range(NT):
                    for f in range(FB):
                        ins = pe.matmul(tile_out(i), hid[:, f, i * P:(i + 1) * P], sw2[:, f],
                                        start=(f == 0), stop=(f == FB - 1))
                ins.then_inc(down_done.sem, 1)

            pe.wait_ge(route_loaded.sem, route_loaded.at(0, 48))
            pe.wait_ge(hot_ready.sem, hot_ready.at(0, 1))
            pe.matmul(ps[:, 0, 0:NE * TILES], ltri[:], hot2[:].rearrange("p e t -> p (e t)"), start=True, stop=True)
            pe.matmul(ps[:, 1, 0:NE * TILES], ones1[:], hot2[:].rearrange("p e t -> p (e t)"),
                      start=True, stop=True).then_inc(rank_done.sem, 1)
            pe.wait_ge(slots_loaded.sem, slots_loaded.at(0, 16))
            pe.transpose(ps[:, 7, 0:SLOT_TILES], slots_r[:], ident[0:SLOT_TILES, 0:SLOT_TILES]
                         ).then_inc(slots_turned.sem, 1)
            pe.wait_ge(pos_ready.sem, pos_ready.at(0, 1))

            def turn_chunk(j):
                pe.wait_ge(xg_loaded.sem, xg_loaded.at(j, 32))
                for k in range(KB):
                    for c in range(2):
                        ins = pe.transpose(ps[:, 6, (2 * k + c) * P:(2 * k + c + 1) * P],
                                           xg[:, c, k * P:(k + 1) * P], ident[:])
                ins.then_inc(xg_turned.sem, 1)

            def expert(q, half, e):
                lo, hi = expert_bounds(pe, e)
                with pe.Fori(lo, hi) as j:
                    pe.wait_ge(w_loaded[half].sem, w_loaded[half].at(q, 64))
                    pe.wait_ge(xgT_ready.sem, xgT_ready.at(j, 1))
                    for f in range(FB):
                        pe.wait_ge(ehid_ready.sem, ehid_ready.at(j, max(f - 3, 0)))
                        for k in range(KB):
                            ins = pe.matmul(ps[:, f % 4, 0:CHUNK], w1[half][:, k, f * P:(f + 1) * P], xgT[:, k],
                                            start=(k == 0), stop=(k == KB - 1))
                        ins.then_inc(eup_done.sem, 1)
                    turn_chunk(j + 1)
                    pe.wait_ge(y_ready.sem, y_ready.at(j, 0))
                    for c in range(2):
                        for f in range(FB):
                            if c == 0:
                                pe.wait_ge(ehid_ready.sem, ehid_ready.at(j, f + 1))
                            ins = pe.matmul(ps[:, 4 + c, 0:D], hidg[:, f, c * P:(c + 1) * P], w2[half][:, f],
                                            start=(f == 0), stop=(f == FB - 1))
                        ins.then_inc(edown_done.sem, 1)

            turn_chunk(0)
            with pe.Fori(0, NE // 2) as q:
                for half in range(2):
                    expert(q, half, 2 * q + half)



def layout(inputs):
    def blocks(w):
        w = np.asarray(w)
        return np.ascontiguousarray(w.reshape(w.shape[0] // P, P, -1).transpose(1, 0, 2))

    def col(v):
        return np.ascontiguousarray(np.asarray(v).reshape(-1, P).T)

    g = {k: np.asarray(v) for k, v in inputs.items()}
    a = {
        "x": g["x"], "ids": g["x_txt"].T, "U": g["L0_txt_U"], "s": g["L0_txt_s"].reshape(R, 1), "vt": g["L0_txt_Vt"],
        "scharr": g["L0_tok_scharr"].reshape(18), "scharr_dx": g["L0_tok_scharr"][:, 0].transpose(2, 0, 1),
        "wqT": blocks(g["L0_attn_Wq"].T), "wkT": blocks(g["L0_attn_Wk"].T), "wvT": blocks(g["L0_attn_Wv"].T),
        "woT": blocks(g["L0_attn_Wo"].T), "bq": col(g["L0_attn_bq"]), "bk": col(g["L0_attn_bk"]),
        "bv": g["L0_attn_bv"], "bo": g["L0_attn_bo"],
    }
    a |= {
        "wr": col(g["L0_ffn_w_router"]), "wb": blocks(g["L0_ffn_w_block"]), "a": g["L1_attn_a_params"].reshape(P, 1),
        "b_w": blocks(g["L1_attn_B_w"]), "c_wT": blocks(g["L1_attn_C_w"].T), "d": g["L1_attn_D"],
        "rwT": blocks(g["L1_ffn_router_w"].T), "rb": g["L1_ffn_router_b"],
        "sw1": blocks(g["L1_ffn_shared_w1"].T), "sw2": blocks(g["L1_ffn_shared_w2"].T),
        "sb1": col(g["L1_ffn_shared_b1"]), "sb2": g["L1_ffn_shared_b2"],
    }
    a |= {
        "w1": np.stack([blocks(w.T) for w in g["L1_ffn_spec_w1"]]), "w2": np.stack([blocks(w.T) for w in g["L1_ffn_spec_w2"]]),
        "b1": np.stack([col(v) for v in g["L1_ffn_spec_b1"]]), "b2": g["L1_ffn_spec_b2"],
    }
    r = np.arange(P)
    c = np.arange(2 * P)
    a["ident"] = np.eye(P, dtype=np.float32)
    a["mask"] = np.where((c[None] <= r[:, None] + P) & (c[None] >= r[:, None]), 0, MASKED).astype(np.float32)
    a["shift"] = np.stack([r[:, None] - r[None] == dy - 1 for dy in range(3)], 1).astype(np.float32)
    a["parity"] = np.stack([(r // DK) % 2 == j for j in range(2)], 1).astype(np.float32)
    a["ltri"] = (r[:, None] < r[None]).astype(np.float32)
    a["ramp"] = (np.arange(RAMP) * CHUNK).astype(np.float32)
    a["tok"] = (np.arange(TILES)[None] * P + r[:, None]).astype(np.float32)
    j = np.arange(T)
    own = np.arange(NT)[:, None] * P + r[:, None, None]
    a["before"] = (j[None, None] < own).astype(np.float32)
    n = np.arange(D)
    angle = 2 * np.pi * np.outer(n, r) / D
    re, im = np.cos(angle), -np.sin(angle)
    im[:, 0] = (-1.0) ** n
    a["dft"] = blocks(np.concatenate([re, im], 1).astype(np.float32))
    scale = np.where(r == 0, 1.0, 2.0) / D
    a["idft"] = blocks(np.concatenate([re * scale, im * scale], 1).astype(np.float32))
    sines = -2 * np.sin(2 * np.pi * np.outer(r + 1, r) / D)
    sines[P - 1] = 0
    sines[:, 0] = 0
    a["sines"] = sines.astype(np.float32)
    return {k: np.ascontiguousarray(v) for k, v in a.items()}


def kernel(**inputs):
    import concourse.bacc as bacc
    from concourse.bass_utils import run_bass_kernel_spmd

    arrays = layout(inputs)
    nc = bacc.Bacc("TRN2", target_bir_lowering=False, num_devices=1)
    t = {k: nc.dram_tensor("in_" + k, v.shape, mybir.dt.from_np(v.dtype), kind="ExternalInput").ap()
         for k, v in arrays.items()}
    t["out"] = nc.dram_tensor("result", (NB, T, D), F32, kind="ExternalOutput").ap().rearrange("b t d -> (b t) d")
    build(nc, t)
    return run_bass_kernel_spmd(nc, [{"in_" + k: v for k, v in arrays.items()}], core_ids=[0]).results[0]["result"]
```

```python
from contextlib import ExitStack

import numpy as np
import concourse.bass as bass
from concourse import mybir

F32 = mybir.dt.float32
F32R = mybir.dt.float32r
BF16 = mybir.dt.bfloat16
I32 = mybir.dt.int32
U32 = mybir.dt.uint32
ALU = mybir.AluOpType
ACT = mybir.ActivationFunctionType
AX_X = mybir.AxisListType.X

P = 128
NB = 16
IMG = 256
D = 256
KB = D // P
NT = 3
T = NT * P
R = 64
NH, DK = 16, 16
SCALE = 0.25
MASKED = -30000.0
GRAY = (0.2989, 0.587, 0.114)
KEEP = 288
F = 1024
FB = F // P
NE = 8
EPS = 1e-5
TILES = NB * NT
CHUNK = 2 * P
CHUNKS = NB * T * 2 // CHUNK + NE
SLOT_TILES = 2 * (CHUNKS + 2)
RAMP = NB * T // CHUNK
SCAT = 12
COMB = 4
HG = 2
NU = NT * NH // HG


PAIRS = P // (HG * DK)
UPT = NH // HG
PB = 4
TURN, PV = 2, 3
SLOTS = NU + PV + 4
TURN0, BLOCK, RANK = 3, 4, 6
TURN1, STATE, OUT = 14, 16, 21
TURN2, GRAY_AT, CONV, UP = 25, 19, 25, 27
NEWTON = 3
GUESS = 0x5F3759DF - 2 ** 30 - 2 ** 22
LN_STEPS = 1 + 4 * NEWTON
CHAIN_STEPS = 15


class Signal:

    def __init__(self, sem, per, start):
        self.sem, self.per, self.start, self.steps = sem, per, start, 0

    def at(self, b, n):
        return b * self.per + (n + self.start)


def build(nc, t):
    with ExitStack() as ctx:
        def sb(name, shape, dt=F32):
            return ctx.enter_context(nc.sbuf_tensor(name, shape, dt))

        signals = []

        def signal(name, per):
            signals.append(Signal(ctx.enter_context(nc.semaphore(name)), per, 1))
            return signals[-1]

        def dma_signal(name, per):
            return Signal(ctx.enter_context(nc.semaphore(name)), per, 0)

        ps = ctx.enter_context(nc.psum_tensor("ps", [P, 8, 512], F32))

        ident = sb("ident", [P, P])
        ident_bf = sb("ident_bf", [P, P], BF16)
        mask_bf = sb("mask_bf", [P, 2, 2 * P], BF16)
        ones9 = sb("ones9", [P, P])
        tap = sb("tap", [P, 18])
        tap_edge = sb("tap_edge", [3, 2, 3])
        band = sb("band", [P, 2, 3, P])
        band_edge = sb("band_edge", [3, 2, 2, P])
        wq = sb("wq", [P, KB, D])
        wk = sb("wk", [P, KB, D])
        wv = sb("wv", [P, KB, D])
        wo = sb("wo", [P, KB, D])
        bq = sb("bq", [P, KB])
        bk = sb("bk", [P, KB])
        bv_row = sb("bv_row", [P, D])
        bo_row = sb("bo_row", [P, D])
        vt = sb("vt", [R, D])
        s_col = sb("s_col", [R, 1])
        ids = sb("ids", [P, NB], I32)
        u_all = sb("u_all", [P, NB, R])

        spare = sb("spare", [P, 1])
        c15 = sb("c15", [P, NT])
        zeros = sb("zeros", [SLOT_TILES, P])
        wr_col = sb("wr_col", [P, KB])
        wr_bc = sb("wr_bc", [P, KB, P])
        wb = sb("wb", [P, KB, D])
        rank_cols = sb("rank_cols", [P, T])
        rank_own = sb("rank_own", [P, NT])
        before = sb("before", [P, NT, T], BF16)
        after = sb("after", [P, NT, T], BF16)
        sines = sb("sines", [P, P])
        a_col = sb("a_col", [P, 1])
        d_diag = sb("d_diag", [P, KB, P])
        fb = sb("fb", [P, KB, D])
        ce = sb("ce", [P, 2, D])
        turn = sb("turn", [P, 2, T])
        om = sb("om", [P, 8])
        ones_t = sb("ones_t", [P, T])
        rw = sb("rw", [P, KB, NE])
        rb_row = sb("rb_row", [P, NE])
        sw1 = sb("sw1", [P, KB, F])
        sw2 = sb("sw2", [P, FB, D])
        sb1 = sb("sb1", [P, FB])
        sb2_row = sb("sb2_row", [P, D])
        top_v = sb("top_v", [P, NB, NT, 2])
        top_i = sb("top_i", [P, NB, NT, 2])

        space = ctx.enter_context(ExitStack())

        def room(name, shape, dt=F32):
            return space.enter_context(nc.sbuf_tensor(name, shape, dt))

        xin = room("xin", [P, 2, 3, IMG])
        gsum = room("gsum", [P, 2, IMG])
        gray = room("gray", [P, 2, IMG + 2])
        halo = room("halo", [3, 2, IMG])
        edges = room("edges", [P, 2, 2 * IMG])
        ub = room("ub", [P, P])
        usT = room("usT", [R, P])
        h = room("h", [P, NT, D])
        hbo = room("hbo", [P, NT, D])
        ln = room("ln", [P, 48])
        xn = room("xn", [P, NT, D])
        xT = room("xT", [P, KB, T])
        q_full = room("q_full", [P, KB, T])
        q_hi = room("q_hi", [P, KB, T], F32R)
        q_lo = room("q_lo", [P, KB, T], F32R)
        k_hi = room("k_hi", [P, KB, T], F32R)
        k_lo = room("k_lo", [P, KB, T], F32R)
        qs = room("qs", [3 * HG * DK, PAIRS, KB, T], F32R)
        ks = room("ks", [3 * HG * DK, PAIRS, KB, HG, T], F32R)
        vaug = room("vaug", [P, NT, NH, DK + 1])
        sumv = room("sumv", [P, D])
        mx = room("mx", [P, 2, HG])
        prob = room("prob", [P, PB, HG, 2 * P])
        pT = room("pT", [P, 2, HG, 2, P])
        rden = room("rden", [P, NH])
        cx = room("cx", [P, D])
        cxT = room("cxT", [P, KB, P])
        h1 = room("h1", [P, NT, D])
        hc = room("hc", [P, NT, D])
        lnc = room("lnc", [P, 48])
        xc = room("xc", [P, NT, D])
        xcT = room("xcT", [P, KB, T])
        srow = room("srow", [P, T])
        own = room("own", [P, NT])
        count = room("count", [P, 2, NT])
        sel = room("sel", [P, NT])
        g = room("g", [P, NT, D])
        rot = room("rot", [P, 4, T])
        cum = room("cum", [P, 2, T])
        st = room("st", [P, 2, T])
        logit = room("logit", [P, NT, NE])
        v8 = room("v8", [P, NT, NE])
        i8 = room("i8", [P, NT, NE], U32)
        hb2 = room("hb2", [P, NT, D])
        hid = room("hid", [P, FB, T])
        place = hid[:].rearrange("p f t -> p (f t)")
        mats = place[:, 0:4 * KB * D].rearrange("p (n k d) -> p n k d", n=4, k=KB)
        dft, idft, b_w, c_wT = (mats[:, n] for n in range(4))
        place = place[:, 4 * KB * D:]
        shift = place[:, 0:3 * P].rearrange("p (n q) -> p n q", n=3)
        mask_f = place[:, 3 * P:5 * P]
        d_row = place[:, 5 * P:5 * P + D]
        h4 = room("h4", [P, NT, D])
        space.close()

        with ExitStack() as space:
            def room(name, shape, dt=F32):
                return space.enter_context(nc.sbuf_tensor(name, shape, dt))

            ltri = room("ltri", [P, P])
            ones1 = room("ones1", [P, P])
            seg = room("seg", [P, NE, TILES])
            ramp = room("ramp", [P, RAMP])
            tok = room("tok", [P, TILES])
            gates = room("gates", [P, 4, TILES])
            hot = room("hot", [P, 2, NE, TILES])
            hot2 = room("hot2", [P, NE, TILES])
            tot = room("tot", [P, NE, TILES])
            incl = room("incl", [P, NE, TILES])
            pos = room("pos", [P, NE, TILES])
            picked = room("picked", [P, 2, NE, TILES])
            pos_f = room("pos_f", [P, 2, TILES])
            pos_i = room("pos_i", [P, 2, TILES], I32)
            over = room("over", [P, NE, RAMP])
            chunks = room("chunks", [P, 3, NE])
            bounds = room("bounds", [P, NE + 1], I32)
            pos_s = room("pos_s", [P, 2, SCAT], I32)
            tok_s = room("tok_s", [P, SCAT])
            slots_r = room("slots_r", [SLOT_TILES, P])
            slots_i = room("slots_i", [P, SLOT_TILES], I32)
            idx_s = room("idx_s", [P, 2], I32)
            xg = room("xg", [P, 2, D])
            xg_hi = room("xg_hi", [P, KB, 2 * P], F32R)
            xg_lo = room("xg_lo", [P, KB, 2 * P], F32R)
            w1_raw = room("w1_raw", [P, KB, F])
            w2_raw = room("w2_raw", [P, FB, D])
            w1_hi = [room(f"w1_hi{j}", [P, KB, F], F32R) for j in range(2)]
            w1_lo = [room(f"w1_lo{j}", [P, KB, F], F32R) for j in range(2)]
            w2_hi = [room(f"w2_hi{j}", [P, FB, D], F32R) for j in range(2)]
            w2_lo = [room(f"w2_lo{j}", [P, FB, D], F32R) for j in range(2)]
            b1 = [room(f"b1_{j}", [P, FB]) for j in range(2)]
            b2_row = [room(f"b2_row{j}", [P, D]) for j in range(2)]
            hid_full = room("hid_full", [P, 4, CHUNK])
            hid_hi = room("hid_hi", [P, FB, CHUNK], F32R)
            hid_lo = room("hid_lo", [P, FB, CHUNK], F32R)
            yb = room("yb", [P, 2, D])
            pos_g = room("pos_g", [P, 2, COMB], I32)
            hsum = room("hsum", [P, COMB, D])
            yg = w1_raw[:].rearrange("p k (c d) -> p k c d", d=D)
            part = w2_raw[:, 0:COMB]
            res = w2_raw[:, COMB:2 * COMB]

        h4_dram = nc.dram_tensor("h4_rows", (NB * T, D), F32, kind="Internal").ap()
        slot_dram = nc.dram_tensor("slot_token", (SLOT_TILES * P, 1), F32, kind="Internal").ap()
        y_dram = nc.dram_tensor("y_rows", ((CHUNKS + 1) * CHUNK, D), F32, kind="Internal").ap()
        xn_dram = nc.dram_tensor("xn_rows", (NB * T, D), F32, kind="Internal").ap()

        zeros_ready = signal("zeros_ready", 0)
        mats_done = signal("mats_done", 0)
        mats_read = signal("mats_read", 0)
        loaded = dma_signal("weights_loaded", 0)
        set_up = signal("constants_ready", 0)
        setup_step = signal("setup_step", 0)
        ids_loaded = dma_signal("ids_loaded", 0)
        u_gathered = dma_signal("u_gathered", 0)
        x_loaded = dma_signal("x_loaded", 32)
        gray_ready = signal("gray_ready", 1)
        halo_loaded = dma_signal("halo_loaded", 96)
        conv_done = signal("conv_done", 2)
        abs_done = signal("abs_done", 2)
        h_ready = signal("h_ready", 1)
        ub_ready = signal("ub_ready", 1)
        uT_ready = signal("uT_ready", 1)
        usT_ready = signal("usT_ready", 1)
        text_done = signal("text_done", 1)
        xn_ready = signal("xn_ready", 1)
        xT_turned = signal("xT_turned", 1)
        xT_ready = signal("xT_ready", 1)
        proj_done = signal("proj_done", 3)
        q_ready = signal("q_ready", 1)
        k_ready = signal("k_ready", 1)
        parts_ready = signal("parts_ready", 1)
        stacked = [dma_signal(f"stacked{g}", 16 * 3 * (1 + HG)) for g in range(PAIRS)]
        v_ready = signal("v_ready", 1)
        sumv_done = signal("sumv_done", 1)
        sumv_ready = signal("sumv_ready", 1)
        hbo_ready = signal("hbo_ready", 1)
        head_step = signal("head_step", 3)
        head_stats_ready = signal("head_stats_ready", 1)
        head_rstd_ready = signal("head_rstd_ready", 1)
        head_pool_step = signal("head_pool_step", LN_STEPS)
        scores_done = signal("scores_done", NU)
        sub_done = signal("sub_done", NU)
        exp_done = signal("exp_done", NU)
        turned = signal("probs_turned", NU)
        pT_ready = signal("pT_ready", NU)
        pv_done = signal("pv_done", NU)
        pv_read = signal("pv_read", NT)
        cx_ready = signal("cx_ready", NT)
        cx_turned = signal("cx_turned", NT)
        cxT_ready = signal("cxT_ready", NT)
        wo_done = signal("wo_done", NT)
        h1_ready = signal("h1_ready", NT)
        att_step = signal("attention_step", NU + NT)
        xc_ready = signal("xc_ready", 3)
        xc_turned = signal("xc_turned", 3)
        xcT_ready = signal("xcT_ready", 3)
        block_done = signal("block_done", 2)
        block_ready = signal("block_ready", 2)
        u_done = signal("u_done", 1)
        u_read = signal("u_read", 1)
        cum_ready = signal("cum_ready", 1)
        rot2_step = signal("rot2_step", 1)
        state_re = signal("state_re_ready", 1)
        state_im = signal("state_im_ready", 1)
        ssm_done = signal("ssm_done", 1)
        h3_ready = signal("h3_ready", 1)
        xn_stored = dma_signal("xn_stored", 16)
        logit_done = signal("logit_done", 1)
        logit_read = signal("logit_read", 1)
        stats_ready = signal("stats_ready", 3)
        rstd_ready = signal("rstd_ready", 3)
        chain_pool_step = signal("chain_pool_step", 3 * LN_STEPS)
        chain_step = signal("chain_step", CHAIN_STEPS)
        hb2_ready = signal("hb2_ready", 1)
        up_done = signal("up_done", FB)
        hid_ready = signal("hid_ready", FB)
        down_done = signal("down_done", 1)
        h4_ready = signal("h4_ready", 1)
        h4_stored = dma_signal("h4_stored", 16)
        h4_sent = signal("h4_sent", 1)
        zeroed = dma_signal("slots_zeroed", 0)
        route_loaded = dma_signal("route_loaded", 0)
        diff_ready = signal("diff_ready", 0)
        ratio_ready = signal("ratio_ready", 0)
        hot_ready = signal("hot_ready", 0)
        rank_done = signal("rank_done", 0)
        route_step = signal("route_step", 0)
        bounds_ready = signal("bounds_ready", 0)
        pos_ready = signal("pos_ready", 0)
        staged = signal("scatter_staged", 1)
        scattered = dma_signal("scattered", 16 * 2 * SCAT)
        slots_loaded = dma_signal("slots_loaded", 0)
        slots_turned = signal("slots_turned", 0)
        slots_ready = signal("slots_ready", 0)
        w_loaded = dma_signal("w_loaded", 32)
        b_loaded = [dma_signal(f"b_loaded{j}", 32) for j in range(2)]
        hi_ready = signal("rounded_weights_ready", 1)
        w_split = signal("weights_split", 1)
        xg_rounded = signal("xg_rounded", 1)
        elo_ready = signal("expert_lo_ready", FB)
        pool_go = signal("pool_go", 0)
        gather_go = signal("gather_go", 1)
        idx_ready = signal("idx_ready", 1)
        xg_loaded = dma_signal("xg_loaded", 32)
        xg_turned = signal("xg_turned", 1)
        xgT_ready = signal("xgT_ready", 1)
        eup_done = signal("expert_up_done", FB)
        ehid_ready = signal("expert_hid_ready", FB)
        edown_done = signal("expert_down_done", 2)
        y_ready = signal("y_ready", 2)
        y_stored = dma_signal("y_stored", 16)
        y_sent = signal("y_sent", 1)
        pos_g_ready = signal("pos_g_ready", 1)
        hsum_loaded = dma_signal("hsum_loaded", 16)
        yg_loaded = dma_signal("yg_loaded", 32 * COMB)
        yg_read = signal("yg_read", 1)
        part_ready = signal("part_ready", 1)
        res_ready = signal("res_ready", 1)
        res_sent = signal("res_sent", 1)
        stored = dma_signal("stored", 16)

        block = ctx.enter_context(nc.Block())

        weight_loads = [
            (ident, t["ident"]), (mask_f, t["mask"]), (shift, t["shift"]),
            (wq, t["wqT"]), (wk, t["wkT"]), (wv, t["wvT"]), (wo, t["woT"]), (bq, t["bq"]), (bk, t["bk"]),
            (bv_row, t["bv"].partition_broadcast(P)), (bo_row, t["bo"].partition_broadcast(P)),
            (tap, t["scharr"].partition_broadcast(P)), (tap_edge, t["scharr_dx"]),
            (vt, t["vt"]), (s_col, t["s"]), (wr_col, t["wr"]), (wb, t["wb"]), (rank_cols, t["rank_cols"].partition_broadcast(P)), (rank_own, t["rank_own"]),
            (dft, t["dft"]), (idft, t["idft"]), (sines, t["sines"]), (a_col, t["a"]), (b_w, t["b_w"]),
            (c_wT, t["c_wT"]), (d_row, t["d"].partition_broadcast(P)), (rw, t["rwT"]),
            (rb_row, t["rb"].partition_broadcast(P)), (sw1, t["sw1"]), (sw2, t["sw2"]), (sb1, t["sb1"]),
            (sb2_row, t["sb2"].partition_broadcast(P)),
        ]
        NLOAD = 16 * len(weight_loads)
        NSET = 6

        def expert_bounds(eng, e):
            lo = eng.value_load(bounds[0:1, bass.ds(e, 1)], min_val=0, max_val=CHUNKS - 1)
            hi = eng.value_load(bounds[0:1, bass.ds(e + 1, 1)], min_val=1, max_val=CHUNKS)
            return lo, hi

        @block.sync
        def _(sp):
            sp.dma_start(ids[:], t["ids"]).then_inc(ids_loaded.sem, 16)
            for dst, src in weight_loads:
                sp.dma_start(dst[:], src).then_inc(loaded.sem, 16)
            sp.wait_ge(zeros_ready.sem, zeros_ready.at(0, 1))
            sp.dma_start(slot_dram.rearrange("(c p) o -> c (p o)", p=P), zeros[:]).then_inc(zeroed.sem, 16)
            def load_image(b):
                sp.wait_ge(gray_ready.sem, gray_ready.at(b, 0))
                for rt in range(2):
                    src = t["x"][bass.ds(b, 1), :, rt * P:(rt + 1) * P, :].rearrange("o c p w -> p (o c) w")
                    sp.dma_start(xin[:, rt], src).then_inc(x_loaded.sem, 16)

            def load_halo(b):
                sp.wait_ge(gray_ready.sem, gray_ready.at(b, 1))
                sp.wait_ge(conv_done.sem, conv_done.at(b, 0))
                for dx in range(3):
                    sp.dma_start(halo[dx:dx + 1, 0, :], gray[0:1, 1, dx:dx + IMG]).then_inc(halo_loaded.sem, 16)
                    sp.dma_start(halo[dx:dx + 1, 1, :], gray[P - 1:P, 0, dx:dx + IMG]).then_inc(halo_loaded.sem, 16)

            def store_rows(b):
                sp.wait_ge(xc_ready.sem, xc_ready.at(b, 3))
                rows = xn_dram.rearrange("(b i p) d -> b p i d", b=NB, i=NT)
                sp.dma_start(rows[bass.ds(b, 1)].rearrange("o p i d -> p (o i) d"), xc[:]).then_inc(xn_stored.sem, 16)

            def store_h4(b):
                sp.wait_ge(h4_ready.sem, h4_ready.at(b, 1))
                rows = h4_dram.rearrange("(b i p) d -> b p i d", b=NB, i=NT)
                sp.dma_start(rows[bass.ds(b, 1)].rearrange("o p i d -> p (o i) d"), h4[:]).then_inc(h4_stored.sem, 16)
                sp.wait_ge(h4_stored.sem, h4_stored.at(b, 16))
                sp.sem_inc(h4_sent.sem, 1)

            def stack(b):
                sp.wait_ge(parts_ready.sem, parts_ready.at(b, 1))
                for g in range(PAIRS):
                    for n, (q, k) in enumerate(((q_hi, k_hi), (q_lo, k_hi), (q_hi, k_lo))):
                        rows = slice(2 * DK * g, 2 * DK * (g + 1))
                        sp.dma_start(qs[2 * DK * n:2 * DK * (n + 1), g].bitcast(F32), q[rows].bitcast(F32)
                                     ).then_inc(stacked[g].sem, 16)
                        for j in range(HG):
                            r = DK * (HG * g + j)
                            sp.dma_start(ks[DK * (HG * n + j):DK * (HG * n + j + 1), g, :, j].bitcast(F32),
                                         k[r:r + DK].bitcast(F32)
                                         ).then_inc(stacked[g].sem, 16)

            def sequence(b, chain, head):
                if head:
                    load_image(b + 1)
                    load_halo(b + 1)
                if chain:
                    store_rows(b - 1)
                if head:
                    stack(b + 1)
                if chain:
                    store_h4(b - 1)

            load_image(0)
            load_halo(0)
            stack(0)
            sequence(0, False, True)
            with sp.Fori(1, NB - 1) as b:
                sequence(b, True, True)
            sequence(NB - 1, True, False)
            sequence(NB, True, False)

            sp.wait_ge(h4_sent.sem, h4_sent.at(NB, 0))
            for dst, src in ((ltri, t["ltri"]), (ramp, t["ramp"].partition_broadcast(P)), (tok, t["tok"])):
                sp.dma_start(dst[:], src).then_inc(route_loaded.sem, 16)

            def load_weights(e):
                for dst, src in ((w1_raw, t["w1"]), (w2_raw, t["w2"])):
                    sp.dma_start(dst[:], src[bass.ds(e, 1)].rearrange("o p k n -> (o p) k n")
                                 ).then_inc(w_loaded.sem, 16)

            def load_biases(half, e):
                sp.dma_start(b1[half][:], t["b1"][bass.ds(e, 1)].rearrange("o p n -> (o p) n")
                             ).then_inc(b_loaded[half].sem, 16)
                sp.dma_start(b2_row[half][:], t["b2"][bass.ds(e, 1)].to_broadcast([P, D])
                             ).then_inc(b_loaded[half].sem, 16)

            load_weights(0)
            for half in range(2):
                load_biases(half, half)
            sp.wait_ge(w_split.sem, w_split.at(0, 1))
            load_weights(1)
            sp.wait_ge(scattered.sem, scattered.at(TILES // SCAT - 1, scattered.per))
            sp.dma_start(slots_r[:], slot_dram.rearrange("(c p) o -> c (p o)", p=P)).then_inc(slots_loaded.sem, 16)
            sp.wait_ge(bounds_ready.sem, bounds_ready.at(0, 1))

            def store_chunk(j):
                sp.dma_start(y_dram.rearrange("(j c p) d -> j p c d", c=2, p=P)[bass.ds(j, 1)]
                             .rearrange("o p c d -> p (o c) d"), yb[:]).then_inc(y_stored.sem, 16)
                sp.wait_ge(y_stored.sem, y_stored.at(j, 16))
                sp.sem_inc(y_sent.sem, 1)

            def store_chunks(e):
                lo, hi = expert_bounds(sp, e)
                with sp.Fori(lo, hi) as j:
                    sp.wait_ge(y_ready.sem, y_ready.at(j, 2))
                    store_chunk(j)

            with sp.Fori(0, NE // 2 - 1) as q:
                for half in range(2):
                    e = 2 * q + half
                    sp.wait_ge(w_split.sem, w_split.at(2 * q, half + 2))
                    load_weights(2 * q + (2 + half))
                    store_chunks(e)
                    load_biases(half, 2 * q + (2 + half))
            for half in range(2):
                store_chunks(NE - 2 + half)
            total = sp.value_load(bounds[0:1, NE:NE + 1], min_val=NE, max_val=CHUNKS)
            with sp.Fori(total, CHUNKS + 1) as j:
                store_chunk(j)
            with sp.Fori(0, TILES // COMB) as c:
                sp.wait_ge(yg_read.sem, yg_read.at(c, 0))
                rows = h4_dram.rearrange("(c i p) d -> c p i d", i=COMB, p=P)
                sp.dma_start(hsum[:], rows[bass.ds(c, 1)].rearrange("o p i d -> p (o i) d")
                             ).then_inc(hsum_loaded.sem, 16)
                sp.wait_ge(res_ready.sem, res_ready.at(c, 1))
                sp.dma_start(t["out"].rearrange("(c i p) d -> c p i d", i=COMB, p=P)[bass.ds(c, 1)]
                             .rearrange("o p i d -> p (o i) d"), res).then_inc(stored.sem, 16)
                sp.wait_ge(stored.sem, stored.at(c, 16))
                sp.sem_inc(res_sent.sem, 1)

        @block.gpsimd
        def _(pool):
            for sig in signals:
                pool.sem_inc(sig.sem, 1)
            pool.memset(zeros[:], 0.0).then_inc(zeros_ready.sem, 1)
            pool.wait_ge(ids_loaded.sem, ids_loaded.at(0, 16))
            for b in range(NB):
                pool.indirect_dma_start(u_all[:, b, :], None, t["U"],
                                        bass.IndirectOffsetOnAxis(ids[:, b:b + 1], axis=0)
                                        ).then_inc(u_gathered.sem, 16)
            pool.wait_ge(loaded.sem, loaded.at(0, NLOAD))

            def link(ins, steps, b):
                steps.steps += 1
                ins.then_inc(steps.sem, 1)
                pool.wait_ge(steps.sem, steps.at(b, steps.steps))

            def residual(b):
                pool.wait_ge(h_ready.sem, h_ready.at(b, 1))
                pool.wait_ge(h1_ready.sem, h1_ready.at(b, 0))
                for i in range(NT):
                    ins = pool.tensor_tensor(hbo[:, i], h[:, i], bo_row[:], ALU.add)
                ins.then_inc(hbo_ready.sem, 1)

            def deviations(w, ready, done, steps, b, n):
                mean = w[:, 18:24].rearrange("p (i s) -> p i s", s=2)
                v, y, z = w[:, 24:27], w[:, 27:30], w[:, 30:33]
                pool.wait_ge(ready.sem, ready.at(b, n + 1))
                pool.sem_inc(pool_go.sem, 1)
                link(pool.tensor_scalar(v, mean[:, :, 1], EPS, -0.5, ALU.add, ALU.mult), steps, b)
                pool.sem_inc(pool_go.sem, 1)
                link(pool.tensor_scalar(y.bitcast(I32), v.bitcast(I32), -0.5, float(GUESS), ALU.mult, ALU.add),
                     steps, b)
                for k in range(NEWTON):
                    link(pool.tensor_tensor(z, y, y, ALU.mult), steps, b)
                    link(pool.tensor_tensor(z, z, v, ALU.mult), steps, b)
                    link(pool.tensor_tensor(z, z, c15[:], ALU.add), steps, b)
                    if k < NEWTON - 1:
                        link(pool.tensor_tensor(y, y, z, ALU.mult), steps, b)
                pool.tensor_tensor(y, y, z, ALU.mult).then_inc(done.sem, 1)

            def chain_deviations(b, n):
                if n == 0:
                    chain_pool_step.steps = 0
                deviations(lnc, stats_ready, rstd_ready, chain_pool_step, b, n)

            def head_deviations(b):
                head_pool_step.steps = 0
                deviations(ln, head_stats_ready, head_rstd_ready, head_pool_step, b, 0)

            def states(b):
                pool.wait_ge(cum_ready.sem, cum_ready.at(b, 1))
                pool.tensor_tensor(rot[:, 2], cum[:, 0], turn[:, 1], ALU.mult)
                pool.tensor_tensor(rot[:, 3], cum[:, 1], turn[:, 0], ALU.mult).then_inc(rot2_step.sem, 1)
                pool.wait_ge(rot2_step.sem, rot2_step.at(b, 1))
                pool.wait_ge(ssm_done.sem, ssm_done.at(b, 0))
                pool.tensor_tensor(st[:, 1], rot[:, 2], rot[:, 3], ALU.add).then_inc(state_im.sem, 1)

            def shared_residual(b):
                pool.wait_ge(h3_ready.sem, h3_ready.at(b, 1))
                pool.wait_ge(h4_ready.sem, h4_ready.at(b, 0))
                for i in range(NT):
                    ins = pool.tensor_tensor(hb2[:, i], hc[:, i], sb2_row[:], ALU.add)
                ins.then_inc(hb2_ready.sem, 1)

            def sequence(b, chain, head):
                if chain:
                    chain_deviations(b - 1, 0)
                    chain_deviations(b - 1, 1)
                    states(b - 1)
                    chain_deviations(b - 1, 2)
                    shared_residual(b - 1)
                if head:
                    head_deviations(b + 1)
                    residual(b + 1)

            head_deviations(0)
            residual(0)
            sequence(0, False, True)
            with pool.Fori(1, NB - 1) as b:
                sequence(b, True, True)
            sequence(NB - 1, True, False)
            sequence(NB, True, False)

            pool.wait_ge(pos_ready.sem, pos_ready.at(0, 1))
            pool.wait_ge(zeroed.sem, zeroed.at(0, 16))
            with pool.Fori(0, TILES // SCAT) as c:
                pool.tensor_copy(pos_s[:], pos_i[:, :, bass.ds(c * SCAT, SCAT)])
                pool.tensor_copy(tok_s[:], tok[:, bass.ds(c * SCAT, SCAT)]).then_inc(staged.sem, 1)
                pool.wait_ge(staged.sem, staged.at(c, 1))
                pool.sem_inc(gather_go.sem, 1)
                for k in range(2):
                    for i in range(SCAT):
                        pool.indirect_dma_start(slot_dram, bass.IndirectOffsetOnAxis(pos_s[:, k, i:i + 1], axis=0),
                                                tok_s[:, i:i + 1], None).then_inc(scattered.sem, 16)
                pool.wait_ge(scattered.sem, scattered.at(c, scattered.per))
            def split_weights(half, e, off):
                pool.wait_ge(w_loaded.sem, w_loaded.at(e, 32 * off + 32))
                pool.sem_inc(pool_go.sem, 1)
                pool.tensor_copy(w1_hi[half][:], w1_raw[:])
                pool.tensor_copy(w2_hi[half][:], w2_raw[:]).then_inc(hi_ready.sem, 1)
                pool.wait_ge(hi_ready.sem, hi_ready.at(e, off + 1))
                pool.tensor_tensor(w1_lo[half][:], w1_raw[:], w1_hi[half][:], ALU.subtract)
                pool.tensor_tensor(w2_lo[half][:], w2_raw[:], w2_hi[half][:], ALU.subtract).then_inc(w_split.sem, 1)

            def gather_rows(j, n):
                pool.wait_ge(xg_turned.sem, xg_turned.at(j, n))
                pool.tensor_copy(idx_s[:], slots_i[:, bass.ds(2 * (j + n), 2)]).then_inc(idx_ready.sem, 1)
                pool.wait_ge(idx_ready.sem, idx_ready.at(j, n + 1))
                pool.sem_inc(gather_go.sem, 1)
                for k in range(2):
                    pool.indirect_dma_start(xg[:, k], None, xn_dram,
                                            bass.IndirectOffsetOnAxis(idx_s[:, k:k + 1], axis=0)
                                            ).then_inc(xg_loaded.sem, 16)

            pool.wait_ge(slots_ready.sem, slots_ready.at(0, 1))
            pool.wait_ge(xn_stored.sem, xn_stored.at(NB - 1, 16))
            gather_rows(0, 0)
            gather_rows(0, 1)

            def rows_ahead(e):
                lo, hi = expert_bounds(pool, e)
                with pool.Fori(lo, hi) as j:
                    gather_rows(j, 2)
                return hi

            with pool.Fori(0, NE // 2 - 1) as q:
                for half in range(2):
                    hi = rows_ahead(2 * q + half)
                    pool.wait_ge(edown_done.sem, edown_done.at(hi, 0))
                    split_weights(half, 2 * q, 2 + half)
            for half in range(2):
                rows_ahead(NE - 2 + half)
            pool.wait_ge(y_sent.sem, y_sent.at(CHUNKS + 1, 0))
            with pool.Fori(0, TILES // COMB) as c:
                pool.wait_ge(yg_read.sem, yg_read.at(c, 0))
                pool.tensor_copy(pos_g[:], pos_i[:, :, bass.ds(c * COMB, COMB)]).then_inc(pos_g_ready.sem, 1)
                pool.wait_ge(pos_g_ready.sem, pos_g_ready.at(c, 1))
                pool.sem_inc(gather_go.sem, 1)
                for i in range(COMB):
                    for k in range(2):
                        pool.indirect_dma_start(yg[:, k, i], None, y_dram,
                                                bass.IndirectOffsetOnAxis(pos_g[:, k, i:i + 1], axis=0)
                                                ).then_inc(yg_loaded.sem, 16)

        @block.scalar
        def _(act):
            act.wait_ge(loaded.sem, loaded.at(0, NLOAD))
            act.wait_ge(u_gathered.sem, u_gathered.at(0, 16 * NB))
            act.wait_ge(set_up.sem, set_up.at(0, NSET))

            def text_rows(b):
                act.wait_ge(uT_ready.sem, uT_ready.at(b, 0))
                act.activation(ub[:, 0:R], u_all[:, bass.ds(b, 1), :], ACT.Copy).then_inc(ub_ready.sem, 1)

            def magnitudes(b):
                act.wait_ge(h_ready.sem, h_ready.at(b, 0))
                for i in range(2):
                    act.wait_ge(conv_done.sem, conv_done.at(b, i + 1))
                    act.activation(edges[:, i], ps[:, i], ACT.Abs, scale=0.5).then_inc(abs_done.sem, 1)

            def projections(b):
                act.wait_ge(xT_turned.sem, xT_turned.at(b, 1))
                act.wait_ge(proj_done.sem, proj_done.at(b, 0))
                act.activation(xT[:], ps[:, 2:4, 0:T], ACT.Copy).then_inc(xT_ready.sem, 1)

            def queries(b):
                act.wait_ge(proj_done.sem, proj_done.at(b, 1))
                act.wait_ge(scores_done.sem, scores_done.at(b, 0))
                for dst in (q_hi, q_full):
                    for m in range(KB):
                        ins = act.activation(dst[:, m], ps[:, m, 0:T], ACT.Identity, bias=bq[:, m:m + 1], scale=SCALE)
                ins.then_inc(q_ready.sem, 1)

            def unit(b, s):
                if s < NU:
                    w = slice(0 if s >= UPT else P, 2 * P)
                    act.wait_ge(sub_done.sem, sub_done.at(b, s + 1))
                    act.activation(prob[:, s % PB, :, w], prob[:, s % PB, :, w], ACT.Exp).then_inc(exp_done.sem, 1)
                if TURN <= s < NU + TURN:
                    u = s - TURN
                    k0 = 0 if u >= UPT else 1
                    act.wait_ge(turned.sem, turned.at(b, u + 1))
                    act.wait_ge(pv_done.sem, pv_done.at(b, max(u - 1, 0)))
                    act.activation(pT[:, u % 2, :, k0:2, :],
                                   ps[:, 2 + u % 2, :].rearrange("p (h k q) -> p h k q", h=2, k=2)[:, :, k0:2, :],
                                   ACT.Copy).then_inc(pT_ready.sem, 1)
                if s >= UPT + PV + 1 and (s - UPT - PV - 1) % UPT == 0:
                    i = (s - UPT - PV - 1) // UPT
                    act.wait_ge(cx_turned.sem, cx_turned.at(b, i + 1))
                    act.wait_ge(wo_done.sem, wo_done.at(b, i))
                    act.activation(cxT[:], ps[:, 5, 0:D].rearrange("p (k q) -> p k q", k=KB), ACT.Copy
                                   ).then_inc(cxT_ready.sem, 1)

            def turned_rows(b, n):
                act.wait_ge(xc_turned.sem, xc_turned.at(b, n + 1))
                if n == 0:
                    act.wait_ge(up_done.sem, up_done.at(b, 0))
                elif n == 1:
                    act.wait_ge(block_done.sem, block_done.at(b, 2))
                else:
                    act.wait_ge(ssm_done.sem, ssm_done.at(b, 1))
                act.activation(xcT[:], ps[:, 6:8, 0:T], ACT.Copy).then_inc(xcT_ready.sem, 1)

            def block_outputs(b, n):
                act.wait_ge(block_done.sem, block_done.at(b, n + 1))
                if n == 0:
                    act.activation(srow[:], ps[:, 7, 0:T], ACT.Copy).then_inc(block_ready.sem, 1)
                else:
                    act.activation(g[:].rearrange("p i d -> p (i d)"),
                                   ps[:, 6:8, :].rearrange("p a c -> p (a c)")[:, 0:NT * D], ACT.Gelu_apprx_tanh
                                   ).then_inc(block_ready.sem, 1)

            def hidden_layer(b, f):
                if f == 0:
                    act.wait_ge(down_done.sem, down_done.at(b, 0))
                act.wait_ge(up_done.sem, up_done.at(b, f + 1))
                act.activation(hid[:, f], ps[:, 6 + f % 2, 0:T], ACT.Gelu_apprx_tanh, bias=sb1[:, f:f + 1]
                               ).then_inc(hid_ready.sem, 1)

            def sequence(b, att, chain, head):
                for s in range(SLOTS):
                    if att:
                        unit(b, s)
                    if chain:
                        if s in (TURN0, TURN1, TURN2):
                            turned_rows(b - 1, (TURN0, TURN1, TURN2).index(s))
                        if s in (BLOCK + 1, BLOCK + 2):
                            block_outputs(b - 1, s - BLOCK - 1)
                        if UP <= s < UP + FB:
                            hidden_layer(b - 1, s - UP)
                    if head and s == CONV - 1:
                        text_rows(b + 1)
                    if head and s == CONV:
                        magnitudes(b + 1)
                rest = range(SLOTS - UP, FB) if chain else ()
                if head:
                    projections(b + 1)
                for f in rest[:1]:
                    hidden_layer(b - 1, f)
                if head:
                    queries(b + 1)
                for f in rest[1:]:
                    hidden_layer(b - 1, f)

            text_rows(0)
            magnitudes(0)
            projections(0)
            queries(0)
            sequence(0, True, False, True)
            with act.Fori(1, NB - 1) as b:
                sequence(b, True, True, True)
            sequence(NB - 1, True, True, False)
            sequence(NB, False, True, False)

            act.wait_ge(diff_ready.sem, diff_ready.at(0, 1))
            act.activation(gates[:, 1], gates[:, 0], ACT.Exp).then_inc(ratio_ready.sem, 1)
            act.wait_ge(bounds_ready.sem, bounds_ready.at(0, 1))

            def hidden(q, half, e):
                lo, hi = expert_bounds(act, e)
                with act.Fori(lo, hi) as j:
                    act.wait_ge(b_loaded[half].sem, b_loaded[half].at(q, 32))
                    act.wait_ge(edown_done.sem, edown_done.at(j, 0))
                    for f in range(FB):
                        act.wait_ge(eup_done.sem, eup_done.at(j, f + 1))
                        act.activation(hid_hi[:, f], ps[:, f % 4, 0:CHUNK], ACT.Gelu_apprx_tanh,
                                       bias=b1[half][:, f:f + 1])
                        act.wait_ge(elo_ready.sem, elo_ready.at(j, max(f - 3, 0)))
                        act.activation(hid_full[:, f % 4], ps[:, f % 4, 0:CHUNK], ACT.Gelu_apprx_tanh,
                                       bias=b1[half][:, f:f + 1]).then_inc(ehid_ready.sem, 1)

            with act.Fori(0, NE // 2) as q:
                for half in range(2):
                    hidden(q, half, 2 * q + half)

        @block.vector
        def _(dve):
            dve.wait_ge(loaded.sem, loaded.at(0, NLOAD))

            def link(ins, steps, b):
                steps.steps += 1
                ins.then_inc(steps.sem, 1)
                dve.wait_ge(steps.sem, steps.at(b, steps.steps))

            dve.memset(ones9[:], 1e-9).then_inc(set_up.sem, 1)
            dve.memset(c15[:], 1.5)
            dve.memset(spare[:], 0.0).then_inc(set_up.sem, 1)
            dve.memset(ks[:].bitcast(F32), 0.0)
            dve.memset(vaug[:], 1.0).then_inc(set_up.sem, 1)
            dve.memset(ub[:], 0.0)
            link(dve.memset(gray[:], 0.0), setup_step, 0)
            dve.tensor_copy(ident_bf[:], ident[:])
            for j in range(2):
                ins = dve.tensor_copy(mask_bf[:, j], mask_f[:])
            ins.then_inc(set_up.sem, 1)
            link(dve.memset(band_edge[:], 0.0), setup_step, 0)
            for dy in range(3):
                for o in range(2):
                    for dx in range(3):
                        k = (o * 3 + dy) * 3 + dx
                        if dy == 0:
                            ins = dve.tensor_scalar(band[:, o, dx], shift[:, dy], tap[:, k:k + 1], None, ALU.mult)
                        else:
                            ins = dve.scalar_tensor_tensor(out=band[:, o, dx], in0=shift[:, dy], scalar=tap[:, k:k + 1],
                                                           in1=band[:, o, dx], op0=ALU.mult, op1=ALU.add)
                link(ins, setup_step, 0)
            for o in range(2):
                dve.tensor_copy(band_edge[:, o, 0, P - 1:P], tap_edge[:, o, 2:3])
                ins = dve.tensor_copy(band_edge[:, o, 1, 0:1], tap_edge[:, o, 0:1])
            ins.then_inc(set_up.sem, 1)
            link(dve.tensor_scalar(bq[:], bq[:], SCALE, None, ALU.mult), setup_step, 0)
            dve.memset(sumv[:], 0.0).then_inc(set_up.sem, 1)

            dve.memset(ones_t[:], 1.0)
            for i in range(NT):
                dve.tensor_scalar(before[:, i], rank_cols[:], rank_own[:, i:i + 1], None, ALU.is_lt)
                dve.tensor_scalar(after[:, i], rank_cols[:], rank_own[:, i:i + 1], None, ALU.is_ge)
            for k in range(KB):
                dve.tensor_tensor(d_diag[:, k], ident[:], d_row[:, k * P:(k + 1) * P], ALU.mult)
                ins = dve.tensor_copy(wr_bc[:, k], wr_col[:, k:k + 1].to_broadcast([P, P]))
            link(ins, setup_step, 0)
            dve.wait_ge(mats_done.sem, mats_done.at(0, 1))
            for k in range(KB):
                dve.tensor_copy(fb[:, k], ps[:, k, 0:D])
                dve.tensor_copy(ce[:, k], ps[:, 2 + k, 0:D])
            w, w2, den, re, im, nim = (om[:, j:j + 1] for j in range(6))
            dve.tensor_copy(w, ps[:, 4, 0:1]).then_inc(mats_read.sem, 1)
            dve.wait_ge(mats_read.sem, mats_read.at(0, 1))
            link(dve.tensor_tensor(w2, w, w, ALU.mult), setup_step, 0)
            link(dve.tensor_scalar(den, w2, 1.0, None, ALU.add), setup_step, 0)
            link(dve.reciprocal(nim, den), setup_step, 0)
            link(dve.tensor_scalar(den, w2, -1.0, 1.0, ALU.mult, ALU.add), setup_step, 0)
            dve.tensor_tensor(re, den, nim, ALU.mult)
            link(dve.scalar_tensor_tensor(out=im, in0=w, scalar=-2.0, in1=nim, op0=ALU.mult, op1=ALU.mult), setup_step, 0)
            dve.memset(turn[:, 0, 0:1], 1.0)
            dve.memset(turn[:, 1, 0:1], 0.0)
            n = 1
            while n < T:
                m = min(n, T - n)
                link(dve.tensor_scalar(nim, im, -1.0, None, ALU.mult), setup_step, 0)
                dve.tensor_scalar(h[:, 0, 0:m], turn[:, 0, 0:m], re, None, ALU.mult)
                dve.tensor_scalar(h[:, 1, 0:m], turn[:, 0, 0:m], im, None, ALU.mult)
                dve.tensor_tensor(w2, im, im, ALU.mult)
                link(dve.tensor_tensor(den, re, im, ALU.mult), setup_step, 0)
                dve.scalar_tensor_tensor(out=turn[:, 0, n:n + m], in0=turn[:, 1, 0:m], scalar=nim,
                                         in1=h[:, 0, 0:m], op0=ALU.mult, op1=ALU.add)
                link(dve.scalar_tensor_tensor(out=turn[:, 1, n:n + m], in0=turn[:, 1, 0:m], scalar=re,
                                                   in1=h[:, 1, 0:m], op0=ALU.mult, op1=ALU.add), setup_step, 0)
                dve.tensor_scalar(im, den, 2.0, None, ALU.mult)
                link(dve.tensor_tensor(re, re, re, ALU.mult), setup_step, 0)
                link(dve.tensor_tensor(re, re, w2, ALU.subtract), setup_step, 0)
                n *= 2


            def statistics(src, w, ready, steps, b):
                for i in range(NT):
                    ins = dve.bn_stats(w[:, 6 * i:6 * i + 6], src[:, i])
                link(ins, steps, b)
                dve.memset(w[:, 40:41], 0.0)
                for i in range(NT):
                    ins = dve.bn_aggr(w[:, 18 + 2 * i:20 + 2 * i], w[:, 6 * i:6 * i + 6])
                ins.then_inc(ready.sem, 1)

            def normalise(src, dst, w):
                for i in range(NT):
                    ins = dve.tensor_scalar(dst[:, i], src[:, i], w[:, 18 + 2 * i:19 + 2 * i], w[:, 27 + i:28 + i],
                                            ALU.subtract, ALU.mult)
                return ins

            def make_gray(b):
                head_step.steps = 0
                dve.wait_ge(x_loaded.sem, x_loaded.at(b, 32))
                dve.wait_ge(conv_done.sem, conv_done.at(b, 0))
                link(dve.tensor_scalar(gsum[:], xin[:, :, 0], GRAY[0], None, ALU.mult), head_step, b)
                link(dve.scalar_tensor_tensor(out=gsum[:], in0=xin[:, :, 1], scalar=GRAY[1], in1=gsum[:],
                                              op0=ALU.mult, op1=ALU.add), head_step, b)
                dve.scalar_tensor_tensor(out=gray[:, :, 1:IMG + 1], in0=xin[:, :, 2], scalar=GRAY[2], in1=gsum[:],
                                         op0=ALU.mult, op1=ALU.add).then_inc(gray_ready.sem, 1)

            def make_text(b):
                dve.wait_ge(uT_ready.sem, uT_ready.at(b, 1))
                dve.wait_ge(text_done.sem, text_done.at(b, 0))
                dve.tensor_scalar(usT[:], ps[0:R, 2, 0:P], s_col[:], None, ALU.mult).then_inc(usT_ready.sem, 1)

            def make_rows(b):
                dve.wait_ge(abs_done.sem, abs_done.at(b, 2))
                dve.wait_ge(hbo_ready.sem, hbo_ready.at(b, 0))
                dve.tensor_tensor(h[:, 0:2], edges[:, :, 0:IMG], edges[:, :, IMG:2 * IMG], ALU.add)
                dve.wait_ge(text_done.sem, text_done.at(b, 1))
                dve.tensor_copy(h[:, 2], ps[:, 2, D:2 * D]).then_inc(h_ready.sem, 1)
                dve.wait_ge(h_ready.sem, h_ready.at(b, 1))
                statistics(h, ln, head_stats_ready, head_step, b)

            def normalise_rows(b):
                dve.wait_ge(xT_turned.sem, xT_turned.at(b, 0))
                dve.wait_ge(head_rstd_ready.sem, head_rstd_ready.at(b, 1))
                normalise(h, xn, ln).then_inc(xn_ready.sem, 1)
                assert head_step.steps == head_step.per

            def keys_and_values(b):
                dve.wait_ge(proj_done.sem, proj_done.at(b, 2))
                dve.wait_ge(scores_done.sem, scores_done.at(b, 0))
                for m in range(KB):
                    ins = dve.tensor_scalar(k_hi[:, m], ps[:, 2 + m, 0:T], bk[:, m:m + 1], None, ALU.add)
                ins.then_inc(k_ready.sem, 1)
                dve.wait_ge(k_ready.sem, k_ready.at(b, 1))
                for m in range(KB):
                    dve.scalar_tensor_tensor(out=k_lo[:, m], in0=ps[:, 2 + m, 0:T], scalar=bk[:, m:m + 1],
                                             in1=k_hi[:, m], op0=ALU.add, op1=ALU.subtract)
                dve.wait_ge(q_ready.sem, q_ready.at(b, 1))
                dve.tensor_tensor(q_lo[:], q_full[:], q_hi[:], ALU.subtract).then_inc(parts_ready.sem, 1)
                dve.wait_ge(proj_done.sem, proj_done.at(b, 3))
                dve.wait_ge(pv_done.sem, pv_done.at(b, 0))
                for i in range(NT):
                    src = ps[:, 4, i * D:(i + 1) * D] if i < 2 else ps[:, 5, 0:D]
                    ins = dve.tensor_tensor(vaug[:, i, :, 0:DK], src.rearrange("p (h d) -> p h d", h=NH),
                                            bv_row[:].rearrange("p (h d) -> p h d", h=NH), ALU.add)
                ins.then_inc(v_ready.sem, 1)

            def values_sum(b):
                dve.wait_ge(sumv_done.sem, sumv_done.at(b, 1))
                dve.tensor_copy(sumv[:], ps[:, 5, D:2 * D]).then_inc(sumv_ready.sem, 1)

            def unit(b, s):
                if s < NU:
                    w = slice(0 if s >= UPT else P, 2 * P)
                    sc = ps[:, s % 2, :].rearrange("p (h k) -> p h k", h=2)[:, :, w]
                    n = 2 * P - w.start
                    dve.wait_ge(scores_done.sem, scores_done.at(b, s + 1))
                    link(dve.tensor_reduce(mx[:, s % 2], sc, AX_X, ALU.max), att_step, b)
                    dve.wait_ge(turned.sem, turned.at(b, max(s - PB + 1, 0)))
                    dve.tensor_tensor(prob[:, s % PB, :, w], sc, mx[:, s % 2].unsqueeze(2).to_broadcast([P, HG, n]),
                                      ALU.subtract).then_inc(sub_done.sem, 1)
                if s >= UPT + PV and (s - UPT - PV) % UPT == 0:
                    i = (s - UPT - PV) // UPT
                    pv = ps[:, 4, 0:NH * (DK + 1)].rearrange("p (h d) -> p h d", h=NH)
                    dve.wait_ge(pv_done.sem, pv_done.at(b, UPT * (i + 1)))
                    link(dve.reciprocal(rden[:], pv[:, :, DK]), att_step, b)
                    dve.wait_ge(cx_turned.sem, cx_turned.at(b, i))
                    dve.tensor_tensor(cx[:].rearrange("p (h d) -> p h d", h=NH), pv[:, :, 0:DK],
                                      rden[:].unsqueeze(2).to_broadcast([P, NH, DK]),
                                      ALU.mult).then_inc(pv_read.sem, 1)
                    dve.wait_ge(pv_read.sem, pv_read.at(b, i + 1))
                    dve.wait_ge(sumv_ready.sem, sumv_ready.at(b, 1))
                    dve.tensor_tensor(cx[:], cx[:], sumv[:], ALU.add).then_inc(cx_ready.sem, 1)
                if s >= UPT + PV + 3 and (s - UPT - PV - 3) % UPT == 0:
                    i = (s - UPT - PV - 3) // UPT
                    dve.wait_ge(wo_done.sem, wo_done.at(b, i + 1))
                    dve.wait_ge(hbo_ready.sem, hbo_ready.at(b, 1))
                    dve.tensor_tensor(h1[:, i], hbo[:, i], ps[:, 5, D:2 * D], ALU.add).then_inc(h1_ready.sem, 1)

            def chain_rows(b, n):
                statistics(hc, lnc, stats_ready, chain_step, b)

            def chain_scale(b, n):
                dve.wait_ge(xc_turned.sem, xc_turned.at(b, n))
                dve.wait_ge(rstd_ready.sem, rstd_ready.at(b, n + 1))
                normalise(hc, xc, lnc).then_inc(xc_ready.sem, 1)

            trial = [rot[:, 0], rot[:, 1], rot[:, 2], rot[:, 3], cum[:, 0], cum[:, 1]]

            def chain(b, s):
                if s == 0:
                    chain_step.steps = 0
                    dve.wait_ge(h1_ready.sem, h1_ready.at(b, NT))
                    link(dve.tensor_copy(hc[:], h1[:]), chain_step, b)
                    chain_rows(b, 0)
                if s == TURN0 - 1:
                    chain_scale(b, 0)
                if s == RANK:
                    dve.wait_ge(block_ready.sem, block_ready.at(b, 1))
                    dve.wait_ge(state_im.sem, state_im.at(b, 0))
                    for i in range(NT):
                        ins = dve.scalar_tensor_tensor(out=trial[i][:, 0:P], in0=srow[:, i * P:(i + 1) * P], scalar=1.0,
                                                       in1=ident[:], op0=ALU.mult, op1=ALU.mult,
                                                       accum_out=own[:, i:i + 1])
                    link(ins, chain_step, b)
                if RANK <= s < RANK + NT:
                    i = s - RANK
                    dve.scalar_tensor_tensor(out=trial[2 * i], in0=srow[:], scalar=own[:, i:i + 1],
                                             in1=before[:, i], op0=ALU.is_ge, op1=ALU.mult,
                                             accum_out=count[:, 0, i:i + 1])
                    ins = dve.scalar_tensor_tensor(out=trial[2 * i + 1], in0=srow[:], scalar=own[:, i:i + 1],
                                                   in1=after[:, i], op0=ALU.is_gt, op1=ALU.mult,
                                                   accum_out=count[:, 1, i:i + 1])
                    if i == NT - 1:
                        link(ins, chain_step, b)
                if s == RANK + NT:
                    link(dve.tensor_tensor(sel[:], count[:, 0], count[:, 1], ALU.add), chain_step, b)
                    dve.tensor_scalar(sel[:], sel[:], KEEP - 0.5, None, ALU.is_lt)
                    dve.wait_ge(block_ready.sem, block_ready.at(b, 2))
                    link(dve.tensor_tensor(g[:], g[:], xc[:], ALU.subtract), chain_step, b)
                if s == RANK + NT + 1:
                    for i in range(NT):
                        ins = dve.scalar_tensor_tensor(out=g[:, i], in0=g[:, i], scalar=sel[:, i:i + 1], in1=xc[:, i],
                                                       op0=ALU.mult, op1=ALU.add)
                    link(ins, chain_step, b)
                if s == RANK + NT + 2:
                    link(dve.tensor_tensor(hc[:], hc[:], g[:], ALU.add), chain_step, b)
                    chain_rows(b, 1)
                if s == TURN1 - 1:
                    chain_scale(b, 1)
                if s == STATE:
                    dve.wait_ge(u_done.sem, u_done.at(b, 1))
                    dve.tensor_tensor(rot[:, 0], ps[:, 6, 0:T], turn[:, 0], ALU.mult)
                    dve.tensor_tensor(rot[:, 1], ps[:, 7, 0:T], turn[:, 1], ALU.mult)
                    dve.tensor_tensor(rot[:, 2], ps[:, 7, 0:T], turn[:, 0], ALU.mult)
                    dve.tensor_tensor(rot[:, 3], ps[:, 6, 0:T], turn[:, 1], ALU.mult).then_inc(u_read.sem, 1)
                    dve.wait_ge(u_read.sem, u_read.at(b, 1))
                if s == STATE + 1:
                    link(dve.tensor_tensor(rot[:, 0], rot[:, 0], rot[:, 1], ALU.add), chain_step, b)
                    link(dve.tensor_tensor(rot[:, 2], rot[:, 2], rot[:, 3], ALU.subtract), chain_step, b)
                    dve.tensor_tensor_scan(cum[:, 0], ones_t[:], rot[:, 0], 0.0, ALU.mult, ALU.add)
                if s == STATE + 2:
                    dve.tensor_tensor_scan(cum[:, 1], ones_t[:], rot[:, 2], 0.0, ALU.mult, ALU.add
                                           ).then_inc(cum_ready.sem, 1)
                    dve.wait_ge(cum_ready.sem, cum_ready.at(b, 1))
                if s == STATE + 3:
                    dve.tensor_tensor(rot[:, 0], cum[:, 0], turn[:, 0], ALU.mult)
                    link(dve.tensor_tensor(rot[:, 1], cum[:, 1], turn[:, 1], ALU.mult), chain_step, b)
                    dve.wait_ge(ssm_done.sem, ssm_done.at(b, 0))
                    dve.tensor_tensor(st[:, 0], rot[:, 0], rot[:, 1], ALU.subtract).then_inc(state_re.sem, 1)
                if s == OUT + 1:
                    dve.wait_ge(ssm_done.sem, ssm_done.at(b, 1))
                    dve.tensor_tensor(hc[:].rearrange("p i d -> p (i d)"), hc[:].rearrange("p i d -> p (i d)"),
                                      ps[:, 6:8, :].rearrange("p a c -> p (a c)")[:, 0:NT * D], ALU.add
                                      ).then_inc(h3_ready.sem, 1)
                    dve.wait_ge(h3_ready.sem, h3_ready.at(b, 1))
                    chain_rows(b, 2)
                if s == TURN2 - 1:
                    chain_scale(b, 2)
                if s == UP:
                    dve.wait_ge(logit_done.sem, logit_done.at(b, 1))
                    for i in range(NT):
                        ins = dve.tensor_tensor(logit[:, i], ps[:, 7, i * NE:(i + 1) * NE], rb_row[:], ALU.add)
                    ins.then_inc(logit_read.sem, 1)
                    dve.wait_ge(logit_read.sem, logit_read.at(b, 1))
                    dve.memset(spare[:], 0.0)
                    for i in range(NT):
                        ins = dve.max(v8[:, i], logit[:, i])
                    link(ins, chain_step, b)
                if s == UP + 1:
                    dve.memset(spare[:], 0.0)
                    for i in range(NT):
                        ins = dve.max_index(i8[:, i], v8[:, i], logit[:, i])
                    link(ins, chain_step, b)
                    dve.tensor_copy(top_v[:, bass.ds(b, 1)].rearrange("p o i k -> p (o i) k"), v8[:, :, 0:2])
                    dve.tensor_copy(top_i[:, bass.ds(b, 1)].rearrange("p o i k -> p (o i) k"), i8[:, :, 0:2])
                    assert chain_step.steps == chain_step.per, chain_step.steps

            def shared_sum(b):
                dve.wait_ge(xn_stored.sem, xn_stored.at(b, 16))
                dve.wait_ge(h4_sent.sem, h4_sent.at(b, 0))
                dve.wait_ge(hb2_ready.sem, hb2_ready.at(b, 1))
                dve.wait_ge(down_done.sem, down_done.at(b, 1))
                dve.tensor_tensor(h4[:].rearrange("p i d -> p (i d)"), hb2[:].rearrange("p i d -> p (i d)"),
                                  ps[:, 6:8, :].rearrange("p a c -> p (a c)")[:, 0:NT * D], ALU.add
                                  ).then_inc(h4_ready.sem, 1)

            def sequence(b, att, chained, head):
                att_step.steps = 0
                for s in range(SLOTS):
                    if att:
                        unit(b, s)
                    if chained:
                        chain(b - 1, s)
                    if head and s == GRAY_AT:
                        make_gray(b + 1)
                    if head and s == CONV + 1:
                        make_text(b + 1)
                    if head and s == CONV + 2:
                        make_rows(b + 1)
                    if head and s == CONV + 4:
                        normalise_rows(b + 1)
                if head:
                    keys_and_values(b + 1)
                if chained:
                    shared_sum(b - 1)
                if head:
                    values_sum(b + 1)

            make_gray(0)
            make_text(0)
            make_rows(0)
            normalise_rows(0)
            keys_and_values(0)
            values_sum(0)
            sequence(0, True, False, True)
            with dve.Fori(1, NB - 1) as b:
                sequence(b, True, True, True)
            sequence(NB - 1, True, True, False)
            sequence(NB, False, True, False)

            dve.wait_ge(h4_sent.sem, h4_sent.at(NB, 0))
            dve.wait_ge(route_loaded.sem, route_loaded.at(0, 48))
            v = top_v[:].rearrange("p b i k -> p (b i) k")
            ix = top_i[:].rearrange("p b i k -> p (b i) k")
            dve.tensor_tensor(gates[:, 0], v[:, :, 1], v[:, :, 0], ALU.subtract).then_inc(diff_ready.sem, 1)
            for k in range(2):
                for e in range(NE):
                    ins = dve.tensor_scalar(hot[:, k, e], ix[:, :, k], float(e), None, ALU.is_equal)
            dve.memset(ones1[:], 1.0)
            link(dve.memset(seg[:], 1.0), route_step, 0)
            dve.memset(seg[:, :, 0:1], 0.0)
            dve.tensor_tensor(hot2[:], hot[:, 0], hot[:, 1], ALU.add).then_inc(hot_ready.sem, 1)
            dve.wait_ge(ratio_ready.sem, ratio_ready.at(0, 1))
            link(dve.tensor_scalar(gates[:, 0], gates[:, 1], 1.0, None, ALU.add), route_step, 0)
            link(dve.reciprocal(gates[:, 2], gates[:, 0]), route_step, 0)
            dve.tensor_tensor(gates[:, 3], gates[:, 1], gates[:, 2], ALU.mult)
            dve.wait_ge(rank_done.sem, rank_done.at(0, 1))
            link(dve.tensor_copy(tot[:], ps[:, 1, 0:NE * TILES].rearrange("p (e t) -> p e t", e=NE)), route_step, 0)
            flat = "p e t -> p (e t)"
            link(dve.tensor_tensor_scan(incl[:].rearrange(flat), seg[:].rearrange(flat), tot[:].rearrange(flat),
                                             0.0, ALU.mult, ALU.add), route_step, 0)
            link(dve.tensor_tensor(over[:], incl[:, :, TILES - 1:TILES].to_broadcast([P, NE, RAMP]),
                                        ramp[:].unsqueeze(1).to_broadcast([P, NE, RAMP]), ALU.is_gt), route_step, 0)
            link(dve.tensor_reduce(chunks[:, 0], over[:], AX_X, ALU.add), route_step, 0)
            link(dve.tensor_scalar(chunks[:, 0], chunks[:, 0], 1.0, None, ALU.max), route_step, 0)
            link(dve.tensor_tensor_scan(chunks[:, 1], ones1[:, 0:NE], chunks[:, 0], 0.0, ALU.mult, ALU.add), route_step, 0)
            link(dve.tensor_tensor(chunks[:, 2], chunks[:, 1], chunks[:, 0], ALU.subtract), route_step, 0)
            dve.memset(bounds[:, 0:1], 0)
            dve.tensor_copy(bounds[:, 1:NE + 1], chunks[:, 1]).then_inc(bounds_ready.sem, 1)
            link(dve.tensor_tensor(incl[:], incl[:], tot[:], ALU.subtract), route_step, 0)
            link(dve.tensor_tensor(pos[:], incl[:], ps[:, 0, 0:NE * TILES].rearrange("p (e t) -> p e t", e=NE),
                                        ALU.add), route_step, 0)
            for e in range(NE):
                ins = dve.scalar_tensor_tensor(out=tot[:, e], in0=chunks[:, 2, e:e + 1].to_broadcast([P, TILES]),
                                             scalar=float(CHUNK), in1=pos[:, e], op0=ALU.mult, op1=ALU.add)
            link(ins, route_step, 0)
            for k in range(2):
                ins = dve.tensor_tensor(picked[:, k], hot[:, k], tot[:], ALU.mult)
            link(ins, route_step, 0)
            for k in range(2):
                ins = dve.tensor_reduce(pos_f[:, k], picked[:, k].rearrange("p e t -> p t e"), AX_X, ALU.add)
            link(ins, route_step, 0)
            dve.tensor_copy(pos_i[:], pos_f[:]).then_inc(pos_ready.sem, 1)
            for e in range(2):
                dve.wait_ge(w_loaded.sem, w_loaded.at(e, 32))
                dve.tensor_copy(w1_hi[e][:], w1_raw[:])
                dve.tensor_copy(w2_hi[e][:], w2_raw[:]).then_inc(hi_ready.sem, 1)
                dve.wait_ge(hi_ready.sem, hi_ready.at(e, 1))
                dve.tensor_tensor(w1_lo[e][:], w1_raw[:], w1_hi[e][:], ALU.subtract)
                dve.tensor_tensor(w2_lo[e][:], w2_raw[:], w2_hi[e][:], ALU.subtract).then_inc(w_split.sem, 1)
            dve.wait_ge(slots_turned.sem, slots_turned.at(0, 1))
            dve.tensor_copy(slots_i[:], ps[:, 7, 0:SLOT_TILES]).then_inc(slots_ready.sem, 1)
            dve.wait_ge(bounds_ready.sem, bounds_ready.at(0, 1))

            def turn_chunk(j):
                dve.wait_ge(xg_turned.sem, xg_turned.at(j, 1))
                rows = ps[:, 6, :].rearrange("p (k n) -> p k n", k=KB)
                dve.tensor_copy(xg_hi[:], rows).then_inc(xg_rounded.sem, 1)
                dve.wait_ge(xg_rounded.sem, xg_rounded.at(j, 1))
                dve.tensor_tensor(xg_lo[:], rows, xg_hi[:], ALU.subtract).then_inc(xgT_ready.sem, 1)

            def outputs(q, half, e):
                lo, hi = expert_bounds(dve, e)
                with dve.Fori(lo, hi) as j:
                    dve.wait_ge(b_loaded[half].sem, b_loaded[half].at(q, 32))
                    for f in range(FB):
                        dve.wait_ge(ehid_ready.sem, ehid_ready.at(j, f + 1))
                        dve.tensor_tensor(hid_lo[:, f], hid_full[:, f % 4], hid_hi[:, f], ALU.subtract
                                          ).then_inc(elo_ready.sem, 1)
                    dve.wait_ge(eup_done.sem, eup_done.at(j, FB))
                    turn_chunk(j + 1)
                    dve.wait_ge(y_sent.sem, y_sent.at(j, 0))
                    for k in range(2):
                        dve.wait_ge(edown_done.sem, edown_done.at(j, k + 1))
                        dve.tensor_tensor(yb[:, k], ps[:, 4 + k, 0:D], b2_row[half][:], ALU.add
                                          ).then_inc(y_ready.sem, 1)

            turn_chunk(0)
            with dve.Fori(0, NE // 2) as q:
                for half in range(2):
                    outputs(q, half, 2 * q + half)
            with dve.Fori(0, TILES // COMB) as c:
                dve.wait_ge(yg_loaded.sem, yg_loaded.at(c, yg_loaded.per))
                dve.wait_ge(hsum_loaded.sem, hsum_loaded.at(c, 16))
                for i in range(COMB):
                    ins = dve.scalar_tensor_tensor(out=part[:, i], in0=yg[:, 0, i],
                                                   scalar=gates[:, 2, bass.ds(c * COMB + i, 1)],
                                                   in1=hsum[:, i],
                                                   op0=ALU.mult, op1=ALU.add)
                ins.then_inc(part_ready.sem, 1)
                dve.wait_ge(part_ready.sem, part_ready.at(c, 1))
                dve.wait_ge(res_sent.sem, res_sent.at(c, 0))
                for i in range(COMB):
                    ins = dve.scalar_tensor_tensor(out=res[:, i], in0=yg[:, 1, i],
                                                   scalar=gates[:, 3, bass.ds(c * COMB + i, 1)], in1=part[:, i],
                                                   op0=ALU.mult, op1=ALU.add)
                ins.then_inc(res_ready.sem, 1)
                dve.wait_ge(res_ready.sem, res_ready.at(c, 1))
                dve.memset(spare[:], 0.0).then_inc(yg_read.sem, 1)

        @block.tensor
        def _(pe):
            pe.wait_ge(loaded.sem, loaded.at(0, NLOAD))
            pe.wait_ge(set_up.sem, set_up.at(0, NSET))
            for k in range(KB):
                for j in range(KB):
                    pe.matmul(ps[:, k, 0:D], b_w[:, j, k * P:(k + 1) * P], dft[:, j], start=(j == 0), stop=(j == KB - 1))
                for j in range(KB):
                    pe.matmul(ps[:, 2 + k, 0:D], idft[:, j, k * P:(k + 1) * P], c_wT[:, j],
                              start=(j == 0), stop=(j == KB - 1))
            pe.matmul(ps[:, 4, 0:1], sines[:], a_col[:], start=True, stop=True).then_inc(mats_done.sem, 1)
            pe.wait_ge(mats_read.sem, mats_read.at(0, 1))

            def convolution(b):
                pe.wait_ge(gray_ready.sem, gray_ready.at(b, 1))
                pe.wait_ge(halo_loaded.sem, halo_loaded.at(b, 96))
                pe.wait_ge(sub_done.sem, sub_done.at(b, 0))
                for i in range(2):
                    for o in range(2):
                        dst = ps[:, i, o * IMG:(o + 1) * IMG]
                        for dx in range(3):
                            pe.matmul(dst, band[:, o, dx], gray[:, i, dx:dx + IMG], start=(dx == 0), stop=False)
                        ins = pe.matmul(dst, band_edge[:, o, i], halo[:, i], start=False, stop=True)
                    ins.then_inc(conv_done.sem, 1)

            def turn_text(b):
                pe.wait_ge(ub_ready.sem, ub_ready.at(b, 1))
                pe.wait_ge(pT_ready.sem, pT_ready.at(b, 0))
                pe.transpose(ps[:, 2, 0:P], ub[:], ident[:]).then_inc(uT_ready.sem, 1)

            def text(b):
                pe.wait_ge(usT_ready.sem, usT_ready.at(b, 1))
                pe.matmul(ps[:, 2, D:2 * D], usT[:], vt[:], start=True, stop=True).then_inc(text_done.sem, 1)

            def turn_rows(b):
                pe.wait_ge(xn_ready.sem, xn_ready.at(b, 1))
                for k in range(KB):
                    for i in range(NT):
                        ins = pe.transpose(ps[:, 2 + k, i * P:(i + 1) * P], xn[:, i, k * P:(k + 1) * P], ident[:])
                ins.then_inc(xT_turned.sem, 1)

            def queries_and_keys(b):
                pe.wait_ge(xT_ready.sem, xT_ready.at(b, 1))
                pe.wait_ge(abs_done.sem, abs_done.at(b, 2))
                for w, first in ((wq, 0), (wk, 2)):
                    for m in range(KB):
                        for k in range(KB):
                            ins = pe.matmul(ps[:, first + m, 0:T], w[:, k, m * P:(m + 1) * P], xT[:, k],
                                            start=(k == 0), stop=(k == KB - 1))
                    ins.then_inc(proj_done.sem, 1)

            def values(b):
                pe.wait_ge(pv_read.sem, pv_read.at(b, 0))
                pe.wait_ge(h1_ready.sem, h1_ready.at(b, 0))
                for i in range(NT):
                    dst = ps[:, 4, i * D:(i + 1) * D] if i < 2 else ps[:, 5, 0:D]
                    for k in range(KB):
                        ins = pe.matmul(dst, xT[:, k, i * P:(i + 1) * P], wv[:, k], start=(k == 0), stop=(k == KB - 1))
                ins.then_inc(proj_done.sem, 1)

            def values_sum(b):
                pe.wait_ge(v_ready.sem, v_ready.at(b, 1))
                for i in range(NT):
                    ins = pe.matmul(ps[:, 5, D:2 * D].rearrange("p (h d) -> p h d", h=NH), ones9[:], vaug[:, i, :, 0:DK],
                                    start=(i == 0), stop=(i == NT - 1))
                ins.then_inc(sumv_done.sem, 1)

            def unit(b, s):
                if s < NU:
                    i, g = s // UPT, s % UPT
                    c0 = 0 if i else P
                    keys = slice((i - 1) * P + c0, (i + 1) * P)
                    m, r = g // PAIRS, g % PAIRS
                    if s < PAIRS:
                        pe.wait_ge(stacked[r].sem, stacked[r].at(b, stacked[r].per))
                    pe.wait_ge(sub_done.sem, sub_done.at(b, max(s - 1, 0)))
                    dst = ps[:, s % 2, :].rearrange("p (h k) -> p h k", h=2)[:, :, c0:2 * P]
                    pe.matmul(dst, qs[:, r, m, i * P:(i + 1) * P], ks[:, r, m, :, keys], start=True, stop=False)
                    pe.matmul(dst, ident_bf[:], mask_bf[:, :, c0:2 * P], start=False, stop=True
                              ).then_inc(scores_done.sem, 1)
                if TURN <= s < NU + TURN:
                    u = s - TURN
                    pe.wait_ge(exp_done.sem, exp_done.at(b, u + 1))
                    pe.wait_ge(pT_ready.sem, pT_ready.at(b, max(u - 1, 0)))
                    for hh in range(HG):
                        for k in range(0 if u >= UPT else 1, 2):
                            ins = pe.transpose(ps[:, 2 + u % 2, (2 * hh + k) * P:(2 * hh + k + 1) * P],
                                               prob[:, u % PB, hh, k * P:(k + 1) * P], ident[:])
                    ins.then_inc(turned.sem, 1)
                if PV <= s < NU + PV:
                    u = s - PV
                    i, g = u // UPT, u % UPT
                    if g == 0:
                        pe.wait_ge(pv_read.sem, pv_read.at(b, i))
                    pe.wait_ge(pT_ready.sem, pT_ready.at(b, u + 1))
                    for hh in range(HG):
                        hd = g * HG + hh
                        for k in range(0 if i else 1, 2):
                            ins = pe.matmul(ps[:, 4, hd * (DK + 1):(hd + 1) * (DK + 1)], pT[:, u % 2, hh, k],
                                            vaug[:, i - 1 + k, hd, :], start=(k == (0 if i else 1)), stop=(k == 1))
                    ins.then_inc(pv_done.sem, 1)
                if s >= UPT + PV + 1 and (s - UPT - PV - 1) % UPT == 0:
                    i = (s - UPT - PV - 1) // UPT
                    pe.wait_ge(cx_ready.sem, cx_ready.at(b, i + 1))
                    pe.wait_ge(h1_ready.sem, h1_ready.at(b, i))
                    for k in range(KB):
                        ins = pe.transpose(ps[:, 5, k * P:(k + 1) * P], cx[:, k * P:(k + 1) * P], ident[:])
                    ins.then_inc(cx_turned.sem, 1)
                if s >= UPT + PV + 2 and (s - UPT - PV - 2) % UPT == 0:
                    i = (s - UPT - PV - 2) // UPT
                    pe.wait_ge(cxT_ready.sem, cxT_ready.at(b, i + 1))
                    for k in range(KB):
                        ins = pe.matmul(ps[:, 5, D:2 * D], cxT[:, k], wo[:, k], start=(k == 0), stop=(k == KB - 1))
                    ins.then_inc(wo_done.sem, 1)

            def tile_out(i):
                return ps[:, 6 + i // 2, (i % 2) * D:(i % 2 + 1) * D]

            def turn_chain(b, n):
                pe.wait_ge(xc_ready.sem, xc_ready.at(b, n + 1))
                pe.wait_ge(xcT_ready.sem, xcT_ready.at(b, n))
                if n == 0:
                    pe.wait_ge(h4_ready.sem, h4_ready.at(b, 0))
                for k in range(KB):
                    for i in range(NT):
                        ins = pe.transpose(ps[:, 6 + k, i * P:(i + 1) * P], xc[:, i, k * P:(k + 1) * P], ident[:])
                ins.then_inc(xc_turned.sem, 1)

            def block_tile(i):
                for k in range(KB):
                    ins = pe.matmul(tile_out(i), xcT[:, k, i * P:(i + 1) * P], wb[:, k],
                                    start=(k == 0), stop=(k == KB - 1))
                return ins

            def up(b, f):
                if f == 1:
                    pe.wait_ge(logit_read.sem, logit_read.at(b, 1))
                pe.wait_ge(hid_ready.sem, hid_ready.at(b, max(f - 1, 0)))
                for k in range(KB):
                    ins = pe.matmul(ps[:, 6 + f % 2, 0:T], sw1[:, k, f * P:(f + 1) * P], xcT[:, k],
                                    start=(k == 0), stop=(k == KB - 1))
                ins.then_inc(up_done.sem, 1)

            def down(b, i):
                pe.wait_ge(hid_ready.sem, hid_ready.at(b, FB))
                for f in range(FB):
                    ins = pe.matmul(tile_out(i), hid[:, f, i * P:(i + 1) * P], sw2[:, f],
                                    start=(f == 0), stop=(f == FB - 1))
                if i == NT - 1:
                    ins.then_inc(down_done.sem, 1)

            def chain(b, s):
                if s in (TURN0, TURN1, TURN2):
                    turn_chain(b, (TURN0, TURN1, TURN2).index(s))
                if s == BLOCK:
                    pe.wait_ge(xcT_ready.sem, xcT_ready.at(b, 1))
                    for k in range(KB):
                        pe.matmul(ps[:, 7, 0:T], wr_bc[:, k], xcT[:, k], start=(k == 0), stop=(k == KB - 1))
                    block_tile(0)
                    block_tile(1).then_inc(block_done.sem, 1)
                if s == BLOCK + 2:
                    pe.wait_ge(block_ready.sem, block_ready.at(b, 1))
                    block_tile(2).then_inc(block_done.sem, 1)
                if s == TURN1 + 1:
                    pe.wait_ge(xcT_ready.sem, xcT_ready.at(b, 2))
                    for m in range(2):
                        for k in range(KB):
                            ins = pe.matmul(ps[:, 6 + m, 0:T], fb[:, k, m * P:(m + 1) * P], xcT[:, k],
                                            start=(k == 0), stop=(k == KB - 1))
                    ins.then_inc(u_done.sem, 1)
                if s == OUT:
                    pe.wait_ge(state_re.sem, state_re.at(b, 1))
                    pe.wait_ge(state_im.sem, state_im.at(b, 1))
                    for i in range(NT):
                        pe.matmul(tile_out(i), st[:, 0, i * P:(i + 1) * P], ce[:, 0], start=True, stop=False)
                        for k in range(KB):
                            pe.matmul(tile_out(i)[:, k * P:(k + 1) * P], xcT[:, k, i * P:(i + 1) * P], d_diag[:, k],
                                      start=False, stop=False)
                        ins = pe.matmul(tile_out(i), st[:, 1, i * P:(i + 1) * P], ce[:, 1], start=False, stop=True)
                    ins.then_inc(ssm_done.sem, 1)
                if s == TURN2 + 1:
                    pe.wait_ge(xcT_ready.sem, xcT_ready.at(b, 3))
                    for i in range(NT):
                        for k in range(KB):
                            ins = pe.matmul(ps[:, 7, i * NE:(i + 1) * NE], xcT[:, k, i * P:(i + 1) * P], rw[:, k],
                                            start=(k == 0), stop=(k == KB - 1))
                    ins.then_inc(logit_done.sem, 1)
                if UP <= s < UP + FB:
                    up(b, s - UP)

            def sequence(b, att, chained, head):
                for s in range(SLOTS):
                    if chained:
                        chain(b - 1, s)
                    if att:
                        unit(b, s)
                    if head and s == CONV:
                        convolution(b + 1)
                        turn_text(b + 1)
                    if head and s == CONV + 1:
                        text(b + 1)
                rest = range(SLOTS - UP, FB) if chained else ()
                if head:
                    turn_rows(b + 1)
                for f in rest[:1]:
                    up(b - 1, f)
                if head:
                    queries_and_keys(b + 1)
                    values(b + 1)
                for f in rest[1:]:
                    up(b - 1, f)
                if chained:
                    for i in range(NT):
                        down(b - 1, i)
                if head:
                    values_sum(b + 1)

            convolution(0)
            turn_text(0)
            text(0)
            turn_rows(0)
            queries_and_keys(0)
            values(0)
            values_sum(0)
            sequence(0, True, False, True)
            with pe.Fori(1, NB - 1) as b:
                sequence(b, True, True, True)
            sequence(NB - 1, True, True, False)
            sequence(NB, False, True, False)

            pe.wait_ge(route_loaded.sem, route_loaded.at(0, 48))
            pe.wait_ge(hot_ready.sem, hot_ready.at(0, 1))
            pe.matmul(ps[:, 0, 0:NE * TILES], ltri[:], hot2[:].rearrange("p e t -> p (e t)"), start=True, stop=True)
            pe.matmul(ps[:, 1, 0:NE * TILES], ones1[:], hot2[:].rearrange("p e t -> p (e t)"),
                      start=True, stop=True).then_inc(rank_done.sem, 1)
            pe.wait_ge(slots_loaded.sem, slots_loaded.at(0, 16))
            pe.transpose(ps[:, 7, 0:SLOT_TILES], slots_r[:], ident[0:SLOT_TILES, 0:SLOT_TILES]
                         ).then_inc(slots_turned.sem, 1)
            pe.wait_ge(pos_ready.sem, pos_ready.at(0, 1))

            def turn_chunk(j):
                pe.wait_ge(xg_loaded.sem, xg_loaded.at(j, 32))
                for k in range(KB):
                    for c in range(2):
                        ins = pe.transpose(ps[:, 6, (2 * k + c) * P:(2 * k + c + 1) * P],
                                           xg[:, c, k * P:(k + 1) * P], ident[:])
                ins.then_inc(xg_turned.sem, 1)

            def expert(q, half, e):
                lo, hi = expert_bounds(pe, e)
                with pe.Fori(lo, hi) as j:
                    pe.wait_ge(w_split.sem, w_split.at(2 * q, half + 1))
                    pe.wait_ge(xgT_ready.sem, xgT_ready.at(j, 1))
                    for f in range(FB):
                        pe.wait_ge(ehid_ready.sem, ehid_ready.at(j, max(f - 3, 0)))
                        cols = slice(f * P, (f + 1) * P)
                        terms = [(w, x, k) for w, x in ((w1_hi, xg_hi), (w1_hi, xg_lo), (w1_lo, xg_hi))
                                 for k in range(KB)]
                        for n, (w, x, k) in enumerate(terms):
                            ins = pe.matmul(ps[:, f % 4, 0:CHUNK], w[half][:, k, cols], x[:, k],
                                            start=(n == 0), stop=(n == len(terms) - 1))
                        ins.then_inc(eup_done.sem, 1)
                    turn_chunk(j + 1)
                    pe.wait_ge(y_ready.sem, y_ready.at(j, 0))
                    for c in range(2):
                        rows = slice(c * P, (c + 1) * P)
                        for f in range(FB):
                            if c == 0:
                                pe.wait_ge(elo_ready.sem, elo_ready.at(j, f + 1))
                            out = ps[:, 4 + c, 0:D]
                            pe.matmul(out, hid_hi[:, f, rows], w2_hi[half][:, f], start=(f == 0), stop=False)
                            pe.matmul(out, hid_hi[:, f, rows], w2_lo[half][:, f], start=False, stop=False)
                            ins = pe.matmul(out, hid_lo[:, f, rows], w2_hi[half][:, f], start=False, stop=(f == FB - 1))
                        ins.then_inc(edown_done.sem, 1)

            turn_chunk(0)
            with pe.Fori(0, NE // 2) as q:
                for half in range(2):
                    expert(q, half, 2 * q + half)



def layout(inputs):
    def blocks(w):
        w = np.asarray(w)
        return np.ascontiguousarray(w.reshape(w.shape[0] // P, P, -1).transpose(1, 0, 2))

    def col(v):
        return np.ascontiguousarray(np.asarray(v).reshape(-1, P).T)

    g = {k: np.asarray(v) for k, v in inputs.items()}
    a = {
        "x": g["x"], "ids": g["x_txt"].T, "U": g["L0_txt_U"], "s": g["L0_txt_s"].reshape(R, 1), "vt": g["L0_txt_Vt"],
        "scharr": g["L0_tok_scharr"].reshape(18), "scharr_dx": g["L0_tok_scharr"][:, 0].transpose(2, 0, 1),
        "wqT": blocks(g["L0_attn_Wq"].T), "wkT": blocks(g["L0_attn_Wk"].T), "wvT": blocks(g["L0_attn_Wv"].T),
        "woT": blocks(g["L0_attn_Wo"].T), "bq": col(g["L0_attn_bq"]), "bk": col(g["L0_attn_bk"]),
        "bv": g["L0_attn_bv"], "bo": g["L0_attn_bo"],
    }
    a |= {
        "wr": col(g["L0_ffn_w_router"]), "wb": blocks(g["L0_ffn_w_block"]), "a": g["L1_attn_a_params"].reshape(P, 1),
        "b_w": blocks(g["L1_attn_B_w"]), "c_wT": blocks(g["L1_attn_C_w"].T), "d": g["L1_attn_D"],
        "rwT": blocks(g["L1_ffn_router_w"].T), "rb": g["L1_ffn_router_b"],
        "sw1": blocks(g["L1_ffn_shared_w1"].T), "sw2": blocks(g["L1_ffn_shared_w2"].T),
        "sb1": col(g["L1_ffn_shared_b1"]), "sb2": g["L1_ffn_shared_b2"],
    }
    a |= {
        "w1": np.stack([blocks(w.T) for w in g["L1_ffn_spec_w1"]]), "w2": np.stack([blocks(w.T) for w in g["L1_ffn_spec_w2"]]),
        "b1": np.stack([col(v) for v in g["L1_ffn_spec_b1"]]), "b2": g["L1_ffn_spec_b2"],
    }
    r = np.arange(P)
    c = np.arange(2 * P)
    a["ident"] = np.eye(P, dtype=np.float32)
    a["mask"] = np.where((c[None] <= r[:, None] + P) & (c[None] >= r[:, None]), 0, MASKED).astype(np.float32)
    a["shift"] = np.stack([r[:, None] - r[None] == dy - 1 for dy in range(3)], 1).astype(np.float32)
    a["ltri"] = (r[:, None] < r[None]).astype(np.float32)
    a["ramp"] = (np.arange(RAMP) * CHUNK).astype(np.float32)
    a["tok"] = (np.arange(TILES)[None] * P + r[:, None]).astype(np.float32)
    j = np.arange(T)
    own = np.arange(NT)[:, None] * P + r[:, None, None]
    a["rank_cols"] = j.astype(np.float32)
    a["rank_own"] = own[:, :, 0].astype(np.float32)
    n = np.arange(D)
    angle = 2 * np.pi * np.outer(n, r) / D
    re, im = np.cos(angle), -np.sin(angle)
    im[:, 0] = (-1.0) ** n
    a["dft"] = blocks(np.concatenate([re, im], 1).astype(np.float32))
    scale = np.where(r == 0, 1.0, 2.0) / D
    a["idft"] = blocks(np.concatenate([re * scale, im * scale], 1).astype(np.float32))
    sines = -2 * np.sin(2 * np.pi * np.outer(r + 1, r) / D)
    sines[P - 1] = 0
    sines[:, 0] = 0
    a["sines"] = sines.astype(np.float32)
    return {k: np.ascontiguousarray(v) for k, v in a.items()}


def kernel(**inputs):
    import concourse.bacc as bacc
    from concourse.bass_utils import run_bass_kernel_spmd

    arrays = layout(inputs)
    nc = bacc.Bacc("TRN2", target_bir_lowering=False, num_devices=1)
    t = {k: nc.dram_tensor("in_" + k, v.shape, mybir.dt.from_np(v.dtype), kind="ExternalInput").ap()
         for k, v in arrays.items()}
    t["out"] = nc.dram_tensor("result", (NB, T, D), F32, kind="ExternalOutput").ap().rearrange("b t d -> (b t) d")
    build(nc, t)
    return run_bass_kernel_spmd(nc, [{"in_" + k: v for k, v in arrays.items()}], core_ids=[0]).results[0]["result"]
```

```python
from contextlib import ExitStack

import numpy as np
import concourse.bass as bass
from concourse import mybir

F32 = mybir.dt.float32
F32R = mybir.dt.float32r
BF16 = mybir.dt.bfloat16
I32 = mybir.dt.int32
U32 = mybir.dt.uint32
ALU = mybir.AluOpType
ACT = mybir.ActivationFunctionType
AX_X = mybir.AxisListType.X

P = 128
NB = 16
IMG = 256
D = 256
KB = D // P
NT = 3
T = NT * P
R = 64
NH, DK = 16, 16
SCALE = 0.25
MASKED = -30000.0
GRAY = (0.2989, 0.587, 0.114)
KEEP = 288
F = 1024
FB = F // P
NE = 8
EPS = 1e-5
TILES = NB * NT
CHUNK = 2 * P
CHUNKS = NB * T * 2 // CHUNK + NE
SLOT_TILES = 2 * (CHUNKS + 2)
RAMP = NB * T // CHUNK
RING = 4
COMB = 4
HG = 2
NU = NT * NH // HG


PAIRS = P // (HG * DK)
UPT = NH // HG
PB = 4
TURN, PV = 2, 3
SLOTS = NU + PV + 4
TURN0, BLOCK, RANK = 1, 3, 5
TURN1, STATE, OUT = 14, 16, 20
TURN2, GRAY_AT, CONV, UP = 24, 19, 25, 27
NEWTON = 3
GUESS = 0x5F3759DF - 2 ** 30 - 2 ** 22
LN_STEPS = 1 + 4 * NEWTON
CHAIN_STEPS = 15


class Signal:

    def __init__(self, sem, per, start):
        self.sem, self.per, self.start, self.steps = sem, per, start, 0

    def at(self, b, n):
        return b * self.per + (n + self.start)


def build(nc, t):
    with ExitStack() as ctx:
        def sb(name, shape, dt=F32):
            return ctx.enter_context(nc.sbuf_tensor(name, shape, dt))

        signals = []

        def signal(name, per):
            signals.append(Signal(ctx.enter_context(nc.semaphore(name)), per, 1))
            return signals[-1]

        def dma_signal(name, per):
            return Signal(ctx.enter_context(nc.semaphore(name)), per, 0)

        ps = ctx.enter_context(nc.psum_tensor("ps", [P, 8, 512], F32))

        ident = sb("ident", [P, P])
        ident_bf = sb("ident_bf", [P, P], BF16)
        mask_bf = sb("mask_bf", [P, 2, 2 * P], BF16)
        ones9 = sb("ones9", [P, P])
        tap = sb("tap", [P, 18])
        tap_edge = sb("tap_edge", [3, 2, 3])
        band = sb("band", [P, 2, 3, P])
        band_edge = sb("band_edge", [3, 2, 2, P])
        wq = sb("wq", [P, KB, D])
        wk = sb("wk", [P, KB, D])
        wv = sb("wv", [P, KB, D])
        wo = sb("wo", [P, KB, D])
        bq = sb("bq", [P, KB])
        bk = sb("bk", [P, KB])
        bv_row = sb("bv_row", [P, D])
        bo_row = sb("bo_row", [P, D])
        vt = sb("vt", [R, D])
        s_col = sb("s_col", [R, 1])
        ids = sb("ids", [P, NB], I32)
        u_all = sb("u_all", [P, NB, R])

        spare = sb("spare", [P, 1])
        c15 = sb("c15", [P, NT])
        zeros = sb("zeros", [SLOT_TILES, P])
        wr_col = sb("wr_col", [P, KB])
        wr_bc = sb("wr_bc", [P, KB, P])
        wb = sb("wb", [P, KB, D])
        rank_cols = sb("rank_cols", [P, T])
        rank_own = sb("rank_own", [P, NT])
        before = sb("before", [P, NT, T], BF16)
        after = sb("after", [P, NT, T], BF16)
        sines = sb("sines", [P, P])
        a_col = sb("a_col", [P, 1])
        d_row = sb("d_row", [P, D])
        fb = sb("fb", [P, KB, D])
        ce = sb("ce", [P, 2, D])
        turn = sb("turn", [P, 2, T])
        om = sb("om", [P, 8])
        ones_t = sb("ones_t", [P, T])
        rw = sb("rw", [P, KB, NE])
        rb_row = sb("rb_row", [P, NE])
        sw1 = sb("sw1", [P, KB, F])
        sw2 = sb("sw2", [P, FB, D])
        sb1 = sb("sb1", [P, FB])
        sb2_row = sb("sb2_row", [P, D])
        top_v = sb("top_v", [P, NB, NT, 2])
        top_i = sb("top_i", [P, NB, NT, 2])

        space = ctx.enter_context(ExitStack())

        def room(name, shape, dt=F32):
            return space.enter_context(nc.sbuf_tensor(name, shape, dt))

        xin = room("xin", [P, 2, 3, IMG])
        gsum = room("gsum", [P, 2, IMG])
        gray = room("gray", [P, 2, IMG + 2])
        halo = room("halo", [3, 2, IMG])
        edges = room("edges", [P, 2, 2 * IMG])
        ub = room("ub", [P, P])
        usT = room("usT", [R, P])
        h = room("h", [P, NT, D])
        hbo = room("hbo", [P, NT, D])
        ln = room("ln", [P, 48])
        xn = room("xn", [P, NT, D])
        xT = room("xT", [P, KB, T])
        q_full = room("q_full", [P, KB, T])
        q_hi = room("q_hi", [P, KB, T], F32R)
        q_lo = room("q_lo", [P, KB, T], F32R)
        k_hi = room("k_hi", [P, KB, T], F32R)
        k_lo = room("k_lo", [P, KB, T], F32R)
        qs = room("qs", [3 * HG * DK, PAIRS, KB, T], F32R)
        ks = room("ks", [3 * HG * DK, PAIRS, KB, HG, T], F32R)
        vaug = room("vaug", [P, NT, NH, DK + 1])
        sumv = room("sumv", [P, D])
        mx = room("mx", [P, 2, HG])
        prob = room("prob", [P, PB, HG, 2 * P])
        pT = room("pT", [P, 2, HG, 2, P])
        rden = room("rden", [P, NH])
        cx = room("cx", [P, D])
        cxT = room("cxT", [P, KB, P])
        h1 = room("h1", [P, NT, D])
        hc = room("hc", [P, NT, D])
        lnc = room("lnc", [P, 48])
        xc = room("xc", [P, NT, D])
        xcT = room("xcT", [P, KB, T])
        srow = room("srow", [P, T])
        own = room("own", [P, NT])
        count = room("count", [P, 2, NT])
        sel = room("sel", [P, NT])
        g = room("g", [P, NT, D])
        rot = room("rot", [P, 4, T])
        cum = room("cum", [P, 2, T])
        st = room("st", [P, 2, T])
        logit = room("logit", [P, NT, NE])
        v8 = room("v8", [P, NT, NE])
        i8 = room("i8", [P, NT, NE], U32)
        hb2 = room("hb2", [P, NT, D])
        hid = room("hid", [P, FB, T])
        place = hid[:].rearrange("p f t -> p (f t)")
        mats = place[:, 0:4 * KB * D].rearrange("p (n k d) -> p n k d", n=4, k=KB)
        dft, idft, b_w, c_wT = (mats[:, n] for n in range(4))
        place = place[:, 4 * KB * D:]
        shift = place[:, 0:3 * P].rearrange("p (n q) -> p n q", n=3)
        mask_f = place[:, 3 * P:5 * P]
        h4 = room("h4", [P, NT, D])
        space.close()

        with ExitStack() as space:
            def room(name, shape, dt=F32):
                return space.enter_context(nc.sbuf_tensor(name, shape, dt))

            ltri = room("ltri", [P, P])
            ones1 = room("ones1", [P, P])
            seg = room("seg", [P, NE, TILES])
            ramp = room("ramp", [P, RAMP])
            tok = room("tok", [P, TILES])
            gates = room("gates", [P, 4, TILES])
            hot = room("hot", [P, 2, NE, TILES])
            hot2 = room("hot2", [P, NE, TILES])
            tot = room("tot", [P, NE, TILES])
            incl = room("incl", [P, NE, TILES])
            pos = room("pos", [P, NE, TILES])
            picked = room("picked", [P, 2, NE, TILES])
            pos_f = room("pos_f", [P, 2, TILES])
            pos_i = room("pos_i", [P, 2, TILES], I32)
            over = room("over", [P, NE, RAMP])
            chunks = room("chunks", [P, 3, NE])
            bounds = room("bounds", [P, NE + 1], I32)
            place_i = room("place_i", [P, 2, 2, TILES], I32)
            place = room("place", [P, 2, 2, TILES])
            place_s = room("place_s", [P, RING])
            slots_i = room("slots_i", [P, SLOT_TILES], I32)
            idx_s = room("idx_s", [P, 2], I32)
            xg = room("xg", [P, 2, D])
            xg_hi = room("xg_hi", [P, KB, 2 * P], F32R)
            xg_lo = room("xg_lo", [P, KB, 2 * P], F32R)
            w1_raw = room("w1_raw", [P, KB, F])
            w2_raw = room("w2_raw", [P, FB, D])
            w1_hi = [room(f"w1_hi{j}", [P, KB, F], F32R) for j in range(2)]
            w1_lo = [room(f"w1_lo{j}", [P, KB, F], F32R) for j in range(2)]
            w2_hi = [room(f"w2_hi{j}", [P, FB, D], F32R) for j in range(2)]
            w2_lo = [room(f"w2_lo{j}", [P, FB, D], F32R) for j in range(2)]
            b1 = [room(f"b1_{j}", [P, FB]) for j in range(2)]
            b2_row = [room(f"b2_row{j}", [P, D]) for j in range(2)]
            hid_full = room("hid_full", [P, 4, CHUNK])
            hid_hi = room("hid_hi", [P, FB, CHUNK], F32R)
            hid_lo = room("hid_lo", [P, FB, CHUNK], F32R)
            yb = room("yb", [P, 2, D])
            pos_g = room("pos_g", [P, 2, 2, COMB], I32)
            yg = [w1_raw[:].rearrange("p k (c d) -> p k c d", d=D),
                  w2_raw[:].rearrange("p (k c) d -> p k c d", k=2)]
            part = hid_full[:]
            res2 = room("res2", [P, 2, COMB, D])
            hsum2 = room("hsum2", [P, 2, COMB, D])
            res = [res2[:, j] for j in range(2)]
            hsum = [hsum2[:, j] for j in range(2)]
            place_row = hid_full[:].rearrange("p n (k q) -> p n k q", k=2)
            place_col = hsum[0][:, :, 0:2 * SLOT_TILES].rearrange("p n (k s) -> p n k s", k=2)

        h4_dram = nc.dram_tensor("h4_rows", (NB * T, D), F32, kind="Internal").ap()
        y_dram = nc.dram_tensor("y_rows", ((CHUNKS + 1) * CHUNK, D), F32, kind="Internal").ap()
        xn_dram = nc.dram_tensor("xn_rows", (NB * T, D), F32, kind="Internal").ap()

        zeros_ready = signal("zeros_ready", 0)
        mats_done = signal("mats_done", 0)
        mats_read = signal("mats_read", 0)
        loaded = dma_signal("weights_loaded", 0)
        late_loaded = dma_signal("late_weights_loaded", 0)
        set_up = signal("constants_ready", 0)
        setup_step = signal("setup_step", 0)
        ids_loaded = dma_signal("ids_loaded", 0)
        u_gathered = dma_signal("u_gathered", 0)
        x_loaded = dma_signal("x_loaded", 32)
        gray_ready = signal("gray_ready", 1)
        halo_loaded = dma_signal("halo_loaded", 96)
        conv_done = signal("conv_done", 2)
        abs_done = signal("abs_done", 2)
        h_ready = signal("h_ready", 1)
        ub_ready = signal("ub_ready", 1)
        uT_ready = signal("uT_ready", 1)
        usT_ready = signal("usT_ready", 1)
        text_done = signal("text_done", 1)
        xn_ready = signal("xn_ready", 1)
        xT_turned = signal("xT_turned", 1)
        xT_ready = signal("xT_ready", 1)
        proj_done = signal("proj_done", 3)
        q_ready = signal("q_ready", 1)
        k_ready = signal("k_ready", 1)
        parts_ready = signal("parts_ready", 1)
        stacked = [dma_signal(f"stacked{g}", 16 * 3 * (1 + HG)) for g in range(PAIRS)]
        v_ready = signal("v_ready", 1)
        sumv_done = signal("sumv_done", 1)
        sumv_ready = signal("sumv_ready", 1)
        hbo_ready = signal("hbo_ready", 1)
        head_step = signal("head_step", 3)
        head_stats_ready = signal("head_stats_ready", 1)
        head_rstd_ready = signal("head_rstd_ready", 1)
        head_pool_step = signal("head_pool_step", LN_STEPS)
        scores_done = signal("scores_done", NU)
        sub_done = signal("sub_done", NU)
        exp_done = signal("exp_done", NU)
        turned = signal("probs_turned", NU)
        pT_ready = signal("pT_ready", NU)
        pv_done = signal("pv_done", NU)
        pv_read = signal("pv_read", NT)
        cx_ready = signal("cx_ready", NT)
        cx_turned = signal("cx_turned", NT)
        cxT_ready = signal("cxT_ready", NT)
        wo_done = signal("wo_done", NT)
        h1_ready = signal("h1_ready", NT)
        att_step = signal("attention_step", NU + NT)
        xc_ready = signal("xc_ready", 3)
        xc_turned = signal("xc_turned", 3)
        xcT_ready = signal("xcT_ready", 3)
        block_done = signal("block_done", 2)
        block_ready = signal("block_ready", 2)
        u_done = signal("u_done", 1)
        u_read = signal("u_read", 1)
        cum_ready = signal("cum_ready", 1)
        rot2_step = signal("rot2_step", 1)
        direct_step = signal("direct_step", 1)
        direct_ready = signal("direct_ready", 1)
        state_re = signal("state_re_ready", 1)
        state_im = signal("state_im_ready", 1)
        ssm_done = signal("ssm_done", 1)
        h3_ready = signal("h3_ready", 1)
        xn_stored = dma_signal("xn_stored", 16)
        logit_done = signal("logit_done", 1)
        logit_read = signal("logit_read", 1)
        stats_ready = signal("stats_ready", 3)
        rstd_ready = signal("rstd_ready", 3)
        chain_pool_step = signal("chain_pool_step", 3 * LN_STEPS)
        chain_step = signal("chain_step", CHAIN_STEPS)
        hb2_ready = signal("hb2_ready", 1)
        up_done = signal("up_done", FB)
        hid_ready = signal("hid_ready", FB)
        down_done = signal("down_done", 1)
        h4_ready = signal("h4_ready", 1)
        h4_stored = dma_signal("h4_stored", 16)
        h4_sent = signal("h4_sent", 1)
        route_loaded = dma_signal("route_loaded", 0)
        diff_ready = signal("diff_ready", 0)
        ratio_ready = signal("ratio_ready", 0)
        hot_ready = signal("hot_ready", 0)
        rank_done = signal("rank_done", 0)
        route_step = signal("route_step", 0)
        bounds_ready = signal("bounds_ready", 0)
        pos_ready = signal("pos_ready", 0)
        place_free = [signal(f"place_free{j}", 1) for j in range(RING)]
        place_copied = signal("place_copied", 1)
        row_ready = signal("place_row_ready", 1)
        col_ready = signal("place_col_ready", 1)
        slots_summed = signal("slots_summed", 0)
        slots_ready = signal("slots_ready", 0)
        w_loaded = dma_signal("w_loaded", 32)
        b_loaded = [dma_signal(f"b_loaded{j}", 32) for j in range(2)]
        hi_ready = signal("rounded_weights_ready", 1)
        w_split = signal("weights_split", 1)
        xg_rounded = signal("xg_rounded", 1)
        elo_ready = signal("expert_lo_ready", FB)
        pool_go = signal("pool_go", 0)
        gather_go = signal("gather_go", 1)
        idx_ready = signal("idx_ready", 1)
        xg_loaded = dma_signal("xg_loaded", 32)
        xg_turned = signal("xg_turned", 1)
        xgT_ready = signal("xgT_ready", 1)
        eup_done = signal("expert_up_done", FB)
        ehid_ready = signal("expert_hid_ready", FB)
        edown_done = signal("expert_down_done", 2)
        y_ready = signal("y_ready", 2)
        y_stored = dma_signal("y_stored", 16)
        y_sent = signal("y_sent", 1)
        pos_g_ready = signal("pos_g_ready", 1)
        y_complete = signal("y_complete", 1)
        hsum_loaded = [dma_signal(f"hsum_loaded{j}", 16) for j in range(2)]
        yg_loaded = [dma_signal(f"yg_loaded{j}", 32 * COMB) for j in range(2)]
        yg_read = [signal(f"yg_read{j}", 1) for j in range(2)]
        part_ready = signal("part_ready", 1)
        res_ready = [signal(f"res_ready{j}", 1) for j in range(2)]
        res_sent = [signal(f"res_sent{j}", 1) for j in range(2)]
        stored = [dma_signal(f"stored{j}", 16) for j in range(2)]

        block = ctx.enter_context(nc.Block())

        weight_loads = [
            (ident, t["ident"]), (mask_f, t["mask"]), (shift, t["shift"]),
            (tap, t["scharr"].partition_broadcast(P)), (tap_edge, t["scharr_dx"]),
            (dft, t["dft"]), (idft, t["idft"]), (sines, t["sines"]), (a_col, t["a"]), (b_w, t["b_w"]),
            (c_wT, t["c_wT"]), (vt, t["vt"]), (s_col, t["s"]),
            (wq, t["wqT"]), (wk, t["wkT"]), (wv, t["wvT"]), (wo, t["woT"]), (bq, t["bq"]), (bk, t["bk"]),
            (bv_row, t["bv"].partition_broadcast(P)), (bo_row, t["bo"].partition_broadcast(P)),
            (wr_col, t["wr"]), (rank_cols, t["rank_cols"].partition_broadcast(P)), (rank_own, t["rank_own"]),
        ]
        NLOAD = 16 * len(weight_loads)
        late_loads = [
            (wb, t["wb"]), (d_row, t["d"].partition_broadcast(P)), (rw, t["rwT"]),
            (rb_row, t["rb"].partition_broadcast(P)), (sw1, t["sw1"]), (sw2, t["sw2"]), (sb1, t["sb1"]),
            (sb2_row, t["sb2"].partition_broadcast(P)),
        ]
        NLATE = 16 * len(late_loads)
        NSET = 6

        def expert_bounds(eng, e):
            lo = eng.value_load(bounds[0:1, bass.ds(e, 1)], min_val=0, max_val=CHUNKS - 1)
            hi = eng.value_load(bounds[0:1, bass.ds(e + 1, 1)], min_val=1, max_val=CHUNKS)
            return lo, hi

        @block.sync
        def _(sp):
            sp.dma_start(ids[:], t["ids"]).then_inc(ids_loaded.sem, 16)
            for dst, src in weight_loads:
                sp.dma_start(dst[:], src).then_inc(loaded.sem, 16)
            def load_image(b):
                sp.wait_ge(gray_ready.sem, gray_ready.at(b, 0))
                for rt in range(2):
                    src = t["x"][bass.ds(b, 1), :, rt * P:(rt + 1) * P, :].rearrange("o c p w -> p (o c) w")
                    sp.dma_start(xin[:, rt], src).then_inc(x_loaded.sem, 16)

            def load_halo(b):
                sp.wait_ge(gray_ready.sem, gray_ready.at(b, 1))
                sp.wait_ge(conv_done.sem, conv_done.at(b, 0))
                for dx in range(3):
                    sp.dma_start(halo[dx:dx + 1, 0, :], gray[0:1, 1, dx:dx + IMG]).then_inc(halo_loaded.sem, 16)
                    sp.dma_start(halo[dx:dx + 1, 1, :], gray[P - 1:P, 0, dx:dx + IMG]).then_inc(halo_loaded.sem, 16)

            def store_rows(b):
                sp.wait_ge(xc_ready.sem, xc_ready.at(b, 3))
                rows = xn_dram.rearrange("(b i p) d -> b p i d", b=NB, i=NT)
                sp.dma_start(rows[bass.ds(b, 1)].rearrange("o p i d -> p (o i) d"), xc[:]).then_inc(xn_stored.sem, 16)

            def store_h4(b):
                sp.wait_ge(h4_ready.sem, h4_ready.at(b, 1))
                rows = h4_dram.rearrange("(b i p) d -> b p i d", b=NB, i=NT)
                sp.dma_start(rows[bass.ds(b, 1)].rearrange("o p i d -> p (o i) d"), h4[:]).then_inc(h4_stored.sem, 16)
                sp.wait_ge(h4_stored.sem, h4_stored.at(b, 16))
                sp.sem_inc(h4_sent.sem, 1)

            def stack(b):
                def put(g, n, q, k):
                    if q is not None:
                        sp.dma_start(qs[2 * DK * n:2 * DK * (n + 1), g].bitcast(F32),
                                     q[2 * DK * g:2 * DK * (g + 1)].bitcast(F32)).then_inc(stacked[g].sem, 16)
                    for j in range(HG if k is not None else 0):
                        r = DK * (HG * g + j)
                        sp.dma_start(ks[DK * (HG * n + j):DK * (HG * n + j + 1), g, :, j].bitcast(F32),
                                     k[r:r + DK].bitcast(F32)).then_inc(stacked[g].sem, 16)

                sp.wait_ge(q_ready.sem, q_ready.at(b, 1))
                sp.wait_ge(zeros_ready.sem, zeros_ready.at(0, 1))
                for g in range(PAIRS):
                    put(g, 0, q_hi, None)
                    put(g, 2, q_hi, None)
                sp.wait_ge(parts_ready.sem, parts_ready.at(b, 1))
                for g in range(PAIRS):
                    put(g, 0, None, k_hi)
                    put(g, 1, q_lo, k_hi)
                    put(g, 2, None, k_lo)

            def sequence(b, chain, head):
                if head:
                    load_image(b + 1)
                    load_halo(b + 1)
                if chain:
                    store_rows(b - 1)
                if head:
                    stack(b + 1)
                if chain:
                    store_h4(b - 1)

            load_image(0)
            for dst, src in late_loads:
                sp.dma_start(dst[:], src).then_inc(late_loaded.sem, 16)
            load_halo(0)
            stack(0)
            sequence(0, False, True)
            with sp.Fori(1, NB - 1) as b:
                sequence(b, True, True)
            sequence(NB - 1, True, False)
            sequence(NB, True, False)

            sp.wait_ge(h4_sent.sem, h4_sent.at(NB, 0))
            for dst, src in ((ltri, t["ltri"]), (ramp, t["ramp"].partition_broadcast(P)), (tok, t["tok"])):
                sp.dma_start(dst[:], src).then_inc(route_loaded.sem, 16)

            def load_weights(e):
                for dst, src in ((w1_raw, t["w1"]), (w2_raw, t["w2"])):
                    sp.dma_start(dst[:], src[bass.ds(e, 1)].rearrange("o p k n -> (o p) k n")
                                 ).then_inc(w_loaded.sem, 16)

            def load_biases(half, e):
                sp.dma_start(b1[half][:], t["b1"][bass.ds(e, 1)].rearrange("o p n -> (o p) n")
                             ).then_inc(b_loaded[half].sem, 16)
                sp.dma_start(b2_row[half][:], t["b2"][bass.ds(e, 1)].to_broadcast([P, D])
                             ).then_inc(b_loaded[half].sem, 16)

            load_weights(0)
            for half in range(2):
                load_biases(half, half)
            sp.wait_ge(w_split.sem, w_split.at(0, 1))
            load_weights(1)
            sp.wait_ge(bounds_ready.sem, bounds_ready.at(0, 1))

            def store_chunk(j):
                sp.dma_start(y_dram.rearrange("(j c p) d -> j p c d", c=2, p=P)[bass.ds(j, 1)]
                             .rearrange("o p c d -> p (o c) d"), yb[:]).then_inc(y_stored.sem, 16)
                sp.wait_ge(y_stored.sem, y_stored.at(j, 16))
                sp.sem_inc(y_sent.sem, 1)

            def store_chunks(e):
                lo, hi = expert_bounds(sp, e)
                with sp.Fori(lo, hi) as j:
                    sp.wait_ge(y_ready.sem, y_ready.at(j, 2))
                    store_chunk(j)

            with sp.Fori(0, NE // 2 - 1) as q:
                for half in range(2):
                    e = 2 * q + half
                    sp.wait_ge(w_split.sem, w_split.at(2 * q, half + 2))
                    load_weights(2 * q + (2 + half))
                    store_chunks(e)
                    load_biases(half, 2 * q + (2 + half))
            for half in range(2):
                store_chunks(NE - 2 + half)
            total = sp.value_load(bounds[0:1, NE:NE + 1], min_val=NE, max_val=CHUNKS)
            with sp.Fori(total, CHUNKS + 1) as j:
                sp.dma_start(y_dram.rearrange("(j c p) d -> j p c d", c=2, p=P)[bass.ds(j, 1)]
                             .rearrange("o p c d -> p (o c) d"), yb[:]).then_inc(y_stored.sem, 16)
            sp.wait_ge(y_stored.sem, y_stored.at(CHUNKS, 16))
            sp.sem_inc(y_complete.sem, 1)
            with sp.Fori(0, TILES // COMB // 2) as q:
                for half in range(2):
                    c = 2 * q + half
                    sp.wait_ge(yg_read[half].sem, yg_read[half].at(q, 0))
                    rows = h4_dram.rearrange("(c i p) d -> c p i d", i=COMB, p=P)
                    sp.dma_start(hsum[half], rows[bass.ds(c, 1)].rearrange("o p i d -> p (o i) d")
                                 ).then_inc(hsum_loaded[half].sem, 16)
                for half in range(2):
                    c = 2 * q + half
                    sp.wait_ge(res_ready[half].sem, res_ready[half].at(q, 1))
                    sp.dma_start(t["out"].rearrange("(c i p) d -> c p i d", i=COMB, p=P)[bass.ds(c, 1)]
                                 .rearrange("o p i d -> p (o i) d"), res[half]).then_inc(stored[half].sem, 16)
                for half in range(2):
                    sp.wait_ge(stored[half].sem, stored[half].at(q, 16))
                    sp.sem_inc(res_sent[half].sem, 1)

        @block.gpsimd
        def _(pool):
            for sig in signals:
                pool.sem_inc(sig.sem, 1)
            pool.memset(ks[:].bitcast(F32), 0.0)
            pool.memset(zeros[:], 0.0).then_inc(zeros_ready.sem, 1)
            pool.wait_ge(ids_loaded.sem, ids_loaded.at(0, 16))
            for b in range(NB):
                pool.indirect_dma_start(u_all[:, b, :], None, t["U"],
                                        bass.IndirectOffsetOnAxis(ids[:, b:b + 1], axis=0)
                                        ).then_inc(u_gathered.sem, 16)
            pool.wait_ge(loaded.sem, loaded.at(0, NLOAD))

            def link(ins, steps, b):
                steps.steps += 1
                ins.then_inc(steps.sem, 1)
                pool.wait_ge(steps.sem, steps.at(b, steps.steps))

            def residual(b):
                pool.wait_ge(h_ready.sem, h_ready.at(b, 1))
                pool.wait_ge(h1_ready.sem, h1_ready.at(b, 0))
                for i in range(NT):
                    ins = pool.tensor_tensor(hbo[:, i], h[:, i], bo_row[:], ALU.add)
                ins.then_inc(hbo_ready.sem, 1)

            def deviations(w, ready, done, steps, b, n):
                mean = w[:, 18:24].rearrange("p (i s) -> p i s", s=2)
                v, y, z = w[:, 24:27], w[:, 27:30], w[:, 30:33]
                pool.wait_ge(ready.sem, ready.at(b, n + 1))
                pool.sem_inc(pool_go.sem, 1)
                link(pool.tensor_scalar(v, mean[:, :, 1], EPS, -0.5, ALU.add, ALU.mult), steps, b)
                pool.sem_inc(pool_go.sem, 1)
                link(pool.tensor_scalar(y.bitcast(I32), v.bitcast(I32), -0.5, float(GUESS), ALU.mult, ALU.add),
                     steps, b)
                for k in range(NEWTON):
                    link(pool.tensor_tensor(z, y, y, ALU.mult), steps, b)
                    link(pool.tensor_tensor(z, z, v, ALU.mult), steps, b)
                    link(pool.tensor_tensor(z, z, c15[:], ALU.add), steps, b)
                    if k < NEWTON - 1:
                        link(pool.tensor_tensor(y, y, z, ALU.mult), steps, b)
                pool.tensor_tensor(y, y, z, ALU.mult).then_inc(done.sem, 1)

            def chain_deviations(b, n):
                if n == 0:
                    chain_pool_step.steps = 0
                deviations(lnc, stats_ready, rstd_ready, chain_pool_step, b, n)

            def head_deviations(b):
                head_pool_step.steps = 0
                deviations(ln, head_stats_ready, head_rstd_ready, head_pool_step, b, 0)

            def states(b):
                pool.wait_ge(cum_ready.sem, cum_ready.at(b, 1))
                pool.tensor_tensor(rot[:, 2], cum[:, 0], turn[:, 1], ALU.mult)
                pool.tensor_tensor(rot[:, 3], cum[:, 1], turn[:, 0], ALU.mult).then_inc(rot2_step.sem, 1)
                pool.wait_ge(rot2_step.sem, rot2_step.at(b, 1))
                pool.wait_ge(ssm_done.sem, ssm_done.at(b, 0))
                pool.tensor_tensor(st[:, 1], rot[:, 2], rot[:, 3], ALU.add).then_inc(state_im.sem, 1)

            def direct_term(b):
                pool.wait_ge(xc_ready.sem, xc_ready.at(b, 2))
                for i in range(NT):
                    ins = pool.tensor_tensor(g[:, i], xc[:, i], d_row[:], ALU.mult)
                ins.then_inc(direct_step.sem, 1)
                pool.wait_ge(direct_step.sem, direct_step.at(b, 1))
                pool.tensor_tensor(hc[:], hc[:], g[:], ALU.add).then_inc(direct_ready.sem, 1)

            def shared_residual(b):
                pool.wait_ge(h3_ready.sem, h3_ready.at(b, 1))
                pool.wait_ge(h4_ready.sem, h4_ready.at(b, 0))
                for i in range(NT):
                    ins = pool.tensor_tensor(hb2[:, i], hc[:, i], sb2_row[:], ALU.add)
                ins.then_inc(hb2_ready.sem, 1)

            def sequence(b, att, chain, head):
                if chain:
                    chain_deviations(b - 1, 1)
                    direct_term(b - 1)
                    states(b - 1)
                    chain_deviations(b - 1, 2)
                    shared_residual(b - 1)
                if head:
                    head_deviations(b + 1)
                    residual(b + 1)
                if att:
                    chain_deviations(b, 0)

            head_deviations(0)
            residual(0)
            sequence(0, True, False, True)
            pool.wait_ge(late_loaded.sem, late_loaded.at(0, NLATE))
            with pool.Fori(1, NB - 1) as b:
                sequence(b, True, True, True)
            sequence(NB - 1, True, True, False)
            sequence(NB, False, True, False)

            pool.wait_ge(pos_ready.sem, pos_ready.at(0, 1))
            with pool.Fori(0, TILES // RING) as q:
                for r in range(RING):
                    pool.wait_ge(place_free[r].sem, place_free[r].at(q, 0))
                    pool.tensor_copy(place_s[:, r:r + 1], place[:, 0, 1, bass.ds(RING * q + r, 1)]
                                     ).then_inc(place_copied.sem, 1)
                    pool.wait_ge(place_copied.sem, place_copied.at(RING * q, r + 1))
                    pool.sem_inc(pool_go.sem, 1)
                    pool.tensor_scalar(place_row[:, r, 1], rank_cols[:, 0:P], place_s[:, r:r + 1], None, ALU.is_equal
                                       ).then_inc(row_ready.sem, 1)
            def split_weights(half, e, off):
                pool.wait_ge(hi_ready.sem, hi_ready.at(e, off + 1))
                pool.tensor_tensor(w1_lo[half][:], w1_raw[:], w1_hi[half][:], ALU.subtract)
                pool.tensor_tensor(w2_lo[half][:], w2_raw[:], w2_hi[half][:], ALU.subtract).then_inc(w_split.sem, 1)

            def gather_rows(j, n):
                pool.wait_ge(xg_turned.sem, xg_turned.at(j, n))
                pool.tensor_copy(idx_s[:], slots_i[:, bass.ds(2 * (j + n), 2)]).then_inc(idx_ready.sem, 1)
                pool.wait_ge(idx_ready.sem, idx_ready.at(j, n + 1))
                pool.sem_inc(gather_go.sem, 1)
                for k in range(2):
                    pool.indirect_dma_start(xg[:, k], None, xn_dram,
                                            bass.IndirectOffsetOnAxis(idx_s[:, k:k + 1], axis=0)
                                            ).then_inc(xg_loaded.sem, 16)

            pool.wait_ge(slots_ready.sem, slots_ready.at(0, 1))
            pool.wait_ge(xn_stored.sem, xn_stored.at(NB - 1, 16))
            gather_rows(0, 0)
            gather_rows(0, 1)
            split_weights(1, 0, 1)

            def rows_ahead(e):
                lo, hi = expert_bounds(pool, e)
                with pool.Fori(lo, hi) as j:
                    gather_rows(j, 2)

            with pool.Fori(0, NE // 2 - 1) as q:
                for half in range(2):
                    rows_ahead(2 * q + half)
                    split_weights(half, 2 * q, 2 + half)
            for half in range(2):
                rows_ahead(NE - 2 + half)
            pool.wait_ge(y_complete.sem, y_complete.at(0, 1))
            with pool.Fori(0, TILES // COMB // 2) as q:
                for half in range(2):
                    c = 2 * q + half
                    pool.wait_ge(yg_read[half].sem, yg_read[half].at(q, 0))
                    pool.tensor_copy(pos_g[:, half], pos_i[:, :, bass.ds(c * COMB, COMB)]
                                     ).then_inc(pos_g_ready.sem, 1)
                    pool.wait_ge(pos_g_ready.sem, pos_g_ready.at(2 * q, half + 1))
                    pool.sem_inc(gather_go.sem, 1)
                    for i in range(COMB):
                        for k in range(2):
                            pool.indirect_dma_start(yg[half][:, k, i], None, y_dram,
                                                    bass.IndirectOffsetOnAxis(pos_g[:, half, k, i:i + 1], axis=0)
                                                    ).then_inc(yg_loaded[half].sem, 16)

        @block.scalar
        def _(act):
            act.wait_ge(loaded.sem, loaded.at(0, NLOAD))
            act.wait_ge(u_gathered.sem, u_gathered.at(0, 16 * NB))
            act.wait_ge(set_up.sem, set_up.at(0, NSET))

            def text_rows(b):
                act.wait_ge(uT_ready.sem, uT_ready.at(b, 0))
                act.activation(ub[:, 0:R], u_all[:, bass.ds(b, 1), :], ACT.Copy).then_inc(ub_ready.sem, 1)

            def magnitudes(b):
                act.wait_ge(h_ready.sem, h_ready.at(b, 0))
                for i in range(2):
                    act.wait_ge(conv_done.sem, conv_done.at(b, i + 1))
                    act.activation(edges[:, i], ps[:, i], ACT.Abs, scale=0.5).then_inc(abs_done.sem, 1)

            def projections(b):
                act.wait_ge(xT_turned.sem, xT_turned.at(b, 1))
                act.wait_ge(proj_done.sem, proj_done.at(b, 0))
                act.activation(xT[:], ps[:, 2:4, 0:T], ACT.Copy).then_inc(xT_ready.sem, 1)

            def queries(b):
                act.wait_ge(proj_done.sem, proj_done.at(b, 1))
                act.wait_ge(scores_done.sem, scores_done.at(b, 0))
                for dst in (q_hi, q_full):
                    for m in range(KB):
                        ins = act.activation(dst[:, m], ps[:, m, 0:T], ACT.Identity, bias=bq[:, m:m + 1], scale=SCALE)
                ins.then_inc(q_ready.sem, 1)

            def unit(b, s):
                if TURN <= s < NU + TURN:
                    u = s - TURN
                    k0 = 0 if u >= UPT else 1
                    act.wait_ge(turned.sem, turned.at(b, u + 1))
                    act.wait_ge(pv_done.sem, pv_done.at(b, max(u - 1, 0)))
                    act.activation(pT[:, u % 2, :, k0:2, :],
                                   ps[:, 2 + u % 2, :].rearrange("p (h k q) -> p h k q", h=2, k=2)[:, :, k0:2, :],
                                   ACT.Copy).then_inc(pT_ready.sem, 1)
                if s < NU:
                    w = slice(0 if s >= UPT else P, 2 * P)
                    act.wait_ge(sub_done.sem, sub_done.at(b, s + 1))
                    act.activation(prob[:, s % PB, :, w], prob[:, s % PB, :, w], ACT.Exp).then_inc(exp_done.sem, 1)
                if s >= UPT + PV + 1 and (s - UPT - PV - 1) % UPT == 0:
                    i = (s - UPT - PV - 1) // UPT
                    act.wait_ge(cx_turned.sem, cx_turned.at(b, i + 1))
                    act.wait_ge(wo_done.sem, wo_done.at(b, i))
                    act.activation(cxT[:], ps[:, 5, 0:D].rearrange("p (k q) -> p k q", k=KB), ACT.Copy
                                   ).then_inc(cxT_ready.sem, 1)

            def turned_rows(b, n):
                act.wait_ge(xc_turned.sem, xc_turned.at(b, n + 1))
                if n == 0:
                    act.wait_ge(up_done.sem, up_done.at(b, 0))
                elif n == 1:
                    act.wait_ge(block_done.sem, block_done.at(b, 2))
                else:
                    act.wait_ge(ssm_done.sem, ssm_done.at(b, 1))
                act.activation(xcT[:], ps[:, 6:8, 0:T], ACT.Copy).then_inc(xcT_ready.sem, 1)

            def block_outputs(b, n):
                act.wait_ge(block_done.sem, block_done.at(b, n + 1))
                if n == 0:
                    act.activation(srow[:], ps[:, 7, 0:T], ACT.Copy).then_inc(block_ready.sem, 1)
                else:
                    act.activation(g[:].rearrange("p i d -> p (i d)"),
                                   ps[:, 6:8, :].rearrange("p a c -> p (a c)")[:, 0:NT * D], ACT.Gelu_apprx_tanh
                                   ).then_inc(block_ready.sem, 1)

            def hidden_layer(b, f):
                if f == 0:
                    act.wait_ge(down_done.sem, down_done.at(b, 0))
                act.wait_ge(up_done.sem, up_done.at(b, f + 1))
                act.activation(hid[:, f], ps[:, 6 + f % 2, 0:T], ACT.Gelu_apprx_tanh, bias=sb1[:, f:f + 1]
                               ).then_inc(hid_ready.sem, 1)

            def sequence(b, att, chain, head):
                for s in range(SLOTS):
                    if chain:
                        if s in (TURN0, TURN1, TURN2):
                            turned_rows(b - 1, (TURN0, TURN1, TURN2).index(s))
                        if s in (BLOCK + 1, BLOCK + 2):
                            block_outputs(b - 1, s - BLOCK - 1)
                    if att:
                        unit(b, s)
                    if chain:
                        if UP <= s < UP + FB:
                            hidden_layer(b - 1, s - UP)
                    if head and s == CONV - 1:
                        text_rows(b + 1)
                    if head and s == CONV:
                        magnitudes(b + 1)
                rest = range(SLOTS - UP, FB) if chain else ()
                for f in rest[:1]:
                    hidden_layer(b - 1, f)
                if head:
                    projections(b + 1)
                for f in rest[1:2]:
                    hidden_layer(b - 1, f)
                if head:
                    queries(b + 1)
                for f in rest[2:]:
                    hidden_layer(b - 1, f)

            text_rows(0)
            magnitudes(0)
            projections(0)
            queries(0)
            sequence(0, True, False, True)
            act.wait_ge(late_loaded.sem, late_loaded.at(0, NLATE))
            with act.Fori(1, NB - 1) as b:
                sequence(b, True, True, True)
            sequence(NB - 1, True, True, False)
            sequence(NB, False, True, False)

            act.wait_ge(diff_ready.sem, diff_ready.at(0, 1))
            act.activation(gates[:, 1], gates[:, 0], ACT.Exp).then_inc(ratio_ready.sem, 1)
            act.wait_ge(w_loaded.sem, w_loaded.at(0, 32))
            act.activation(w1_hi[0][:], w1_raw[:], ACT.Copy)
            act.activation(w2_hi[0][:], w2_raw[:], ACT.Copy).then_inc(hi_ready.sem, 1)
            act.wait_ge(bounds_ready.sem, bounds_ready.at(0, 1))

            def hidden(q, half, e):
                lo, hi = expert_bounds(act, e)
                with act.Fori(lo, hi) as j:
                    act.wait_ge(b_loaded[half].sem, b_loaded[half].at(q, 32))
                    act.wait_ge(edown_done.sem, edown_done.at(j, 0))
                    for f in range(FB):
                        act.wait_ge(eup_done.sem, eup_done.at(j, f + 1))
                        act.activation(hid_hi[:, f], ps[:, f % 4, 0:CHUNK], ACT.Gelu_apprx_tanh,
                                       bias=b1[half][:, f:f + 1])
                        act.wait_ge(elo_ready.sem, elo_ready.at(j, max(f - 3, 0)))
                        act.activation(hid_full[:, f % 4], ps[:, f % 4, 0:CHUNK], ACT.Gelu_apprx_tanh,
                                       bias=b1[half][:, f:f + 1]).then_inc(ehid_ready.sem, 1)

            with act.Fori(0, NE // 2) as q:
                for half in range(2):
                    hidden(q, half, 2 * q + half)

        @block.vector
        def _(dve):

            def link(ins, steps, b):
                steps.steps += 1
                ins.then_inc(steps.sem, 1)
                dve.wait_ge(steps.sem, steps.at(b, steps.steps))

            dve.memset(ones9[:], 1e-9).then_inc(set_up.sem, 1)
            dve.memset(c15[:], 1.5)
            dve.memset(spare[:], 0.0).then_inc(set_up.sem, 1)
            dve.memset(vaug[:], 1.0).then_inc(set_up.sem, 1)
            dve.memset(ub[:], 0.0)
            link(dve.memset(gray[:], 0.0), setup_step, 0)
            dve.wait_ge(loaded.sem, loaded.at(0, NLOAD))
            dve.tensor_copy(ident_bf[:], ident[:])
            for j in range(2):
                ins = dve.tensor_copy(mask_bf[:, j], mask_f[:])
            ins.then_inc(set_up.sem, 1)
            link(dve.memset(band_edge[:], 0.0), setup_step, 0)
            for dy in range(3):
                for o in range(2):
                    for dx in range(3):
                        k = (o * 3 + dy) * 3 + dx
                        if dy == 0:
                            ins = dve.tensor_scalar(band[:, o, dx], shift[:, dy], tap[:, k:k + 1], None, ALU.mult)
                        else:
                            ins = dve.scalar_tensor_tensor(out=band[:, o, dx], in0=shift[:, dy], scalar=tap[:, k:k + 1],
                                                           in1=band[:, o, dx], op0=ALU.mult, op1=ALU.add)
                link(ins, setup_step, 0)
            for o in range(2):
                dve.tensor_copy(band_edge[:, o, 0, P - 1:P], tap_edge[:, o, 2:3])
                ins = dve.tensor_copy(band_edge[:, o, 1, 0:1], tap_edge[:, o, 0:1])
            ins.then_inc(set_up.sem, 1)
            link(dve.tensor_scalar(bq[:], bq[:], SCALE, None, ALU.mult), setup_step, 0)
            dve.memset(sumv[:], 0.0).then_inc(set_up.sem, 1)

            dve.memset(ones_t[:], 1.0)
            for i in range(NT):
                dve.tensor_scalar(before[:, i], rank_cols[:], rank_own[:, i:i + 1], None, ALU.is_lt)
                dve.tensor_scalar(after[:, i], rank_cols[:], rank_own[:, i:i + 1], None, ALU.is_ge)
            for k in range(KB):
                ins = dve.tensor_copy(wr_bc[:, k], wr_col[:, k:k + 1].to_broadcast([P, P]))
            link(ins, setup_step, 0)
            dve.wait_ge(mats_done.sem, mats_done.at(0, 1))
            for k in range(KB):
                dve.tensor_copy(fb[:, k], ps[:, k, 0:D])
                dve.tensor_copy(ce[:, k], ps[:, 2 + k, 0:D])
            dve.tensor_copy(om[:, 0:1], ps[:, 4, 0:1]).then_inc(mats_read.sem, 1)
            dve.wait_ge(mats_read.sem, mats_read.at(0, 1))

            w, w2, den, re, im, nim = (om[:, j:j + 1] for j in range(6))

            def eigenvalues():
                link(dve.tensor_tensor(w2, w, w, ALU.mult), setup_step, 0)
                link(dve.tensor_scalar(den, w2, 1.0, None, ALU.add), setup_step, 0)
                link(dve.reciprocal(nim, den), setup_step, 0)
                link(dve.tensor_scalar(den, w2, -1.0, 1.0, ALU.mult, ALU.add), setup_step, 0)
                dve.tensor_tensor(re, den, nim, ALU.mult)
                link(dve.scalar_tensor_tensor(out=im, in0=w, scalar=-2.0, in1=nim, op0=ALU.mult, op1=ALU.mult), setup_step, 0)
                dve.memset(turn[:, 0, 0:1], 1.0)
                dve.memset(turn[:, 1, 0:1], 0.0)

            def powers(n):
                m = min(n, T - n)
                link(dve.tensor_scalar(nim, im, -1.0, None, ALU.mult), setup_step, 0)
                dve.tensor_scalar(rot[:, 0, 0:m], turn[:, 0, 0:m], re, None, ALU.mult)
                dve.tensor_scalar(rot[:, 1, 0:m], turn[:, 0, 0:m], im, None, ALU.mult)
                dve.tensor_tensor(w2, im, im, ALU.mult)
                link(dve.tensor_tensor(den, re, im, ALU.mult), setup_step, 0)
                dve.scalar_tensor_tensor(out=turn[:, 0, n:n + m], in0=turn[:, 1, 0:m], scalar=nim,
                                         in1=rot[:, 0, 0:m], op0=ALU.mult, op1=ALU.add)
                link(dve.scalar_tensor_tensor(out=turn[:, 1, n:n + m], in0=turn[:, 1, 0:m], scalar=re,
                                                   in1=rot[:, 1, 0:m], op0=ALU.mult, op1=ALU.add), setup_step, 0)
                dve.tensor_scalar(im, den, 2.0, None, ALU.mult)
                link(dve.tensor_tensor(re, re, re, ALU.mult), setup_step, 0)
                link(dve.tensor_tensor(re, re, w2, ALU.subtract), setup_step, 0)

            def statistics(src, w, ready, steps, b):
                for i in range(NT):
                    ins = dve.bn_stats(w[:, 6 * i:6 * i + 6], src[:, i])
                link(ins, steps, b)
                dve.memset(w[:, 40:41], 0.0)
                for i in range(NT):
                    ins = dve.bn_aggr(w[:, 18 + 2 * i:20 + 2 * i], w[:, 6 * i:6 * i + 6])
                ins.then_inc(ready.sem, 1)

            def normalise(src, dst, w):
                for i in range(NT):
                    ins = dve.tensor_scalar(dst[:, i], src[:, i], w[:, 18 + 2 * i:19 + 2 * i], w[:, 27 + i:28 + i],
                                            ALU.subtract, ALU.mult)
                return ins

            def make_gray(b):
                head_step.steps = 0
                dve.wait_ge(x_loaded.sem, x_loaded.at(b, 32))
                dve.wait_ge(conv_done.sem, conv_done.at(b, 0))
                link(dve.tensor_scalar(gsum[:], xin[:, :, 0], GRAY[0], None, ALU.mult), head_step, b)
                link(dve.scalar_tensor_tensor(out=gsum[:], in0=xin[:, :, 1], scalar=GRAY[1], in1=gsum[:],
                                              op0=ALU.mult, op1=ALU.add), head_step, b)
                dve.scalar_tensor_tensor(out=gray[:, :, 1:IMG + 1], in0=xin[:, :, 2], scalar=GRAY[2], in1=gsum[:],
                                         op0=ALU.mult, op1=ALU.add).then_inc(gray_ready.sem, 1)

            def make_text(b):
                dve.wait_ge(uT_ready.sem, uT_ready.at(b, 1))
                dve.wait_ge(text_done.sem, text_done.at(b, 0))
                dve.tensor_scalar(usT[:], ps[0:R, 2, 0:P], s_col[:], None, ALU.mult).then_inc(usT_ready.sem, 1)

            def make_rows(b):
                dve.wait_ge(abs_done.sem, abs_done.at(b, 2))
                dve.wait_ge(hbo_ready.sem, hbo_ready.at(b, 0))
                dve.tensor_tensor(h[:, 0:2], edges[:, :, 0:IMG], edges[:, :, IMG:2 * IMG], ALU.add)
                dve.wait_ge(text_done.sem, text_done.at(b, 1))
                dve.tensor_copy(h[:, 2], ps[:, 2, D:2 * D]).then_inc(h_ready.sem, 1)
                dve.wait_ge(h_ready.sem, h_ready.at(b, 1))
                statistics(h, ln, head_stats_ready, head_step, b)

            def normalise_rows(b):
                dve.wait_ge(xT_turned.sem, xT_turned.at(b, 0))
                dve.wait_ge(head_rstd_ready.sem, head_rstd_ready.at(b, 1))
                normalise(h, xn, ln).then_inc(xn_ready.sem, 1)
                assert head_step.steps == head_step.per

            def keys_and_values(b):
                dve.wait_ge(proj_done.sem, proj_done.at(b, 2))
                dve.wait_ge(scores_done.sem, scores_done.at(b, 0))
                for m in range(KB):
                    ins = dve.tensor_scalar(k_hi[:, m], ps[:, 2 + m, 0:T], bk[:, m:m + 1], None, ALU.add)
                ins.then_inc(k_ready.sem, 1)
                dve.wait_ge(k_ready.sem, k_ready.at(b, 1))
                for m in range(KB):
                    dve.scalar_tensor_tensor(out=k_lo[:, m], in0=ps[:, 2 + m, 0:T], scalar=bk[:, m:m + 1],
                                             in1=k_hi[:, m], op0=ALU.add, op1=ALU.subtract)
                dve.wait_ge(q_ready.sem, q_ready.at(b, 1))
                dve.tensor_tensor(q_lo[:], q_full[:], q_hi[:], ALU.subtract).then_inc(parts_ready.sem, 1)
                dve.wait_ge(proj_done.sem, proj_done.at(b, 3))
                dve.wait_ge(pv_done.sem, pv_done.at(b, 0))
                for i in range(NT):
                    src = ps[:, 4, i * D:(i + 1) * D] if i < 2 else ps[:, 5, 0:D]
                    ins = dve.tensor_tensor(vaug[:, i, :, 0:DK], src.rearrange("p (h d) -> p h d", h=NH),
                                            bv_row[:].rearrange("p (h d) -> p h d", h=NH), ALU.add)
                ins.then_inc(v_ready.sem, 1)

            def values_sum(b):
                dve.wait_ge(sumv_done.sem, sumv_done.at(b, 1))
                dve.tensor_copy(sumv[:], ps[:, 5, D:2 * D]).then_inc(sumv_ready.sem, 1)

            def unit(b, s):
                if s < NU:
                    w = slice(0 if s >= UPT else P, 2 * P)
                    sc = ps[:, s % 2, :].rearrange("p (h k) -> p h k", h=2)[:, :, w]
                    n = 2 * P - w.start
                    dve.wait_ge(scores_done.sem, scores_done.at(b, s + 1))
                    link(dve.tensor_reduce(mx[:, s % 2], sc, AX_X, ALU.max), att_step, b)
                    dve.wait_ge(turned.sem, turned.at(b, max(s - PB + 1, 0)))
                    dve.tensor_tensor(prob[:, s % PB, :, w], sc, mx[:, s % 2].unsqueeze(2).to_broadcast([P, HG, n]),
                                      ALU.subtract).then_inc(sub_done.sem, 1)
                if s >= UPT + PV and (s - UPT - PV) % UPT == 0:
                    i = (s - UPT - PV) // UPT
                    pv = ps[:, 4, 0:NH * (DK + 1)].rearrange("p (h d) -> p h d", h=NH)
                    dve.wait_ge(pv_done.sem, pv_done.at(b, UPT * (i + 1)))
                    link(dve.reciprocal(rden[:], pv[:, :, DK]), att_step, b)
                    dve.wait_ge(cx_turned.sem, cx_turned.at(b, i))
                    dve.tensor_tensor(cx[:].rearrange("p (h d) -> p h d", h=NH), pv[:, :, 0:DK],
                                      rden[:].unsqueeze(2).to_broadcast([P, NH, DK]),
                                      ALU.mult).then_inc(pv_read.sem, 1)
                    dve.wait_ge(pv_read.sem, pv_read.at(b, i + 1))
                    dve.wait_ge(sumv_ready.sem, sumv_ready.at(b, 1))
                    dve.tensor_tensor(cx[:], cx[:], sumv[:], ALU.add).then_inc(cx_ready.sem, 1)
                if s >= UPT + PV + 3 and (s - UPT - PV - 3) % UPT == 0:
                    i = (s - UPT - PV - 3) // UPT
                    dve.wait_ge(wo_done.sem, wo_done.at(b, i + 1))
                    dve.wait_ge(hbo_ready.sem, hbo_ready.at(b, 1))
                    dve.tensor_tensor(h1[:, i], hbo[:, i], ps[:, 5, D:2 * D], ALU.add).then_inc(h1_ready.sem, 1)

            def chain_rows(b, n):
                statistics(hc, lnc, stats_ready, chain_step, b)

            def chain_scale(b, n):
                dve.wait_ge(xc_turned.sem, xc_turned.at(b, n))
                dve.wait_ge(rstd_ready.sem, rstd_ready.at(b, n + 1))
                normalise(hc, xc, lnc).then_inc(xc_ready.sem, 1)

            trial = [rot[:, 0], rot[:, 1], rot[:, 2], rot[:, 3], cum[:, 0], cum[:, 1]]

            def chain_start(b, chained):
                chain_step.steps = 0
                dve.wait_ge(h1_ready.sem, h1_ready.at(b, NT))
                dve.wait_ge(hb2_ready.sem, hb2_ready.at(b, 0))
                link(dve.tensor_copy(hc[:], h1[:]), chain_step, b)
                chain_rows(b, 0)
                if chained:
                    dve.wait_ge(xn_stored.sem, xn_stored.at(b - 1, 16))

            def chain(b, s):
                if s == RANK:
                    dve.wait_ge(block_ready.sem, block_ready.at(b, 1))
                    dve.wait_ge(state_im.sem, state_im.at(b, 0))
                    for i in range(NT):
                        ins = dve.scalar_tensor_tensor(out=trial[i][:, 0:P], in0=srow[:, i * P:(i + 1) * P], scalar=1.0,
                                                       in1=ident[:], op0=ALU.mult, op1=ALU.mult,
                                                       accum_out=own[:, i:i + 1])
                    link(ins, chain_step, b)
                if RANK <= s < RANK + NT:
                    i = s - RANK
                    dve.scalar_tensor_tensor(out=trial[2 * i], in0=srow[:], scalar=own[:, i:i + 1],
                                             in1=before[:, i], op0=ALU.is_ge, op1=ALU.mult,
                                             accum_out=count[:, 0, i:i + 1])
                    ins = dve.scalar_tensor_tensor(out=trial[2 * i + 1], in0=srow[:], scalar=own[:, i:i + 1],
                                                   in1=after[:, i], op0=ALU.is_gt, op1=ALU.mult,
                                                   accum_out=count[:, 1, i:i + 1])
                    if i == NT - 1:
                        link(ins, chain_step, b)
                if s == RANK + NT:
                    link(dve.tensor_tensor(sel[:], count[:, 0], count[:, 1], ALU.add), chain_step, b)
                    dve.tensor_scalar(sel[:], sel[:], KEEP - 0.5, None, ALU.is_lt)
                    dve.wait_ge(block_ready.sem, block_ready.at(b, 2))
                    link(dve.tensor_tensor(g[:], g[:], xc[:], ALU.subtract), chain_step, b)
                if s == RANK + NT + 1:
                    for i in range(NT):
                        ins = dve.scalar_tensor_tensor(out=g[:, i], in0=g[:, i], scalar=sel[:, i:i + 1], in1=xc[:, i],
                                                       op0=ALU.mult, op1=ALU.add)
                    link(ins, chain_step, b)
                if s == RANK + NT + 2:
                    link(dve.tensor_tensor(hc[:], hc[:], g[:], ALU.add), chain_step, b)
                if s == RANK + NT + 3:
                    chain_rows(b, 1)
                if s == TURN1 - 1:
                    chain_scale(b, 1)
                if s == STATE:
                    dve.wait_ge(u_done.sem, u_done.at(b, 1))
                    dve.tensor_tensor(rot[:, 0], ps[:, 6, 0:T], turn[:, 0], ALU.mult)
                    dve.tensor_tensor(rot[:, 1], ps[:, 7, 0:T], turn[:, 1], ALU.mult)
                    dve.tensor_tensor(rot[:, 2], ps[:, 7, 0:T], turn[:, 0], ALU.mult)
                    dve.tensor_tensor(rot[:, 3], ps[:, 6, 0:T], turn[:, 1], ALU.mult).then_inc(u_read.sem, 1)
                    dve.wait_ge(u_read.sem, u_read.at(b, 1))
                if s == STATE + 1:
                    link(dve.tensor_tensor(rot[:, 0], rot[:, 0], rot[:, 1], ALU.add), chain_step, b)
                    link(dve.tensor_tensor(rot[:, 2], rot[:, 2], rot[:, 3], ALU.subtract), chain_step, b)
                    dve.tensor_tensor_scan(cum[:, 0], ones_t[:], rot[:, 0], 0.0, ALU.mult, ALU.add)
                if s == STATE + 2:
                    dve.tensor_tensor_scan(cum[:, 1], ones_t[:], rot[:, 2], 0.0, ALU.mult, ALU.add
                                           ).then_inc(cum_ready.sem, 1)
                    dve.wait_ge(cum_ready.sem, cum_ready.at(b, 1))
                if s == STATE + 3:
                    dve.tensor_tensor(rot[:, 0], cum[:, 0], turn[:, 0], ALU.mult)
                    link(dve.tensor_tensor(rot[:, 1], cum[:, 1], turn[:, 1], ALU.mult), chain_step, b)
                    dve.wait_ge(ssm_done.sem, ssm_done.at(b, 0))
                    dve.tensor_tensor(st[:, 0], rot[:, 0], rot[:, 1], ALU.subtract).then_inc(state_re.sem, 1)
                if s == OUT + 1:
                    dve.wait_ge(direct_ready.sem, direct_ready.at(b, 1))
                    dve.wait_ge(ssm_done.sem, ssm_done.at(b, 1))
                    dve.tensor_tensor(hc[:].rearrange("p i d -> p (i d)"), hc[:].rearrange("p i d -> p (i d)"),
                                      ps[:, 6:8, :].rearrange("p a c -> p (a c)")[:, 0:NT * D], ALU.add
                                      ).then_inc(h3_ready.sem, 1)
                    dve.wait_ge(h3_ready.sem, h3_ready.at(b, 1))
                    chain_rows(b, 2)
                if s == TURN2 - 1:
                    chain_scale(b, 2)
                if s == UP:
                    dve.wait_ge(logit_done.sem, logit_done.at(b, 1))
                    for i in range(NT):
                        ins = dve.tensor_tensor(logit[:, i], ps[:, 7, i * NE:(i + 1) * NE], rb_row[:], ALU.add)
                    ins.then_inc(logit_read.sem, 1)
                    dve.wait_ge(logit_read.sem, logit_read.at(b, 1))
                    dve.memset(spare[:], 0.0)
                    for i in range(NT):
                        ins = dve.max(v8[:, i], logit[:, i])
                    link(ins, chain_step, b)
                if s == UP + 1:
                    dve.memset(spare[:], 0.0)
                    for i in range(NT):
                        ins = dve.max_index(i8[:, i], v8[:, i], logit[:, i])
                    link(ins, chain_step, b)
                    dve.tensor_copy(top_v[:, bass.ds(b, 1)].rearrange("p o i k -> p (o i) k"), v8[:, :, 0:2])
                    dve.tensor_copy(top_i[:, bass.ds(b, 1)].rearrange("p o i k -> p (o i) k"), i8[:, :, 0:2])
                    assert chain_step.steps == chain_step.per, chain_step.steps

            def shared_sum(b):
                dve.wait_ge(h4_sent.sem, h4_sent.at(b, 0))
                dve.wait_ge(hb2_ready.sem, hb2_ready.at(b, 1))
                dve.wait_ge(down_done.sem, down_done.at(b, 1))
                dve.tensor_tensor(h4[:].rearrange("p i d -> p (i d)"), hb2[:].rearrange("p i d -> p (i d)"),
                                  ps[:, 6:8, :].rearrange("p a c -> p (a c)")[:, 0:NT * D], ALU.add
                                  ).then_inc(h4_ready.sem, 1)

            def sequence(b, att, chained, head, first=False):
                att_step.steps = 0
                for s in range(SLOTS):
                    if first and s == 1:
                        eigenvalues()
                    if first and 2 <= s < 2 + (T - 1).bit_length():
                        powers(2 ** (s - 2))
                    if chained:
                        chain(b - 1, s)
                    if att:
                        unit(b, s)
                    if head and s == GRAY_AT:
                        make_gray(b + 1)
                    if head and s == CONV + 1:
                        make_text(b + 1)
                    if head and s == CONV + 2:
                        make_rows(b + 1)
                    if head and s == CONV + 4:
                        normalise_rows(b + 1)
                if head:
                    keys_and_values(b + 1)
                if att:
                    chain_start(b, chained)
                    chain_scale(b, 0)
                if chained:
                    shared_sum(b - 1)
                if head:
                    values_sum(b + 1)

            make_gray(0)
            make_text(0)
            make_rows(0)
            normalise_rows(0)
            keys_and_values(0)
            values_sum(0)
            sequence(0, True, False, True, first=True)
            dve.wait_ge(late_loaded.sem, late_loaded.at(0, NLATE))
            with dve.Fori(1, NB - 1) as b:
                sequence(b, True, True, True)
            sequence(NB - 1, True, True, False)
            sequence(NB, False, True, False)

            dve.wait_ge(h4_sent.sem, h4_sent.at(NB, 0))
            dve.wait_ge(route_loaded.sem, route_loaded.at(0, 48))
            v = top_v[:].rearrange("p b i k -> p (b i) k")
            ix = top_i[:].rearrange("p b i k -> p (b i) k")
            dve.tensor_tensor(gates[:, 0], v[:, :, 1], v[:, :, 0], ALU.subtract).then_inc(diff_ready.sem, 1)
            for k in range(2):
                for e in range(NE):
                    ins = dve.tensor_scalar(hot[:, k, e], ix[:, :, k], float(e), None, ALU.is_equal)
            dve.memset(ones1[:], 1.0)
            link(dve.memset(seg[:], 1.0), route_step, 0)
            dve.memset(seg[:, :, 0:1], 0.0)
            dve.tensor_tensor(hot2[:], hot[:, 0], hot[:, 1], ALU.add).then_inc(hot_ready.sem, 1)
            dve.wait_ge(ratio_ready.sem, ratio_ready.at(0, 1))
            link(dve.tensor_scalar(gates[:, 0], gates[:, 1], 1.0, None, ALU.add), route_step, 0)
            link(dve.reciprocal(gates[:, 2], gates[:, 0]), route_step, 0)
            dve.tensor_tensor(gates[:, 3], gates[:, 1], gates[:, 2], ALU.mult)
            dve.wait_ge(rank_done.sem, rank_done.at(0, 1))
            link(dve.tensor_copy(tot[:], ps[:, 1, 0:NE * TILES].rearrange("p (e t) -> p e t", e=NE)), route_step, 0)
            flat = "p e t -> p (e t)"
            link(dve.tensor_tensor_scan(incl[:].rearrange(flat), seg[:].rearrange(flat), tot[:].rearrange(flat),
                                             0.0, ALU.mult, ALU.add), route_step, 0)
            link(dve.tensor_tensor(over[:], incl[:, :, TILES - 1:TILES].to_broadcast([P, NE, RAMP]),
                                        ramp[:].unsqueeze(1).to_broadcast([P, NE, RAMP]), ALU.is_gt), route_step, 0)
            link(dve.tensor_reduce(chunks[:, 0], over[:], AX_X, ALU.add), route_step, 0)
            link(dve.tensor_scalar(chunks[:, 0], chunks[:, 0], 1.0, None, ALU.max), route_step, 0)
            link(dve.tensor_tensor_scan(chunks[:, 1], ones1[:, 0:NE], chunks[:, 0], 0.0, ALU.mult, ALU.add), route_step, 0)
            link(dve.tensor_tensor(chunks[:, 2], chunks[:, 1], chunks[:, 0], ALU.subtract), route_step, 0)
            dve.memset(bounds[:, 0:1], 0)
            dve.tensor_copy(bounds[:, 1:NE + 1], chunks[:, 1]).then_inc(bounds_ready.sem, 1)
            link(dve.tensor_tensor(incl[:], incl[:], tot[:], ALU.subtract), route_step, 0)
            link(dve.tensor_tensor(pos[:], incl[:], ps[:, 0, 0:NE * TILES].rearrange("p (e t) -> p e t", e=NE),
                                        ALU.add), route_step, 0)
            for e in range(NE):
                ins = dve.scalar_tensor_tensor(out=tot[:, e], in0=chunks[:, 2, e:e + 1].to_broadcast([P, TILES]),
                                             scalar=float(CHUNK), in1=pos[:, e], op0=ALU.mult, op1=ALU.add)
            link(ins, route_step, 0)
            for k in range(2):
                ins = dve.tensor_tensor(picked[:, k], hot[:, k], tot[:], ALU.mult)
            link(ins, route_step, 0)
            for k in range(2):
                ins = dve.tensor_reduce(pos_f[:, k], picked[:, k].rearrange("p e t -> p t e"), AX_X, ALU.add)
            link(ins, route_step, 0)
            link(dve.tensor_copy(pos_i[:], pos_f[:]), route_step, 0)
            dve.tensor_scalar(place_i[:, 0], pos_i[:], P - 1, None, ALU.bitwise_and)
            link(dve.tensor_scalar(place_i[:, 1], pos_i[:], P.bit_length() - 1, None, ALU.logical_shift_right),
                 route_step, 0)
            dve.tensor_copy(place[:], place_i[:]).then_inc(pos_ready.sem, 1)
            dve.wait_ge(pos_ready.sem, pos_ready.at(0, 1))
            with dve.Fori(0, TILES // RING) as q:
                for r in range(RING):
                    dve.wait_ge(place_free[r].sem, place_free[r].at(q, 0))
                    dve.tensor_scalar(place_row[:, r, 0], rank_cols[:, 0:P],
                                      place[:, 0, 0, bass.ds(RING * q + r, 1)], None, ALU.is_equal)
                    for k in range(2):
                        ins = dve.tensor_scalar(place_col[:, r, k], rank_cols[:, 0:SLOT_TILES],
                                                place[:, 1, k, bass.ds(RING * q + r, 1)],
                                                tok[:, bass.ds(RING * q + r, 1)], ALU.is_equal, ALU.mult)
                    ins.then_inc(col_ready.sem, 1)
            dve.wait_ge(slots_summed.sem, slots_summed.at(0, 1))
            dve.tensor_copy(slots_i[:], ps[:, 7, 0:SLOT_TILES]).then_inc(slots_ready.sem, 1)
            dve.wait_ge(hi_ready.sem, hi_ready.at(0, 1))
            dve.tensor_tensor(w1_lo[0][:], w1_raw[:], w1_hi[0][:], ALU.subtract)
            dve.tensor_tensor(w2_lo[0][:], w2_raw[:], w2_hi[0][:], ALU.subtract).then_inc(w_split.sem, 1)
            dve.wait_ge(bounds_ready.sem, bounds_ready.at(0, 1))

            def turn_chunk(j):
                dve.wait_ge(xg_turned.sem, xg_turned.at(j, 1))
                rows = ps[:, 6, :].rearrange("p (k n) -> p k n", k=KB)
                dve.tensor_copy(xg_hi[:], rows).then_inc(xg_rounded.sem, 1)
                dve.wait_ge(xg_rounded.sem, xg_rounded.at(j, 1))
                dve.tensor_tensor(xg_lo[:], rows, xg_hi[:], ALU.subtract).then_inc(xgT_ready.sem, 1)

            def outputs(q, half, e):
                lo, hi = expert_bounds(dve, e)
                with dve.Fori(lo, hi) as j:
                    dve.wait_ge(b_loaded[half].sem, b_loaded[half].at(q, 32))
                    for f in range(FB):
                        dve.wait_ge(ehid_ready.sem, ehid_ready.at(j, f + 1))
                        dve.tensor_tensor(hid_lo[:, f], hid_full[:, f % 4], hid_hi[:, f], ALU.subtract
                                          ).then_inc(elo_ready.sem, 1)
                    dve.wait_ge(eup_done.sem, eup_done.at(j, FB))
                    turn_chunk(j + 1)
                    dve.wait_ge(y_sent.sem, y_sent.at(j, 0))
                    for k in range(2):
                        dve.wait_ge(edown_done.sem, edown_done.at(j, k + 1))
                        dve.tensor_tensor(yb[:, k], ps[:, 4 + k, 0:D], b2_row[half][:], ALU.add
                                          ).then_inc(y_ready.sem, 1)

            turn_chunk(0)
            def round_weights(half, e, off):
                dve.wait_ge(w_loaded.sem, w_loaded.at(e, 32 * off + 32))
                dve.tensor_copy(w1_hi[half][:], w1_raw[:])
                dve.tensor_copy(w2_hi[half][:], w2_raw[:]).then_inc(hi_ready.sem, 1)

            round_weights(1, 0, 1)
            with dve.Fori(0, NE // 2 - 1) as q:
                for half in range(2):
                    outputs(q, half, 2 * q + half)
                    round_weights(half, 2 * q, half + 2)
            for half in range(2):
                outputs(NE // 2 - 1, half, NE - 2 + half)
            with dve.Fori(0, TILES // COMB // 2) as q:
                for half in range(2):
                    c = 2 * q + half
                    dve.wait_ge(yg_loaded[half].sem, yg_loaded[half].at(q, yg_loaded[half].per))
                    dve.wait_ge(hsum_loaded[half].sem, hsum_loaded[half].at(q, 16))
                    for i in range(COMB):
                        ins = dve.scalar_tensor_tensor(out=part[:, i], in0=yg[half][:, 0, i],
                                                       scalar=gates[:, 2, bass.ds(c * COMB + i, 1)],
                                                       in1=hsum[half][:, i], op0=ALU.mult, op1=ALU.add)
                    ins.then_inc(part_ready.sem, 1)
                    dve.wait_ge(part_ready.sem, part_ready.at(2 * q, half + 1))
                    dve.wait_ge(res_sent[half].sem, res_sent[half].at(q, 0))
                    for i in range(COMB):
                        ins = dve.scalar_tensor_tensor(out=res[half][:, i], in0=yg[half][:, 1, i],
                                                       scalar=gates[:, 3, bass.ds(c * COMB + i, 1)],
                                                       in1=part[:, i], op0=ALU.mult, op1=ALU.add)
                    ins.then_inc(res_ready[half].sem, 1)
                    dve.wait_ge(res_ready[half].sem, res_ready[half].at(q, 1))
                    dve.memset(spare[:], 0.0).then_inc(yg_read[half].sem, 1)

        @block.tensor
        def _(pe):
            pe.wait_ge(loaded.sem, loaded.at(0, NLOAD))
            for k in range(KB):
                for j in range(KB):
                    pe.matmul(ps[:, k, 0:D], b_w[:, j, k * P:(k + 1) * P], dft[:, j], start=(j == 0), stop=(j == KB - 1))
                for j in range(KB):
                    pe.matmul(ps[:, 2 + k, 0:D], idft[:, j, k * P:(k + 1) * P], c_wT[:, j],
                              start=(j == 0), stop=(j == KB - 1))
            pe.matmul(ps[:, 4, 0:1], sines[:], a_col[:], start=True, stop=True).then_inc(mats_done.sem, 1)
            pe.wait_ge(set_up.sem, set_up.at(0, NSET))
            pe.wait_ge(mats_read.sem, mats_read.at(0, 1))

            def convolution(b):
                pe.wait_ge(gray_ready.sem, gray_ready.at(b, 1))
                pe.wait_ge(halo_loaded.sem, halo_loaded.at(b, 96))
                pe.wait_ge(sub_done.sem, sub_done.at(b, 0))
                for i in range(2):
                    for o in range(2):
                        dst = ps[:, i, o * IMG:(o + 1) * IMG]
                        for dx in range(3):
                            pe.matmul(dst, band[:, o, dx], gray[:, i, dx:dx + IMG], start=(dx == 0), stop=False)
                        ins = pe.matmul(dst, band_edge[:, o, i], halo[:, i], start=False, stop=True)
                    ins.then_inc(conv_done.sem, 1)

            def turn_text(b):
                pe.wait_ge(ub_ready.sem, ub_ready.at(b, 1))
                pe.wait_ge(pT_ready.sem, pT_ready.at(b, 0))
                pe.transpose(ps[:, 2, 0:P], ub[:], ident[:]).then_inc(uT_ready.sem, 1)

            def text(b):
                pe.wait_ge(usT_ready.sem, usT_ready.at(b, 1))
                pe.matmul(ps[:, 2, D:2 * D], usT[:], vt[:], start=True, stop=True).then_inc(text_done.sem, 1)

            def turn_rows(b):
                pe.wait_ge(xn_ready.sem, xn_ready.at(b, 1))
                for k in range(KB):
                    for i in range(NT):
                        ins = pe.transpose(ps[:, 2 + k, i * P:(i + 1) * P], xn[:, i, k * P:(k + 1) * P], ident[:])
                ins.then_inc(xT_turned.sem, 1)

            def queries_and_keys(b):
                pe.wait_ge(xT_ready.sem, xT_ready.at(b, 1))
                pe.wait_ge(abs_done.sem, abs_done.at(b, 2))
                for w, first in ((wq, 0), (wk, 2)):
                    for m in range(KB):
                        for k in range(KB):
                            ins = pe.matmul(ps[:, first + m, 0:T], w[:, k, m * P:(m + 1) * P], xT[:, k],
                                            start=(k == 0), stop=(k == KB - 1))
                    ins.then_inc(proj_done.sem, 1)

            def values(b):
                pe.wait_ge(pv_read.sem, pv_read.at(b, 0))
                pe.wait_ge(h1_ready.sem, h1_ready.at(b, 0))
                for i in range(NT):
                    dst = ps[:, 4, i * D:(i + 1) * D] if i < 2 else ps[:, 5, 0:D]
                    for k in range(KB):
                        ins = pe.matmul(dst, xT[:, k, i * P:(i + 1) * P], wv[:, k], start=(k == 0), stop=(k == KB - 1))
                ins.then_inc(proj_done.sem, 1)

            def values_sum(b):
                pe.wait_ge(v_ready.sem, v_ready.at(b, 1))
                for i in range(NT):
                    ins = pe.matmul(ps[:, 5, D:2 * D].rearrange("p (h d) -> p h d", h=NH), ones9[:], vaug[:, i, :, 0:DK],
                                    start=(i == 0), stop=(i == NT - 1))
                ins.then_inc(sumv_done.sem, 1)

            def unit(b, s):
                if s < NU:
                    i, g = s // UPT, s % UPT
                    c0 = 0 if i else P
                    keys = slice((i - 1) * P + c0, (i + 1) * P)
                    m, r = g // PAIRS, g % PAIRS
                    if s < PAIRS:
                        pe.wait_ge(stacked[r].sem, stacked[r].at(b, stacked[r].per))
                    pe.wait_ge(sub_done.sem, sub_done.at(b, max(s - 1, 0)))
                    dst = ps[:, s % 2, :].rearrange("p (h k) -> p h k", h=2)[:, :, c0:2 * P]
                    pe.matmul(dst, qs[:, r, m, i * P:(i + 1) * P], ks[:, r, m, :, keys], start=True, stop=False)
                    pe.matmul(dst, ident_bf[:], mask_bf[:, :, c0:2 * P], start=False, stop=True
                              ).then_inc(scores_done.sem, 1)
                if TURN <= s < NU + TURN:
                    u = s - TURN
                    pe.wait_ge(exp_done.sem, exp_done.at(b, u + 1))
                    pe.wait_ge(pT_ready.sem, pT_ready.at(b, max(u - 1, 0)))
                    for hh in range(HG):
                        for k in range(0 if u >= UPT else 1, 2):
                            ins = pe.transpose(ps[:, 2 + u % 2, (2 * hh + k) * P:(2 * hh + k + 1) * P],
                                               prob[:, u % PB, hh, k * P:(k + 1) * P], ident[:])
                    ins.then_inc(turned.sem, 1)
                if PV <= s < NU + PV:
                    u = s - PV
                    i, g = u // UPT, u % UPT
                    if g == 0:
                        pe.wait_ge(pv_read.sem, pv_read.at(b, i))
                    pe.wait_ge(pT_ready.sem, pT_ready.at(b, u + 1))
                    for hh in range(HG):
                        hd = g * HG + hh
                        for k in range(0 if i else 1, 2):
                            ins = pe.matmul(ps[:, 4, hd * (DK + 1):(hd + 1) * (DK + 1)], pT[:, u % 2, hh, k],
                                            vaug[:, i - 1 + k, hd, :], start=(k == (0 if i else 1)), stop=(k == 1))
                    ins.then_inc(pv_done.sem, 1)
                if s >= UPT + PV + 1 and (s - UPT - PV - 1) % UPT == 0:
                    i = (s - UPT - PV - 1) // UPT
                    pe.wait_ge(cx_ready.sem, cx_ready.at(b, i + 1))
                    pe.wait_ge(h1_ready.sem, h1_ready.at(b, i))
                    for k in range(KB):
                        ins = pe.transpose(ps[:, 5, k * P:(k + 1) * P], cx[:, k * P:(k + 1) * P], ident[:])
                    ins.then_inc(cx_turned.sem, 1)
                if s >= UPT + PV + 2 and (s - UPT - PV - 2) % UPT == 0:
                    i = (s - UPT - PV - 2) // UPT
                    pe.wait_ge(cxT_ready.sem, cxT_ready.at(b, i + 1))
                    for k in range(KB):
                        ins = pe.matmul(ps[:, 5, D:2 * D], cxT[:, k], wo[:, k], start=(k == 0), stop=(k == KB - 1))
                    ins.then_inc(wo_done.sem, 1)

            def tile_out(i):
                return ps[:, 6 + i // 2, (i % 2) * D:(i % 2 + 1) * D]

            def turn_chain(b, n):
                pe.wait_ge(xc_ready.sem, xc_ready.at(b, n + 1))
                pe.wait_ge(xcT_ready.sem, xcT_ready.at(b, n))
                if n == 0:
                    pe.wait_ge(h4_ready.sem, h4_ready.at(b, 0))
                for k in range(KB):
                    for i in range(NT):
                        ins = pe.transpose(ps[:, 6 + k, i * P:(i + 1) * P], xc[:, i, k * P:(k + 1) * P], ident[:])
                ins.then_inc(xc_turned.sem, 1)

            def block_tile(i):
                for k in range(KB):
                    ins = pe.matmul(tile_out(i), xcT[:, k, i * P:(i + 1) * P], wb[:, k],
                                    start=(k == 0), stop=(k == KB - 1))
                return ins

            def up(b, f):
                if f == 1:
                    pe.wait_ge(logit_read.sem, logit_read.at(b, 1))
                pe.wait_ge(hid_ready.sem, hid_ready.at(b, max(f - 1, 0)))
                for k in range(KB):
                    ins = pe.matmul(ps[:, 6 + f % 2, 0:T], sw1[:, k, f * P:(f + 1) * P], xcT[:, k],
                                    start=(k == 0), stop=(k == KB - 1))
                ins.then_inc(up_done.sem, 1)

            def down(b, i):
                pe.wait_ge(hid_ready.sem, hid_ready.at(b, FB))
                for f in range(FB):
                    ins = pe.matmul(tile_out(i), hid[:, f, i * P:(i + 1) * P], sw2[:, f],
                                    start=(f == 0), stop=(f == FB - 1))
                if i == NT - 1:
                    ins.then_inc(down_done.sem, 1)

            def chain(b, s):
                if s in (TURN0, TURN1, TURN2):
                    turn_chain(b, (TURN0, TURN1, TURN2).index(s))
                if s == BLOCK:
                    pe.wait_ge(xcT_ready.sem, xcT_ready.at(b, 1))
                    for k in range(KB):
                        pe.matmul(ps[:, 7, 0:T], wr_bc[:, k], xcT[:, k], start=(k == 0), stop=(k == KB - 1))
                    block_tile(0)
                    block_tile(1).then_inc(block_done.sem, 1)
                if s == BLOCK + 2:
                    pe.wait_ge(block_ready.sem, block_ready.at(b, 1))
                    block_tile(2).then_inc(block_done.sem, 1)
                if s == TURN1 + 2:
                    pe.wait_ge(xcT_ready.sem, xcT_ready.at(b, 2))
                    for m in range(2):
                        for k in range(KB):
                            ins = pe.matmul(ps[:, 6 + m, 0:T], fb[:, k, m * P:(m + 1) * P], xcT[:, k],
                                            start=(k == 0), stop=(k == KB - 1))
                    ins.then_inc(u_done.sem, 1)
                if s == OUT:
                    pe.wait_ge(state_re.sem, state_re.at(b, 1))
                    pe.wait_ge(state_im.sem, state_im.at(b, 1))
                    for i in range(NT):
                        pe.matmul(tile_out(i), st[:, 0, i * P:(i + 1) * P], ce[:, 0], start=True, stop=False)
                        ins = pe.matmul(tile_out(i), st[:, 1, i * P:(i + 1) * P], ce[:, 1], start=False, stop=True)
                    ins.then_inc(ssm_done.sem, 1)
                if s == TURN2 + 1:
                    pe.wait_ge(xcT_ready.sem, xcT_ready.at(b, 3))
                    for i in range(NT):
                        for k in range(KB):
                            ins = pe.matmul(ps[:, 7, i * NE:(i + 1) * NE], xcT[:, k, i * P:(i + 1) * P], rw[:, k],
                                            start=(k == 0), stop=(k == KB - 1))
                    ins.then_inc(logit_done.sem, 1)
                if UP <= s < UP + FB:
                    up(b, s - UP)

            def sequence(b, att, chained, head):
                for s in range(SLOTS):
                    if chained:
                        chain(b - 1, s)
                    if att:
                        unit(b, s)
                    if head and s == CONV:
                        convolution(b + 1)
                        turn_text(b + 1)
                    if head and s == CONV + 1:
                        text(b + 1)
                rest = range(SLOTS - UP, FB) if chained else ()
                for f in rest[:1]:
                    up(b - 1, f)
                if head:
                    turn_rows(b + 1)
                for f in rest[1:2]:
                    up(b - 1, f)
                if head:
                    queries_and_keys(b + 1)
                    values(b + 1)
                for f in rest[2:]:
                    up(b - 1, f)
                if chained:
                    for i in range(NT):
                        down(b - 1, i)
                if head:
                    values_sum(b + 1)

            convolution(0)
            turn_text(0)
            text(0)
            turn_rows(0)
            queries_and_keys(0)
            values(0)
            values_sum(0)
            sequence(0, True, False, True)
            pe.wait_ge(late_loaded.sem, late_loaded.at(0, NLATE))
            with pe.Fori(1, NB - 1) as b:
                sequence(b, True, True, True)
            sequence(NB - 1, True, True, False)
            sequence(NB, False, True, False)

            pe.wait_ge(route_loaded.sem, route_loaded.at(0, 48))
            pe.wait_ge(hot_ready.sem, hot_ready.at(0, 1))
            pe.matmul(ps[:, 0, 0:NE * TILES], ltri[:], hot2[:].rearrange("p e t -> p (e t)"), start=True, stop=True)
            pe.matmul(ps[:, 1, 0:NE * TILES], ones1[:], hot2[:].rearrange("p e t -> p (e t)"),
                      start=True, stop=True).then_inc(rank_done.sem, 1)
            slots = ps[:, 7, 0:SLOT_TILES]
            nothing = ident[0:SLOT_TILES, 0:SLOT_TILES]
            pe.matmul(slots, zeros[:], nothing, start=True, stop=False)
            with pe.Fori(0, TILES // RING) as q:
                for r in range(RING):
                    pe.wait_ge(row_ready.sem, row_ready.at(RING * q, r + 1))
                    pe.wait_ge(col_ready.sem, col_ready.at(RING * q, r + 1))
                    for k in range(2):
                        ins = pe.matmul(slots, place_row[:, r, k], place_col[:, r, k], start=False, stop=False)
                    ins.then_inc(place_free[r].sem, 1)
            pe.matmul(slots, zeros[:], nothing, start=False, stop=True).then_inc(slots_summed.sem, 1)
            pe.wait_ge(pos_ready.sem, pos_ready.at(0, 1))

            def turn_chunk(j):
                pe.wait_ge(xg_loaded.sem, xg_loaded.at(j, 32))
                for k in range(KB):
                    for c in range(2):
                        ins = pe.transpose(ps[:, 6, (2 * k + c) * P:(2 * k + c + 1) * P],
                                           xg[:, c, k * P:(k + 1) * P], ident[:])
                ins.then_inc(xg_turned.sem, 1)

            def expert(q, half, e):
                lo, hi = expert_bounds(pe, e)
                with pe.Fori(lo, hi) as j:
                    pe.wait_ge(w_split.sem, w_split.at(2 * q, half + 1))
                    pe.wait_ge(xgT_ready.sem, xgT_ready.at(j, 1))
                    for f in range(FB):
                        pe.wait_ge(ehid_ready.sem, ehid_ready.at(j, max(f - 3, 0)))
                        cols = slice(f * P, (f + 1) * P)
                        terms = [(w, x, k) for w, x in ((w1_hi, xg_hi), (w1_hi, xg_lo), (w1_lo, xg_hi))
                                 for k in range(KB)]
                        for n, (w, x, k) in enumerate(terms):
                            ins = pe.matmul(ps[:, f % 4, 0:CHUNK], w[half][:, k, cols], x[:, k],
                                            start=(n == 0), stop=(n == len(terms) - 1))
                        ins.then_inc(eup_done.sem, 1)
                    turn_chunk(j + 1)
                    pe.wait_ge(y_ready.sem, y_ready.at(j, 0))
                    for c in range(2):
                        rows = slice(c * P, (c + 1) * P)
                        for f in range(FB):
                            if c == 0:
                                pe.wait_ge(elo_ready.sem, elo_ready.at(j, f + 1))
                            out = ps[:, 4 + c, 0:D]
                            pe.matmul(out, hid_hi[:, f, rows], w2_hi[half][:, f], start=(f == 0), stop=False)
                            pe.matmul(out, hid_hi[:, f, rows], w2_lo[half][:, f], start=False, stop=False)
                            ins = pe.matmul(out, hid_lo[:, f, rows], w2_hi[half][:, f], start=False, stop=(f == FB - 1))
                        ins.then_inc(edown_done.sem, 1)

            turn_chunk(0)
            with pe.Fori(0, NE // 2) as q:
                for half in range(2):
                    expert(q, half, 2 * q + half)



def layout(inputs):
    def blocks(w):
        w = np.asarray(w)
        return np.ascontiguousarray(w.reshape(w.shape[0] // P, P, -1).transpose(1, 0, 2))

    def col(v):
        return np.ascontiguousarray(np.asarray(v).reshape(-1, P).T)

    g = {k: np.asarray(v) for k, v in inputs.items()}
    a = {
        "x": g["x"], "ids": g["x_txt"].T, "U": g["L0_txt_U"], "s": g["L0_txt_s"].reshape(R, 1), "vt": g["L0_txt_Vt"],
        "scharr": g["L0_tok_scharr"].reshape(18), "scharr_dx": g["L0_tok_scharr"][:, 0].transpose(2, 0, 1),
        "wqT": blocks(g["L0_attn_Wq"].T), "wkT": blocks(g["L0_attn_Wk"].T), "wvT": blocks(g["L0_attn_Wv"].T),
        "woT": blocks(g["L0_attn_Wo"].T), "bq": col(g["L0_attn_bq"]), "bk": col(g["L0_attn_bk"]),
        "bv": g["L0_attn_bv"], "bo": g["L0_attn_bo"],
    }
    a |= {
        "wr": col(g["L0_ffn_w_router"]), "wb": blocks(g["L0_ffn_w_block"]), "a": g["L1_attn_a_params"].reshape(P, 1),
        "b_w": blocks(g["L1_attn_B_w"]), "c_wT": blocks(g["L1_attn_C_w"].T), "d": g["L1_attn_D"],
        "rwT": blocks(g["L1_ffn_router_w"].T), "rb": g["L1_ffn_router_b"],
        "sw1": blocks(g["L1_ffn_shared_w1"].T), "sw2": blocks(g["L1_ffn_shared_w2"].T),
        "sb1": col(g["L1_ffn_shared_b1"]), "sb2": g["L1_ffn_shared_b2"],
    }
    a |= {
        "w1": np.stack([blocks(w.T) for w in g["L1_ffn_spec_w1"]]), "w2": np.stack([blocks(w.T) for w in g["L1_ffn_spec_w2"]]),
        "b1": np.stack([col(v) for v in g["L1_ffn_spec_b1"]]), "b2": g["L1_ffn_spec_b2"],
    }
    r = np.arange(P)
    c = np.arange(2 * P)
    a["ident"] = np.eye(P, dtype=np.float32)
    a["mask"] = np.where((c[None] <= r[:, None] + P) & (c[None] >= r[:, None]), 0, MASKED).astype(np.float32)
    a["shift"] = np.stack([r[:, None] - r[None] == dy - 1 for dy in range(3)], 1).astype(np.float32)
    a["ltri"] = (r[:, None] < r[None]).astype(np.float32)
    a["ramp"] = (np.arange(RAMP) * CHUNK).astype(np.float32)
    a["tok"] = (np.arange(TILES)[None] * P + r[:, None]).astype(np.float32)
    j = np.arange(T)
    own = np.arange(NT)[:, None] * P + r[:, None, None]
    a["rank_cols"] = j.astype(np.float32)
    a["rank_own"] = own[:, :, 0].astype(np.float32)
    n = np.arange(D)
    angle = 2 * np.pi * np.outer(n, r) / D
    re, im = np.cos(angle), -np.sin(angle)
    im[:, 0] = (-1.0) ** n
    a["dft"] = blocks(np.concatenate([re, im], 1).astype(np.float32))
    scale = np.where(r == 0, 1.0, 2.0) / D
    a["idft"] = blocks(np.concatenate([re * scale, im * scale], 1).astype(np.float32))
    sines = -2 * np.sin(2 * np.pi * np.outer(r + 1, r) / D)
    sines[P - 1] = 0
    sines[:, 0] = 0
    a["sines"] = sines.astype(np.float32)
    return {k: np.ascontiguousarray(v) for k, v in a.items()}


def kernel(**inputs):
    import concourse.bacc as bacc
    from concourse.bass_utils import run_bass_kernel_spmd

    arrays = layout(inputs)
    nc = bacc.Bacc("TRN2", target_bir_lowering=False, num_devices=1)
    t = {k: nc.dram_tensor("in_" + k, v.shape, mybir.dt.from_np(v.dtype), kind="ExternalInput").ap()
         for k, v in arrays.items()}
    t["out"] = nc.dram_tensor("result", (NB, T, D), F32, kind="ExternalOutput").ap().rearrange("b t d -> (b t) d")
    build(nc, t)
    return run_bass_kernel_spmd(nc, [{"in_" + k: v for k, v in arrays.items()}], core_ids=[0]).results[0]["result"]
```
